# Optimizing a Trainium2 kernel written in Bass

```python
import numpy as np
import jax
import jax.numpy as jnp

def _softmax(x, axis=-1):
    return jax.nn.softmax(x, axis=axis)

def _gelu(x):
    return jax.nn.gelu(x, approximate=True)

def _silu(x):
    return jax.nn.silu(x)

def _sigmoid(x):
    return jax.nn.sigmoid(x)

def _layernorm(x, axis=-1, eps=1e-05):
    m = jnp.mean(x, axis=axis, keepdims=True)
    v = jnp.var(x, axis=axis, keepdims=True)
    return (x - m) / jnp.sqrt(v + eps)

def _scatter_add(tgt, idx, src, axis=0):
    return tgt.at[idx].add(src)

def _segment_sum(src, seg, n):
    return jax.ops.segment_sum(src, seg, n)
kernel_name = 'mk_decoder_postln_d2_seqx_r8_db8e00'

def setup_inputs(seed: int=0):
    np.random.seed(seed)
    _w = jnp.asarray

    def _rec_inputs():
        import jax
        import jax.numpy as jnp
        _rk = jax.random.key(seed)
        x = -0.0002928 + 1 * jax.random.normal(jax.random.fold_in(_rk, 1), (8, 256, 128), jnp.float32)
        _lenS = 256 - jax.random.randint(jax.random.fold_in(_rk, 7), (8,), 0, max(1, 256 // 4) + 1, jnp.int32)
        _lenS2 = 256 - jax.random.randint(jax.random.fold_in(_rk, 8), (8,), 0, max(1, 256 // 4) + 1, jnp.int32)
        _ctx_1024P = jax.random.normal(jax.random.fold_in(_rk, 11), (8, 16, 128), jnp.float32)
        _ctx_1024c = jax.random.dirichlet(jax.random.fold_in(_rk, 511), 0.3 * jnp.ones((16,), jnp.float32), (8, 256))
        _ctx_1024t = jnp.einsum('bsk,bkd->bsd', _ctx_1024c, _ctx_1024P)
        _ctx_1024t = _ctx_1024t * jax.lax.rsqrt(jnp.mean(jnp.square(_ctx_1024t)) + 1e-12) * 0.953939
        ctx_1024 = -1.39393e-06 + 0.999914 * (_ctx_1024t + 0.3 * jax.random.normal(jax.random.fold_in(_rk, 611), (8, 256, 128), jnp.float32))
        _validS = jnp.arange(256)[None, :] < _lenS[:, None]
        _validS2 = jnp.arange(256)[None, :] < _lenS2[:, None]
        _causal = jnp.tril(jnp.ones((256, 256), dtype=bool))
        mask_Bx1xSxS2_if1 = jnp.where(jnp.ones((8, 1, 256, 256), dtype=bool), 1, 0).astype(jnp.int32)
        return (x, ctx_1024, mask_Bx1xSxS2_if1)
    x, ctx_1024, mask_Bx1xSxS2_if1 = _rec_inputs()

    def _L0_attn_setup():
        import jax, jax.numpy as jnp
        import numpy as np
        D_MODEL = 128
        N_HEADS = 16
        HEAD_DIM = D_MODEL // N_HEADS
        ROPE_BASE = 10000.0

        def rope_sin_cos(seq_len, head_dim, dtype=jnp.float32):
            inv_freq = 1.0 / ROPE_BASE ** (jnp.arange(0, head_dim, 2, dtype=jnp.float32) / head_dim)
            t = jnp.arange(seq_len, dtype=jnp.float32)
            ang = jnp.einsum('i,j->ij', t, inv_freq)
            return (jnp.sin(ang).astype(dtype), jnp.cos(ang).astype(dtype))

        def apply_rotary_emb(x, sin, cos):
            x1 = x[..., ::2]
            x2 = x[..., 1::2]
            sin = sin[None, None, :, :]
            cos = cos[None, None, :, :]
            return jnp.concatenate([x1 * cos - x2 * sin, x1 * sin + x2 * cos], axis=-1)
        key = jax.random.key(seed)
        ks = jax.random.split(key, 5)
        B, S, D = (2, 256, D_MODEL)
        scale = 1.0 / np.sqrt(D)
        return {'x': jax.random.normal(ks[0], (B, S, D), dtype=jnp.float32), 'Wq': jax.random.normal(ks[1], (D, D), dtype=jnp.float32) * scale, 'Wk': jax.random.normal(ks[2], (D, D), dtype=jnp.float32) * scale, 'Wv': jax.random.normal(ks[3], (D, D), dtype=jnp.float32) * scale, 'Wo': jax.random.normal(ks[4], (D, D), dtype=jnp.float32) * scale}
    _L0_attn_all = _L0_attn_setup()
    _L0_attn_in = {k: v for k, v in _L0_attn_all.items() if k in ('Wq', 'Wk', 'Wv', 'Wo')}
    del _L0_attn_all

    def _L0_xattn_setup():
        import jax, jax.numpy as jnp
        import numpy as np
        N_HEAD = 16
        MAX_SEQ_LEN = 256
        RATIO = 1
        NEG_INF = -jnp.inf

        def make_alibi_bias(n_head: int, max_seq_len: int, ratio: int) -> jnp.ndarray:
            s = jnp.arange(max_seq_len)[None, :] * ratio
            t = jnp.arange(max_seq_len * ratio)[:, None]
            bias = (s - t).astype(jnp.float32)
            bias = jnp.where(bias > 0, NEG_INF, bias)
            m = jnp.cumprod(jnp.full((n_head,), 2.0 ** (-8.0 / n_head), dtype=jnp.float32))
            return bias[None, :, :] * m[:, None, None]
        key = jax.random.key(seed)
        kq, kk, kv = jax.random.split(key, 3)
        B, T, D = (2, 256, 128)
        return {'q': jax.random.normal(kq, (B, T, D), dtype=jnp.float32), 'k': jax.random.normal(kk, (B, T, D), dtype=jnp.float32), 'v': jax.random.normal(kv, (B, T, D), dtype=jnp.float32)}
    _L0_xattn_all = _L0_xattn_setup()
    _L0_xattn_in = {k: v for k, v in _L0_xattn_all.items() if k in ()}
    del _L0_xattn_all

    def _L0_ffn_setup():
        import math
        import jax, jax.numpy as jnp
        import numpy as np
        B, T, D = (4, 512, 128)
        H = 16
        HD = D // H
        CAP = int(512 * 0.125)
        DFF = int(D * 4 * 2 / 3)
        EPS = 1e-06

        def rmsnorm(x, g):
            return x * jax.lax.rsqrt(jnp.mean(x * x, axis=-1, keepdims=True) + EPS) * g
        key = jax.random.key(seed)
        ks = jax.random.split(key, 9)
        s = lambda k, shape: jax.random.normal(k, shape, jnp.float32) * 0.02
        return {'x': jax.random.normal(ks[0], (B, T, D), jnp.float32), 'w_router': s(ks[1], (D,)), 'W_qkv': s(ks[2], (3 * D, D)), 'W_out': s(ks[3], (D, D)), 'g1': jnp.ones((D,), jnp.float32), 'g2': jnp.ones((D,), jnp.float32), 'W1': s(ks[4], (DFF, D)), 'W2': s(ks[5], (DFF, D)), 'W3': s(ks[6], (D, DFF))}
    _L0_ffn_all = _L0_ffn_setup()
    _L0_ffn_in = {k: v for k, v in _L0_ffn_all.items() if k in ('w_router', 'W_qkv', 'W_out', 'g1', 'g2', 'W1', 'W2', 'W3')}
    del _L0_ffn_all

    def _L1_attn_setup():
        import jax, jax.numpy as jnp
        import numpy as np
        B, S, DM, H = (4, 128, 128, 16)
        D = DM // H

        def _split_heads(x):
            return x.reshape(x.shape[0], x.shape[1], H, D).transpose(0, 2, 1, 3)
        key = jax.random.key(seed)
        ks = jax.random.split(key, 16)
        sc = 0.02
        return {'hidden_states': jax.random.normal(ks[0], (B, S, DM), jnp.float32), 'wq': jax.random.normal(ks[1], (DM, DM), jnp.float32) * sc, 'bq': jax.random.normal(ks[2], (DM,), jnp.float32) * sc, 'wk': jax.random.normal(ks[3], (DM, DM), jnp.float32) * sc, 'bk': jax.random.normal(ks[4], (DM,), jnp.float32) * sc, 'wv': jax.random.normal(ks[5], (DM, DM), jnp.float32) * sc, 'bv': jax.random.normal(ks[6], (DM,), jnp.float32) * sc, 'wo': jax.random.normal(ks[7], (DM, DM), jnp.float32) * sc, 'bo': jax.random.normal(ks[8], (DM,), jnp.float32) * sc, 'wfq': jax.random.normal(ks[9], (DM, DM), jnp.float32) * sc, 'bfq': jax.random.normal(ks[10], (DM,), jnp.float32) * sc, 'wfg': jax.random.normal(ks[11], (DM, DM), jnp.float32) * sc, 'bfg': jax.random.normal(ks[12], (DM,), jnp.float32) * sc, 'up': jax.random.normal(ks[13], (H, 1, D), jnp.float32) * sc, 'uz': jax.random.normal(ks[14], (H, 1, D), jnp.float32) * sc}
    _L1_attn_all = _L1_attn_setup()
    _L1_attn_in = {k: v for k, v in _L1_attn_all.items() if k in ('wq', 'bq', 'wk', 'bk', 'wv', 'bv', 'wo', 'bo', 'wfq', 'bfq', 'wfg', 'bfg', 'up', 'uz')}
    del _L1_attn_all

    def _L1_xattn_setup():
        import jax, jax.numpy as jnp
        import numpy as np
        N, S, E, H = (4, 256, 128, 16)
        D = E // H
        key = jax.random.key(seed)
        ks = jax.random.split(key, 9)
        scale = 1.0 / np.sqrt(E)
        return {'values': jax.random.normal(ks[0], (N, S, E), jnp.float32), 'keys': jax.random.normal(ks[1], (N, S, E), jnp.float32), 'query': jax.random.normal(ks[2], (N, S, E), jnp.float32), 'mask': jnp.ones((N, 1, S, S), jnp.int32), 'Wv': jax.random.normal(ks[3], (E, E), jnp.float32) * scale, 'Wk': jax.random.normal(ks[4], (E, E), jnp.float32) * scale, 'Wq': jax.random.normal(ks[5], (E, E), jnp.float32) * scale, 'Wo': jax.random.normal(ks[6], (E, E), jnp.float32) * scale, 'bo': jax.random.normal(ks[7], (E,), jnp.float32) * scale}
    _L1_xattn_all = _L1_xattn_setup()
    _L1_xattn_in = {k: v for k, v in _L1_xattn_all.items() if k in ('Wv', 'Wk', 'Wq', 'Wo', 'bo')}
    del _L1_xattn_all

    def _L1_ffn_setup():
        import jax, jax.numpy as jnp
        import numpy as np
        TOP_K = 2
        NUM_EXPERTS = 8
        B, T, H, F = (4, 256, 128, 512)
        key = jax.random.key(seed)
        ks = jax.random.split(key, 6)
        s_in = 1.0 / np.sqrt(H)
        s_ff = 1.0 / np.sqrt(F)
        return {'x': jax.random.normal(ks[0], (B, T, H), dtype=jnp.float32), 'router_w': jax.random.normal(ks[1], (NUM_EXPERTS, H), dtype=jnp.float32) * s_in, 'router_b': jax.random.normal(ks[2], (NUM_EXPERTS,), dtype=jnp.float32) * 0.01, 'gate_w': jax.random.normal(ks[3], (NUM_EXPERTS, F, H), dtype=jnp.float32) * s_in, 'up_w': jax.random.normal(ks[4], (NUM_EXPERTS, F, H), dtype=jnp.float32) * s_in, 'down_w': jax.random.normal(ks[5], (NUM_EXPERTS, H, F), dtype=jnp.float32) * s_ff}
    _L1_ffn_all = _L1_ffn_setup()
    _L1_ffn_in = {k: v for k, v in _L1_ffn_all.items() if k in ('router_w', 'router_b', 'gate_w', 'up_w', 'down_w')}
    del _L1_ffn_all
    return {'x': x, 'ctx_1024': ctx_1024, 'mask_Bx1xSxS2_if1': mask_Bx1xSxS2_if1, 'L0_attn_Wq': _L0_attn_in['Wq'], 'L0_attn_Wk': _L0_attn_in['Wk'], 'L0_attn_Wv': _L0_attn_in['Wv'], 'L0_attn_Wo': _L0_attn_in['Wo'], 'L0_ffn_w_router': _L0_ffn_in['w_router'], 'L0_ffn_W_qkv': _L0_ffn_in['W_qkv'], 'L0_ffn_W_out': _L0_ffn_in['W_out'], 'L0_ffn_g1': _L0_ffn_in['g1'], 'L0_ffn_g2': _L0_ffn_in['g2'], 'L0_ffn_W1': _L0_ffn_in['W1'], 'L0_ffn_W2': _L0_ffn_in['W2'], 'L0_ffn_W3': _L0_ffn_in['W3'], 'L1_attn_wq': _L1_attn_in['wq'], 'L1_attn_bq': _L1_attn_in['bq'], 'L1_attn_wk': _L1_attn_in['wk'], 'L1_attn_bk': _L1_attn_in['bk'], 'L1_attn_wv': _L1_attn_in['wv'], 'L1_attn_bv': _L1_attn_in['bv'], 'L1_attn_wo': _L1_attn_in['wo'], 'L1_attn_bo': _L1_attn_in['bo'], 'L1_attn_wfq': _L1_attn_in['wfq'], 'L1_attn_bfq': _L1_attn_in['bfq'], 'L1_attn_wfg': _L1_attn_in['wfg'], 'L1_attn_bfg': _L1_attn_in['bfg'], 'L1_attn_up': _L1_attn_in['up'], 'L1_attn_uz': _L1_attn_in['uz'], 'L1_xattn_Wv': _L1_xattn_in['Wv'], 'L1_xattn_Wk': _L1_xattn_in['Wk'], 'L1_xattn_Wq': _L1_xattn_in['Wq'], 'L1_xattn_Wo': _L1_xattn_in['Wo'], 'L1_xattn_bo': _L1_xattn_in['bo'], 'L1_ffn_router_w': _L1_ffn_in['router_w'], 'L1_ffn_router_b': _L1_ffn_in['router_b'], 'L1_ffn_gate_w': _L1_ffn_in['gate_w'], 'L1_ffn_up_w': _L1_ffn_in['up_w'], 'L1_ffn_down_w': _L1_ffn_in['down_w']}

def reference(x, ctx_1024, mask_Bx1xSxS2_if1, L0_attn_Wq, L0_attn_Wk, L0_attn_Wv, L0_attn_Wo, L0_ffn_w_router, L0_ffn_W_qkv, L0_ffn_W_out, L0_ffn_g1, L0_ffn_g2, L0_ffn_W1, L0_ffn_W2, L0_ffn_W3, L1_attn_wq, L1_attn_bq, L1_attn_wk, L1_attn_bk, L1_attn_wv, L1_attn_bv, L1_attn_wo, L1_attn_bo, L1_attn_wfq, L1_attn_bfq, L1_attn_wfg, L1_attn_bfg, L1_attn_up, L1_attn_uz, L1_xattn_Wv, L1_xattn_Wk, L1_xattn_Wq, L1_xattn_Wo, L1_xattn_bo, L1_ffn_router_w, L1_ffn_router_b, L1_ffn_gate_w, L1_ffn_up_w, L1_ffn_down_w):
    import jax
    import jax.numpy as jnp

    def _L0_attn_ref(x, Wq, Wk, Wv, Wo):
        import jax, jax.numpy as jnp
        import numpy as np
        D_MODEL = 128
        N_HEADS = 16
        HEAD_DIM = D_MODEL // N_HEADS
        ROPE_BASE = 10000.0

        def rope_sin_cos(seq_len, head_dim, dtype=jnp.float32):
            inv_freq = 1.0 / ROPE_BASE ** (jnp.arange(0, head_dim, 2, dtype=jnp.float32) / head_dim)
            t = jnp.arange(seq_len, dtype=jnp.float32)
            ang = jnp.einsum('i,j->ij', t, inv_freq)
            return (jnp.sin(ang).astype(dtype), jnp.cos(ang).astype(dtype))

        def apply_rotary_emb(x, sin, cos):
            x1 = x[..., ::2]
            x2 = x[..., 1::2]
            sin = sin[None, None, :, :]
            cos = cos[None, None, :, :]
            return jnp.concatenate([x1 * cos - x2 * sin, x1 * sin + x2 * cos], axis=-1)
        B, S, D = x.shape
        H, Dh = (N_HEADS, HEAD_DIM)

        def split_heads(t):
            return t.reshape(B, S, H, Dh).transpose(0, 2, 1, 3)
        q = split_heads(x @ Wq.T)
        k = split_heads(x @ Wk.T)
        v = split_heads(x @ Wv.T)
        sin, cos = rope_sin_cos(S, Dh, dtype=x.dtype)
        q = apply_rotary_emb(q, sin, cos)
        k = apply_rotary_emb(k, sin, cos)
        scores = jnp.einsum('bhqd,bhkd->bhqk', q, k) / jnp.sqrt(jnp.asarray(Dh, x.dtype))
        attn = jax.nn.softmax(scores, axis=-1)
        out = jnp.einsum('bhqk,bhkd->bhqd', attn, v)
        out = out.transpose(0, 2, 1, 3).reshape(B, S, D)
        return out @ Wo.T

    def _L0_xattn_ref(q, k, v):
        import jax, jax.numpy as jnp
        import numpy as np
        N_HEAD = 16
        MAX_SEQ_LEN = 256
        RATIO = 1
        NEG_INF = -jnp.inf

        def make_alibi_bias(n_head: int, max_seq_len: int, ratio: int) -> jnp.ndarray:
            s = jnp.arange(max_seq_len)[None, :] * ratio
            t = jnp.arange(max_seq_len * ratio)[:, None]
            bias = (s - t).astype(jnp.float32)
            bias = jnp.where(bias > 0, NEG_INF, bias)
            m = jnp.cumprod(jnp.full((n_head,), 2.0 ** (-8.0 / n_head), dtype=jnp.float32))
            return bias[None, :, :] * m[:, None, None]
        B, T, D = q.shape
        S = k.shape[1]
        H = N_HEAD
        dh = D // H
        qh = q.reshape(B, T, H, dh).transpose(0, 2, 1, 3)
        kh = k.reshape(B, S, H, dh).transpose(0, 2, 1, 3)
        vh = v.reshape(B, S, H, dh).transpose(0, 2, 1, 3)
        scores = jnp.einsum('bhtd,bhsd->bhts', qh, kh) / jnp.sqrt(jnp.float32(dh))
        bias = make_alibi_bias(H, MAX_SEQ_LEN, RATIO)[:, -T:, -S:]
        attn = jax.nn.softmax(scores + bias[None], axis=-1)
        out = jnp.einsum('bhts,bhsd->bhtd', attn, vh)
        return out.transpose(0, 2, 1, 3).reshape(B, T, D)

    def _L0_ffn_ref(x, w_router, W_qkv, W_out, g1, g2, W1, W2, W3):
        import math
        import jax, jax.numpy as jnp
        import numpy as np
        B, T, D = (4, 512, 128)
        H = 16
        HD = D // H
        CAP = int(512 * 0.125)
        DFF = int(D * 4 * 2 / 3)
        EPS = 1e-06

        def rmsnorm(x, g):
            return x * jax.lax.rsqrt(jnp.mean(x * x, axis=-1, keepdims=True) + EPS) * g
        Bq, Tq, Dq = x.shape
        scores = x @ w_router
        _, idx = jax.lax.top_k(scores, CAP)
        x_sel = jnp.take_along_axis(x, idx[:, :, None], axis=1)
        h = rmsnorm(x_sel, g1)
        qkv = (h @ W_qkv.T).reshape(Bq, CAP, 3, H, HD)
        q, k, v = jnp.moveaxis(qkv, 2, 0)
        att = jnp.einsum('bqhd,bkhd->bhqk', q, k) / math.sqrt(HD)
        mask = jnp.triu(jnp.ones((CAP, CAP), bool), 1)
        att = jnp.where(mask, -jnp.inf, att)
        att = jax.nn.softmax(att, axis=-1)
        o = jnp.einsum('bhqk,bkhd->bqhd', att, v).reshape(Bq, CAP, Dq)
        x_attn = o @ W_out.T
        h2 = rmsnorm(x_sel + x_attn, g2)
        x_ff = jax.nn.silu(h2 @ W1.T) * (h2 @ W2.T) @ W3.T
        x_proc = x_sel + x_attn + x_ff
        out = x.at[jnp.arange(Bq)[:, None], idx].set(x_proc)
        return out

    def _L1_attn_ref(hidden_states, wq, bq, wk, bk, wv, bv, wo, bo, wfq, bfq, wfg, bfg, up, uz):
        import jax, jax.numpy as jnp
        import numpy as np
        B, S, DM, H = (4, 128, 128, 16)
        D = DM // H

        def _split_heads(x):
            return x.reshape(x.shape[0], x.shape[1], H, D).transpose(0, 2, 1, 3)
        key_len = hidden_states.shape[1]
        mixed_q = hidden_states @ wq + bq
        mixed_k = hidden_states @ wk + bk
        mixed_v = hidden_states @ wv + bv
        glo = jnp.mean(mixed_q, axis=1, keepdims=True)
        c = jnp.tanh(mixed_q @ wfq + bfq + (glo @ wfg + bfg))
        c = _split_heads(c)
        p = jnp.sum(c * up[None], axis=-1)
        z = jnp.sum(c * uz[None], axis=-1)
        P = jax.nn.sigmoid(p) * key_len
        Z = jax.nn.sigmoid(z) * key_len
        j = jnp.arange(key_len, dtype=P.dtype)
        G = -(j[None, None, None, :] - P[..., None]) ** 2 * 2.0 / Z[..., None] ** 2
        q = _split_heads(mixed_q)
        k = _split_heads(mixed_k)
        v = _split_heads(mixed_v)
        scores = jnp.einsum('bhqd,bhkd->bhqk', q, k) / jnp.sqrt(jnp.float32(D))
        scores = scores + G
        probs = jax.nn.softmax(scores, axis=-1)
        ctx = jnp.einsum('bhqk,bhkd->bhqd', probs, v)
        ctx = ctx.transpose(0, 2, 1, 3).reshape(ctx.shape[0], key_len, H * D)
        return ctx @ wo + bo

    def _L1_xattn_ref(values, keys, query, mask, Wv, Wk, Wq, Wo, bo):
        import jax, jax.numpy as jnp
        import numpy as np
        N, S, E, H = (4, 256, 128, 16)
        D = E // H
        n, q_len = (query.shape[0], query.shape[1])
        v = (values @ Wv.T).reshape(n, -1, H, D)
        k = (keys @ Wk.T).reshape(n, -1, H, D)
        q = (query @ Wq.T).reshape(n, q_len, H, D)
        energy = jnp.einsum('nqhd,nkhd->nhqk', q, k)
        energy = jnp.where(mask == 0, jnp.float32(-1e+20), energy)
        attn = jax.nn.softmax(energy / np.sqrt(D), axis=3)
        out = jnp.einsum('nhqk,nkhd->nqhd', attn, v).reshape(n, q_len, E)
        return out @ Wo.T + bo

    def _L1_ffn_ref(x, router_w, router_b, gate_w, up_w, down_w):
        import jax, jax.numpy as jnp
        import numpy as np
        TOP_K = 2
        NUM_EXPERTS = 8
        B, T, H, F = (4, 256, 128, 512)
        logits = jnp.einsum('bth,eh->bte', x, router_w) + router_b
        topv, topi = jax.lax.top_k(logits, TOP_K)
        gates = jax.nn.softmax(topv, axis=-1)

        def body(acc, inputs):
            e, gw, uw, dw = inputs
            w = jnp.sum(gates * (topi == e), axis=-1)
            h = jax.nn.silu(jnp.einsum('bth,fh->btf', x, gw)) * jnp.einsum('bth,fh->btf', x, uw)
            y = jnp.einsum('btf,hf->bth', h, dw)
            return (acc + y * w[..., None], None)
        init = jnp.zeros_like(x)
        xs = (jnp.arange(NUM_EXPERTS), gate_w, up_w, down_w)
        out, _ = jax.lax.scan(body, init, xs)
        return out
    x = _layernorm(x + _L0_attn_ref(x, L0_attn_Wq, L0_attn_Wk, L0_attn_Wv, L0_attn_Wo), axis=-1)
    x = _layernorm(x + _L0_xattn_ref(x, ctx_1024, ctx_1024), axis=-1)
    x = _layernorm(x + _L0_ffn_ref(x, L0_ffn_w_router, L0_ffn_W_qkv, L0_ffn_W_out, L0_ffn_g1, L0_ffn_g2, L0_ffn_W1, L0_ffn_W2, L0_ffn_W3), axis=-1)
    x = _layernorm(x + _L1_attn_ref(x, L1_attn_wq, L1_attn_bq, L1_attn_wk, L1_attn_bk, L1_attn_wv, L1_attn_bv, L1_attn_wo, L1_attn_bo, L1_attn_wfq, L1_attn_bfq, L1_attn_wfg, L1_attn_bfg, L1_attn_up, L1_attn_uz), axis=-1)
    x = _layernorm(x + _L1_xattn_ref(ctx_1024, ctx_1024, x, mask_Bx1xSxS2_if1, L1_xattn_Wv, L1_xattn_Wk, L1_xattn_Wq, L1_xattn_Wo, L1_xattn_bo), axis=-1)
    x = _layernorm(x + _L1_ffn_ref(x, L1_ffn_router_w, L1_ffn_router_b, L1_ffn_gate_w, L1_ffn_up_w, L1_ffn_down_w), axis=-1)
    return x

_drawn_inputs = setup_inputs


def setup_inputs(seed=0):
    import zlib

    import numpy as np

    out = dict(_drawn_inputs(seed))
    spreads = {'L0_ffn_g1': (1.0, 0.6), 'L0_ffn_g2': (1.0, 0.6)}
    factors = {'L0_ffn_w_router': 3.175,
     'L0_ffn_W_qkv': 3.451,
     'L0_ffn_W_out': 2.778,
     'L0_ffn_W1': 6.348,
     'L0_ffn_W2': 4.194,
     'L0_ffn_W3': 4.524,
     'L1_attn_wq': 7.842,
     'L1_attn_bq': 29.179,
     'L1_attn_wk': 6.626,
     'L1_attn_bk': 64.0,
     'L1_attn_wfq': 26.632,
     'L1_attn_bfq': 64.0,
     'L1_attn_wfg': 49.223,
     'L1_attn_bfg': 64.0,
     'L1_attn_up': 30.755,
     'L1_attn_uz': 39.799}
    for name, (base, spread) in spreads.items():
        noise = np.random.default_rng([zlib.crc32(name.encode()), seed]).standard_normal(out[name].shape)
        drawn = base * np.exp(spread * noise) if base else spread * noise
        out[name] = jnp.asarray(drawn.astype(out[name].dtype))
    for name, factor in factors.items():
        out[name] = (out[name] * factor).astype(out[name].dtype)
    return out
```

```python
from contextlib import ExitStack

import numpy as np

import concourse.bass as bass
from concourse import mybir

F32 = mybir.dt.float32
BF16 = mybir.dt.bfloat16
I32 = mybir.dt.int32
U32 = mybir.dt.uint32
ALU = mybir.AluOpType
ACT = mybir.ActivationFunctionType
AX_X = mybir.AxisListType.X

P = 128
D = 128
H = 16
DH = D // H
B = 8
S = 256
T = B * S
NT = T // P
CH = 512
TC = CH // P
NC = T // CH
SCALE = float(DH) ** -0.5
EPS = 1e-5
PARTS = 6
ROWS = PARTS * DH
XROW = ROWS
MROW = 96
NEG_CAUSAL = -1e30
NEG_MASK = -1e20
PVW = 32
SEL = 64
F0 = 341
EX = 8
FE = 512


class Batch:

    def __init__(self, c, i=None):
        self.no = c if i is None else 2 * i + c
        self.par = c % 2
        self.use = c // 2 if i is None else i + c // 2
        self.first = c if i is None else None


class Signal:

    def __init__(self, sem, base):
        self.sem, self.base = sem, base

    def at(self, n):
        return self.sem, self.base + n


class Tally:

    def __init__(self, eng, raised):
        self.eng, self.raised, self.n, self.base = eng, raised, 0, 0

    def done(self, ins):
        self.n += 1
        ins.then_inc(self.raised.sem, 1)
        self.eng.wait_ge(*self.raised.at(self.base + self.n))

    def loop(self, i, per):
        self.start, self.per, self.base = self.n, per, i * per

    def end(self, turns):
        assert self.n - self.start == self.per, (self.n - self.start, self.per)
        self.n += self.per * (turns - 1)
        self.base = 0



class Split:

    def __init__(self, g, name, jobs, values, nchunks):
        self.g, self.jobs, self.values, self.nchunks = g, jobs, values, nchunks
        self.has_pe = [j for j in jobs if j["kind"] != "sbuf"]
        kinds = [j["kind"] for j in jobs]
        n, n_v, n_rope = len(jobs), nchunks if values else 0, kinds.count("rope")
        self.projected = g.shared_sem("split_projected", len(self.has_pe))
        self.turned = g.shared_sem("split_turned", n_rope)
        self.rotated = g.shared_sem("split_rotated", n_rope)
        self.s1_ready = g.shared_sem("split_s1_ready", n)
        self.r1_ready = g.shared_sem("split_r1_ready", n)
        self.s2_ready = g.shared_sem("split_s2_ready", n)
        self.s3_ready = g.shared_sem("split_s3_ready", n)
        self.v_projected = g.shared_sem("split_v_projected", n_v)
        self.v_ready = g.shared_sem("split_v_ready", n_v)
        self.kept = g.shared_sem("split_kept", kinds.count("keep"))
        self.written = [g.shared_sem(f"split_written{i}", 48 * ((n - i + 1) // 2)) for i in range(2)]
        for n, j in enumerate(self.has_pe):
            j["n_pe"] = n
        for n, j in enumerate(j for j in jobs if j["kind"] == "keep"):
            j["n_keep"] = n

    def bank(self, job):
        return 2 * (job["n_pe"] % 2)

    def tensor(self, pe, ready):
        g, nc = self.g, self.g.nc
        per = len(self.jobs) // self.nchunks
        for c in range(self.nchunks):
            ready(c)
            for j in self.jobs[c * per:(c + 1) * per]:
                if j["kind"] == "sbuf":
                    continue
                n, b = j["n_pe"], self.bank(j)
                if n >= 2:
                    before = self.has_pe[n - 2]
                    if before["kind"] == "rope":
                        pe.wait_ge(*self.turned.at(before["n_pe"] + 1))
                    elif before["kind"] == "keep":
                        pe.wait_ge(*self.kept.at(before["n_keep"] + 1))
                    else:
                        pe.wait_ge(*self.r1_ready.at(self.jobs.index(before) + 1))
                for i, w in enumerate(j["w"]):
                    last = nc.tensor.matmul(g.bank[b + i][:, :], w, j["src"], start=True, stop=True)
                last.then_inc(self.projected.sem, 1)
            if self.values:
                w, src, bias = self.values
                if c >= 1:
                    pe.wait_ge(*self.v_ready.at(c))
                if bias is not None:
                    nc.tensor.matmul(g.bank[4][:, :].rearrange("p (t d) -> p t d", t=TC), g.ones_row[0:1, :],
                                     bias.unsqueeze(1).to_broadcast([1, TC, D]), start=True, stop=False)
                for t in range(TC):
                    last = nc.tensor.matmul(g.bank[4][:, t * P:(t + 1) * P], src[:, (c * TC + t) * P:(c * TC + t + 1) * P],
                                            w, start=bias is None, stop=bias is None or t == TC - 1)
                last.then_inc(self.v_projected.sem, 1)

    def scalar(self, act, ready=None):
        g, nc = self.g, self.g.nc
        per = len(self.jobs) // self.nchunks
        for n, j in enumerate(self.jobs):
            c = n // per
            if n % per == 0 and ready:
                ready(act, c)
            if n >= 2:
                act.wait_ge(*self.written[n % 2].at(48 * (n // 2)))
            s = g.parts[n % 2]
            src = j.get("src")
            if j["kind"] == "rope":
                act.wait_ge(*self.rotated.at(j["n_pe"] + 1))
                src = g.fbuf[n % 2][:, :]
            elif j["kind"] == "psum":
                act.wait_ge(*self.projected.at(j["n_pe"] + 1))
                src = g.bank[self.bank(j)][:, :]
            elif j["kind"] == "keep":
                act.wait_ge(*self.projected.at(j["n_pe"] + 1))
                nc.scalar.activation(j["keep"], g.bank[self.bank(j)][:, :], ACT.Identity,
                                     bias=j["bias"]).then_inc(self.kept.sem, 1)
                act.wait_ge(*self.kept.at(j["n_keep"] + 1))
                src = j["keep"]
            if j["kind"] == "psum" and j.get("bias") is not None:
                nc.scalar.activation(s[:, 0, :], src, ACT.Identity, bias=j["bias"]).then_inc(self.s1_ready.sem, 1)
            else:
                nc.scalar.copy(s[:, 0, :], src).then_inc(self.s1_ready.sem, 1)
            act.wait_ge(*self.r1_ready.at(n + 1))
            nc.scalar.copy(s[:, 1, :], g.rbuf[n % 2][:, :]).then_inc(self.s2_ready.sem, 1)
            if self.values and n % per == per - 1:
                act.wait_ge(*self.v_projected.at(c + 1))
                nc.scalar.copy(g.V[:, c * TC:(c + 1) * TC, :], g.bank[4][:, :].rearrange("p (t d) -> p t d", t=TC))\
                   .then_inc(self.v_ready.sem, 1)

    def vector(self, dve):
        g, nc = self.g, self.g.nc
        for n, j in enumerate(self.jobs):
            if j["kind"] == "rope":
                dve.wait_ge(*self.projected.at(j["n_pe"] + 1))
                if j["n_pe"] >= 1:
                    dve.wait_ge(*self.rotated.at(j["n_pe"]))
                b = self.bank(j)
                for i, table in enumerate((g.cos, g.sin)):
                    last = nc.vector.tensor_tensor(
                        g.turn[i][:, :].rearrange("p (b s) -> p b s", s=S),
                        g.bank[b + i][:, :].rearrange("p (b s) -> p b s", s=S),
                        table[:, :].unsqueeze(1).to_broadcast([P, CH // S, S]), ALU.mult)
                last.then_inc(self.turned.sem, 1)
                src = g.fbuf[n % 2][:, :]
            elif j["kind"] == "psum":
                src = g.bank[self.bank(j)][:, :]
            else:
                src = j["keep"] if j["kind"] == "keep" else j["src"]
            dve.wait_ge(*self.s1_ready.at(n + 1))
            if n >= 2:
                dve.wait_ge(*self.s3_ready.at(n - 1))
            s1 = g.parts[n % 2][:, 0, :]
            if j["kind"] == "psum" and j.get("bias") is not None:
                ins = nc.vector.scalar_tensor_tensor(g.rbuf[n % 2][:, :], src, j["bias"], s1, ALU.add, ALU.subtract)
            else:
                ins = nc.vector.tensor_tensor(g.rbuf[n % 2][:, :], src, s1, ALU.subtract)
            ins.then_inc(self.r1_ready.sem, 1)

    def gpsimd(self, pool):
        g, nc = self.g, self.g.nc
        for n, j in enumerate(self.jobs):
            if j["kind"] == "rope":
                pool.wait_ge(*self.turned.at(j["n_pe"] + 1))
                if n >= 2:
                    pool.wait_ge(*self.r1_ready.at(n - 1))
                nc.gpsimd.tensor_tensor(g.fbuf[n % 2][:, :], g.turn[0][:, :], g.turn[1][:, :], ALU.add)\
                  .then_inc(self.rotated.sem, 1)
            pool.wait_ge(*self.s2_ready.at(n + 1))
            nc.gpsimd.tensor_tensor(g.parts[n % 2][:, 2, :], g.rbuf[n % 2][:, :], g.parts[n % 2][:, 1, :],
                                    ALU.subtract).then_inc(self.s3_ready.sem, 1)

    def sync(self, sp):
        g = self.g
        per = len(self.jobs) // self.nchunks
        for n, j in enumerate(self.jobs):
            c = n // per
            s = g.parts[n % 2]
            rows = j["to"].rearrange("(r d) h t -> (d h) r t", d=DH)[:, :, c * CH:(c + 1) * CH]
            sp.wait_ge(*self.s3_ready.at(n + 1))
            first = 0
            for k in (3, 2, 1):
                part = s[:, 3 - k, :].unsqueeze(1).to_broadcast([P, k, CH]) if j["query"] else s[:, 0:k, :]
                sp.dma_start(rows[:, first:first + k, :], part)\
                  .then_inc(self.written[n % 2].sem, 16)
                first += k

    def wait_written(self, eng):
        n = len(self.jobs)
        for i in range(2):
            uses = (n - i + 1) // 2
            if uses:
                eng.wait_ge(*self.written[i].at(48 * uses))


class Core:

    def __init__(self, g, name, nb, nqt, causal=False, bias=None, xrows=0):
        self.g, self.nb, self.nqt, self.bias, self.xrows = g, nb, nqt, bias, xrows
        self.split = causal and nqt == 2
        self.queries = [(0, nqt * P)] + ([(P, P)] if self.split else [(0, nqt * P)]) * (nqt - 1)
        self.offset = [0, nqt * P][:nqt]
        self.width = sum(n for _, n in self.queries)
        self.keys = [P, 2 * P] if self.split else [nqt * P] * nqt
        self.nfeat = 2 + (1 if xrows else 0)
        self.st_ready = g.shared_sem("core_st_ready", 8 * nb)
        self.exp_done = g.shared_sem("core_exp_done", 8 * nb)
        self.mx_ready = g.shared_sem("core_mx_ready", 8 * nqt * nb)
        self.mx_done = g.shared_sem("core_mx_done", 8 * nqt * nb)
        self.mb_ready = g.shared_sem("core_mb_ready", 2 * nb)
        self.mt_ready = g.shared_sem("core_mt_ready", 2 * nb)
        self.mts_done = g.shared_sem("core_mts_done", 2 * nb)
        self.pv_done = g.shared_sem("core_pv_done", 4 * nb)
        self.ot_done = g.shared_sem("core_ot_done", 4 * nb)
        self.va_ready = g.shared_sem("core_va_ready", nb)
        self.cxt_ready = g.shared_sem("core_cxt_ready", nqt * nb)
        self.cx_done = g.shared_sem("core_cx_done", nqt * nb)
        self.chain = g.shared_sem("core_chain", (2 + nqt) * nb)
        self.feat = [[g.shared_sem(f"core_feat{p}{h}", 16 * self.nfeat * nb // 2) for h in range(2)] for p in range(2)]
        self.m_in = [[g.shared_sem(f"core_m_in{p}{h}", 32 * nb // 2) for h in range(2)] for p in range(2)]

    def steps(self, eng, body, last):
        body(0, None)
        body(1, None)
        turns = (last - 1) // 2
        if turns:
            with eng.Fori(0, turns) as i:
                body(2, i)
                body(3, i)
        for j in range(2 + 2 * turns, self.nb + 2):
            body(j, None)

    def batches(self, j, i):
        out = []
        for lag in range(3):
            c = j - lag
            out.append(None if c < 0 or c >= self.nb else Batch(c, i))
        return out

    def bias_for(self, b, transposed):
        g = self.g
        if self.bias == "batch":
            if transposed:
                return g.mask_k[:, bass.ts(b.no, 2 * S)]
            return g.mask_q[:, bass.ts(b.no, 2 * S)]
        return self.bias[1 if transposed else 0]

    def tensor(self, pe, ready):
        g, nc = self.g, self.g.nc
        ready()
        nqt = self.nqt

        def scores(b, u):
            if u % 4 == 0:
                pe.wait_ge(*self.m_in[b.par][u // 4].at((b.use + 1) * 32))
            if b.first is None or b.first * 8 + u >= 2:
                pe.wait_ge(*self.exp_done.at(b.no * 8 + u - 1))
            for hh in range(2):
                h = 2 * u + hh
                bank = g.bank[2 * (u % 2) + hh]
                if self.bias is not None:
                    nc.tensor.matmul(bank[:, 0:self.width], g.ident_bf[:, :],
                                     self.bias_for(b, True)[:, 0:self.width], start=True, stop=False)
                for kt in range(nqt):
                    lo, n = self.queries[kt]
                    last = nc.tensor.matmul(bank[:, self.offset[kt]:self.offset[kt] + n],
                                            g.K6[b.par][:, h, kt * P:(kt + 1) * P], g.Q6[b.par][:, h, lo:lo + n],
                                            start=self.bias is None, stop=self.bias is None or kt == nqt - 1)
            last.then_inc(self.st_ready.sem, 1)

        def maxima(b, pair, qt, v):
            if pair % 4 == 0 and qt == 0:
                pe.wait_ge(*self.feat[b.par][pair // 4].at((b.use + 1) * 16 * self.nfeat))
            if b.first is None or b.first * 8 * nqt + v >= 2:
                pe.wait_ge(*self.mx_done.at(b.no * (8 * nqt) + v - 1))
            kw = self.keys[qt]
            bank = g.bank[4 + v % 2][:, 0:2 * kw].rearrange("p (a k) -> p a k", a=2)
            if self.bias is not None:
                bias = self.bias_for(b, False)[:, qt * nqt * P:qt * nqt * P + kw]
                nc.tensor.matmul(bank, g.ident_bf[:, :], bias.unsqueeze(1).to_broadcast([P, 2, kw]), start=True, stop=False)
            for a in range(2):
                h = 2 * pair + a
                last = nc.tensor.matmul(bank[:, a, :], g.Q6[b.par][0:MROW, h, qt * P:(qt + 1) * P],
                                        g.K6[b.par][0:MROW, h, 0:kw], start=self.bias is None,
                                        stop=self.bias is None or a == 1)
            last.then_inc(self.mx_ready.sem, 1)

        def turn_m(b, half):
            pe.wait_ge(*self.mb_ready.at(b.no * 2 + half + 1))
            for qt in range(nqt):
                last = nc.tensor.transpose(g.aux_bf[0:16, qt * P:(qt + 1) * P], g.MB[half][:, qt, :], g.ident_bf[:, :])
            last.then_inc(self.mt_ready.sem, 1)

        def values(b, grp, kt):
            if kt == 0:
                if grp == 0:
                    pe.wait_ge(*self.va_ready.at(b.no + 1))
                pe.wait_ge(*self.exp_done.at(b.no * 8 + 2 * grp + 2))
                if b.first is None or b.first * 4 + grp >= 1:
                    pe.wait_ge(*self.ot_done.at(b.no * 4 + grp))
            lo, n = self.queries[kt]
            for hh in range(4):
                last = nc.tensor.matmul(
                    g.bank[6][PVW * hh:PVW * hh + PVW, lo:lo + n],
                    g.VA[b.par][:, kt, 4 * grp + hh, :],
                    g.PT[grp % 2][:, hh, self.offset[kt]:self.offset[kt] + n],
                    start=kt == 0, stop=kt == nqt - 1)
            if kt == nqt - 1:
                last.then_inc(self.pv_done.sem, 1)

        def turn_context(b, qt):
            pe.wait_ge(*self.ot_done.at(b.no * 4 + 4))
            for grp in range(4):
                last = nc.tensor.transpose(g.bank[7][:, grp * P:(grp + 1) * P], g.OT[b.par][:, grp, qt * P:(qt + 1) * P],
                                           g.ident[:, :])
            last.then_inc(self.cxt_ready.sem, 1)

        def step(j, i):
            bm, be, bc = self.batches(j, i)
            for grp in range(4):
                for slot in range(2 * nqt):
                    if bm:
                        maxima(bm, 2 * grp + slot // nqt, slot % nqt, grp * 2 * nqt + slot)
                    if be and slot % nqt == 0:
                        scores(be, 2 * grp + slot // nqt)
                    if slot % 2 == 1:
                        if be and grp >= 1:
                            values(be, grp - 1, slot // 2)
                        if bc and grp == 0:
                            values(bc, 3, slot // 2)
                    if slot == nqt:
                        if be and grp == 0:
                            if bc:
                                pe.wait_ge(*self.cx_done.at(bc.no * nqt))
                            pe.wait_ge(*self.mts_done.at(be.no * 2 + 1))
                            turn_m(be, 1)
                        if bm and grp == 2:
                            if bc:
                                pe.wait_ge(*self.cx_done.at(bc.no * nqt + 1))
                            if be:
                                pe.wait_ge(*self.mts_done.at(be.no * 2 + 2))
                            turn_m(bm, 0)
                if bc and grp % 2 == 1 and grp // 2 < nqt:
                    pe.wait_ge(*self.cx_done.at(bc.no * nqt + grp // 2))
                    if grp == 1 and be:
                        pe.wait_ge(*self.mts_done.at(be.no * 2 + 2))
                    if grp == 3 and bm:
                        pe.wait_ge(*self.mts_done.at(bm.no * 2 + 1))
                    turn_context(bc, grp // 2)

        self.steps(pe, step, self.nb - 1)

    def scalar(self, act):
        g, nc = self.g, self.g.nc

        def evacuate(b, grp):
            act.wait_ge(*self.pv_done.at(b.no * 4 + grp + 1))
            if grp == 0 and (b.first is None or b.first >= 2):
                act.wait_ge(*self.cxt_ready.at((b.no - 1) * self.nqt))
            w = self.nqt * P
            nc.scalar.copy(g.OT[b.par][:, grp, 0:w], g.bank[6][:, 0:w])\
              .then_inc(self.ot_done.sem, 1)

        def m_rows(b, half):
            act.wait_ge(*self.mt_ready.at(b.no * 2 + half + 1))
            if b.first is None or b.first >= 1:
                act.wait_ge(*self.m_in[1 - b.par][half].at((b.use + b.par) * 32))
            w = self.nqt * P
            nc.scalar.copy(g.MT[half][:, 0:w], g.aux_bf[0:16, 0:w]).then_inc(self.mts_done.sem, 1)

        def step(j, i):
            bm, be, bc = self.batches(j, i)
            for grp in range(4):
                if bc and grp < 2:
                    evacuate(bc, 2 + grp)
                if be and grp >= 2:
                    evacuate(be, grp - 2)
                if be:
                    for u in (2 * grp, 2 * grp + 1):
                        act.wait_ge(*self.st_ready.at(be.no * 8 + u + 1))
                        if u % 2 == 0 and (be.first is None or be.first * 4 + grp >= 2):
                            act.wait_ge(*self.pv_done.at(be.no * 4 + grp - 1))
                        nc.scalar.activation(g.PT[grp % 2][:, 2 * (u % 2):2 * (u % 2) + 2, 0:self.width],
                                             g.bank2[u % 2][:, :, 0:self.width], ACT.Exp, scale=SCALE)\
                          .then_inc(self.exp_done.sem, 1)
                if be and grp == 0:
                    m_rows(be, 1)
                if bm and grp == 2:
                    m_rows(bm, 0)

        self.steps(act, step, self.nb - 1)

    def vector(self, dve):
        g, nc = self.g, self.g.nc
        nqt = self.nqt
        t = Tally(dve, self.chain)

        def parts_of_m(b, half):
            dve.wait_ge(*self.mx_done.at(b.no * 8 * nqt + (half + 1) * 4 * nqt))
            m = g.MS[:, 0:nqt, 8 * half:8 * half + 8]
            hi, lo = g.MB[half][:, 0:nqt, 0:8], g.MB[half][:, 0:nqt, 8:16]
            if b.first is None or b.first >= 1:
                dve.wait_ge(*self.mt_ready.at(b.no * 2 + half - 1))
            t.done(nc.vector.tensor_scalar(hi, m, -1.0, None, ALU.mult))
            nc.vector.scalar_tensor_tensor(lo, m, -1.0, hi, ALU.mult, ALU.subtract).then_inc(self.mb_ready.sem, 1)

        def context(b, qt):
            dve.wait_ge(*self.cxt_ready.at(b.no * nqt + qt + 1))
            sums = g.bank[7][:, :].rearrange("p (h w) -> p h w", w=PVW)
            t.done(nc.vector.reciprocal(g.rsum[:, :], sums[:, :, DH]))
            nc.vector.tensor_tensor(g.CX[:, bass.ds(b.no * nqt + qt, 1), :].rearrange("p o (d h) -> p (o h) d", d=DH),
                                    sums[:, :, 0:DH],
                                    g.rsum[:, :].unsqueeze(2).to_broadcast([P, H, DH]), ALU.mult)\
              .then_inc(self.cx_done.sem, 1)

        def step(j, i):
            bm, be, bc = self.batches(j, i)
            for grp in range(4):
                if bm:
                    for k in range(2 * nqt):
                        pair, qt, v = 2 * grp + k // nqt, k % nqt, grp * 2 * nqt + k
                        kw = self.keys[qt]
                        dve.wait_ge(*self.mx_ready.at(bm.no * (8 * nqt) + v + 1))
                        nc.vector.reduce_max(g.MS[:, qt, 2 * pair:2 * pair + 2],
                                             g.bank[4 + v % 2][:, 0:2 * kw].rearrange("p (a k) -> p a k", a=2),
                                             axis=AX_X).then_inc(self.mx_done.sem, 1)
                if bm and grp % 2 == 1:
                    parts_of_m(bm, grp // 2)
                if bc and grp % 2 == 1 and grp // 2 < nqt:
                    context(bc, grp // 2)

        body = self.steps
        per = 2 * (2 + nqt)

        def looped(j, i):
            if i is not None and j == 2:
                t.loop(i, per)
            step(j, i)
            if i is not None and j == 3:
                t.end((self.nb - 2) // 2)

        body(dve, looped, self.nb - 1)

    def gpsimd(self, pool, values, ready):
        g, nc = self.g, self.g.nc
        nqt = self.nqt
        ready()

        def step(j, i):
            bm, _, _ = self.batches(j, i)
            if not bm:
                return
            if bm.first is None or bm.first >= 2:
                pool.wait_ge(*self.pv_done.at(bm.no * 4 - 4))
            nc.gpsimd.tensor_copy(g.VA[bm.par][:, 0:nqt, :, 0:DH],
                                  values[:, bass.ds(bm.no * nqt, nqt), :].rearrange("p t (d h) -> p t h d", d=DH))\
              .then_inc(self.va_ready.sem, 1)

        self.steps(pool, step, self.nb - 1)

    def sync(self, sp, q_rows, k_rows, x_rows=None):
        g = self.g
        w = self.nqt * P

        def load(b, half):
            hs = slice(8 * half, 8 * half + 8)
            for buf, rows in ((g.Q6, q_rows), (g.K6, k_rows)):
                sp.dma_start(buf[b.par][0:ROWS, hs, 0:w], rows[:, hs, bass.ts(b.no, w)])\
                  .then_inc(self.feat[b.par][half].sem, 16)
            if x_rows is not None:
                sp.dma_start(g.Q6[b.par][XROW:XROW + self.xrows, hs, 0:w], x_rows[:, hs, bass.ts(b.no, w)])\
                  .then_inc(self.feat[b.par][half].sem, 16)

        def m_rows(b, half):
            sp.wait_ge(*self.mts_done.at(b.no * 2 + half + 1))
            for part in range(2):
                sp.dma_start(g.Q6[b.par][MROW + part:MROW + part + 1, 8 * half:8 * half + 8, 0:w],
                             g.MT[half][8 * part:8 * part + 8, 0:w]).then_inc(self.m_in[b.par][half].sem, 16)

        def step(j, i):
            bm, be, _ = self.batches(j, i)
            more = i is not None or j + 1 < self.nb
            if j == 0:
                for half in range(2):
                    load(Batch(0), half)
            for half in range(2):
                if be and half == 0:
                    m_rows(be, 1)
                if bm and half == 1:
                    m_rows(bm, 0)
                if more:
                    if be:
                        sp.wait_ge(*self.st_ready.at(be.no * 8 + 4 * half + 4))
                    load(Batch(j + 1, i), half)

        self.steps(sp, step, self.nb - 3)


def rsqrt(g, t, out, v, scratch, n):
    nc = g.nc
    out, v, half, sq = out[:, 0:n], v[:, 0:n], scratch[0][:, 0:n], scratch[1][:, 0:n]
    t.done(nc.vector.tensor_scalar(out.bitcast(I32), v.bitcast(I32), -0.5, float(0x5F3759DF), ALU.mult, ALU.add))
    t.done(nc.vector.tensor_scalar(half, v, -0.5, None, ALU.mult))
    for _ in range(3):
        t.done(nc.vector.tensor_tensor(sq, out, out, ALU.mult))
        t.done(nc.vector.tensor_tensor(sq, sq, half, ALU.mult))
        t.done(nc.vector.scalar_tensor_tensor(out, sq, 1.5, out, ALU.add, ALU.mult))


def layernorm(g, t, y, out):
    nc = g.nc
    n = y.shape[1]
    for i in range(n):
        last = nc.vector.bn_stats(g.stats[:, i, :], y[:, i, :])
    t.done(last)
    for i in range(n):
        last = nc.vector.bn_aggr(g.meanvar[:, i, :], g.stats[:, i, :])
    t.done(last)
    t.done(nc.vector.tensor_scalar(g.var[:, 0:n], g.meanvar[:, 0:n, 1], EPS, None, ALU.add))
    rsqrt(g, t, g.rstd, g.var, (g.half, g.square), n)
    for i in range(n):
        last = nc.vector.tensor_scalar(out[:, i, :], y[:, i, :], g.meanvar[:, i, 0:1], g.rstd[:, i:i + 1],
                                       ALU.subtract, ALU.mult)
    return last


NORM_CHAIN = 3 + 2 + 9


class Post:

    def __init__(self, g, name, w=None, bias=None):
        self.g, self.w, self.bias = g, w, bias
        n = NC if w is not None else 0
        self.turned = g.shared_sem("post_turned", n)
        self.ct_ready = g.shared_sem("post_ct_ready", n)
        self.projected = g.shared_sem("post_projected", n)
        self.added = g.shared_sem("post_added", NC)
        self.normed = g.shared_sem("post_normed", NC)
        self.xt_turned = g.shared_sem("post_xt_turned", NC)
        self.xt_ready = g.shared_sem("post_xt_ready", NC)
        self.chain = g.shared_sem("post_chain", NC * NORM_CHAIN)

    def tensor(self, pe, ready):
        g, nc = self.g, self.g.nc
        ready()

        def turn_x(c):
            pe.wait_ge(*self.normed.at(c + 1))
            if c >= 1:
                pe.wait_ge(*self.xt_ready.at(c))
            for t in range(TC):
                last = nc.tensor.transpose(g.bank[7][:, t * P:(t + 1) * P], g.X[:, c * TC + t, :], g.ident[:, :])
            last.then_inc(self.xt_turned.sem, 1)

        for c in range(NC):
            if self.w is not None:
                if c >= 1:
                    pe.wait_ge(*self.ct_ready.at(c))
                for t in range(TC):
                    last = nc.tensor.transpose(g.bank[5][:, t * P:(t + 1) * P], g.CX[:, c * TC + t, :], g.ident[:, :])
                last.then_inc(self.turned.sem, 1)
                pe.wait_ge(*self.ct_ready.at(c + 1))
                if c >= 1:
                    pe.wait_ge(*self.added.at(c))
                if self.bias is not None:
                    nc.tensor.matmul(g.bank[6][:, :].rearrange("p (t d) -> p t d", t=TC), g.ones_row[0:1, :],
                                     self.bias.unsqueeze(1).to_broadcast([1, TC, D]), start=True, stop=False)
                for t in range(TC):
                    last = nc.tensor.matmul(g.bank[6][:, t * P:(t + 1) * P], g.CXT[:, c % 2, t * P:(t + 1) * P], self.w,
                                            start=self.bias is None, stop=self.bias is None or t == TC - 1)
                last.then_inc(self.projected.sem, 1)
            if c >= 1:
                turn_x(c - 1)
        turn_x(NC - 1)

    def scalar(self, act):
        g, nc = self.g, self.g.nc

        def copy_x(c):
            act.wait_ge(*self.xt_turned.at(c + 1))
            nc.scalar.copy(g.XT[:, c * CH:(c + 1) * CH], g.bank[7][:, :]).then_inc(self.xt_ready.sem, 1)

        for c in range(NC):
            if self.w is not None:
                act.wait_ge(*self.turned.at(c + 1))
                if c >= 2:
                    act.wait_ge(*self.projected.at(c - 1))
                nc.scalar.copy(g.CXT[:, c % 2, :], g.bank[5][:, :]).then_inc(self.ct_ready.sem, 1)
            if c >= 1:
                copy_x(c - 1)
        copy_x(NC - 1)

    def vector(self, dve):
        g, nc = self.g, self.g.nc
        t = Tally(dve, self.chain)
        for c in range(NC):
            x = g.X[:, c * TC:(c + 1) * TC, :]
            y = g.Y[:, :, :]
            if self.w is not None:
                dve.wait_ge(*self.projected.at(c + 1))
                more = g.bank[6][:, :].rearrange("p (t d) -> p t d", t=TC)
            else:
                more = g.CX[:, c * TC:(c + 1) * TC, :]
            if c >= 1:
                dve.wait_ge(*self.normed.at(c))
            nc.vector.tensor_tensor(y, more, x, ALU.add).then_inc(self.added.sem, 1)
            dve.wait_ge(*self.added.at(c + 1))
            layernorm(g, t, y, x).then_inc(self.normed.sem, 1)


class Depths:

    NP = B // 2
    FC = [(0, P), (P, P), (2 * P, F0 - 2 * P)]

    def __init__(self, g, name):
        self.g = g
        self.scored = g.sem(f"{name}_scored")
        self.ranked = g.sem(f"{name}_ranked")
        self.gathered = g.sem(f"{name}_gathered")
        self.taken = g.sem(f"{name}_taken")
        self.hidden = g.sem(f"{name}_hidden")
        self.h_turned = g.sem(f"{name}_h_turned")
        self.h_ready = g.sem(f"{name}_h_ready")
        self.g_turned = g.sem(f"{name}_g_turned")
        self.g_ready = g.sem(f"{name}_g_ready")
        self.cx_turned = g.sem(f"{name}_cx_turned")
        self.cx_ready = g.sem(f"{name}_cx_ready")
        self.attended = g.sem(f"{name}_attended")
        self.added = g.sem(f"{name}_added")
        self.h2 = g.sem(f"{name}_h2")
        self.h2_turned = g.sem(f"{name}_h2_turned")
        self.h2_ready = g.sem(f"{name}_h2_ready")
        self.gate_up = g.sem(f"{name}_gate_up")
        self.tanh = g.sem(f"{name}_tanh")
        self.mixed = g.sem(f"{name}_mixed")
        self.down = g.sem(f"{name}_down")
        self.delta = g.sem(f"{name}_delta")
        self.scattered = g.sem(f"{name}_scattered")
        self.summed = g.sem(f"{name}_summed")
        self.normed = g.sem(f"{name}_normed")
        self.xt_turned = g.sem(f"{name}_xt_turned")
        self.xt_ready = g.sem(f"{name}_xt_ready")
        self.chain = g.sem(f"{name}_chain")
        self.g_free = g.sem(f"{name}_g_free")
        sb = g.sb
        self.scol = sb("scol", [P, NT])
        self.above = sb("above", [P, NT])
        self.ties = sb("ties", [P, NT])
        self.rank = sb("rank", [P, NT])
        self.junk = g.fbuf[0]
        free = [buf[:, :, :].rearrange("p a b -> p (a b)") for buf in g.PT]
        self.G = free[0][:, 0:2 * B * SEL].rearrange("p (k b r) -> p k b r", k=2, b=B)
        self.GT = sb("GT", [P, self.NP, 2, P])
        self.XS = sb("XS", [P, self.NP, D])
        self.X1 = sb("X1", [P, self.NP, D])
        self.XA = sb("XA", [P, self.NP, D])
        self.HN = sb("HN", [P, self.NP, D])
        self.HT = sb("HT", [P, CH])
        self.U = g.PT[0][:, 0:3, :]
        self.TH = g.PT[1][:, 0:3, :]
        self.ss = sb("ss", [P, self.NP])


    def select_tensor(self, pe, ready):
        g, nc = self.g, self.g.nc
        for c in range(NC):
            ready(c)
            nc.tensor.matmul(g.bank[c][:, :], g.router[:, :], g.XT[:, c * CH:(c + 1) * CH], start=True, stop=True)\
              .then_inc(self.scored.sem, 1)
        pe.wait_ge(*self.ranked.at(1))
        for p in range(self.NP):
            for half in range(2):
                b = 2 * p + half
                for k in range(2):
                    last = nc.tensor.matmul(g.bank[4][SEL * half:SEL * half + SEL, p * D:(p + 1) * D],
                                            self.G[:, k, b, :], g.X[:, 2 * b + k, :], start=k == 0, stop=k == 1)
        last.then_inc(self.gathered.sem, 1)
        for p in range(self.NP):
            for k in range(2):
                n = 2 * p + k
                last = nc.tensor.transpose(g.bank[n // 4][:, (n % 4) * P:(n % 4 + 1) * P],
                                           self.G[:, k, 2 * p:2 * p + 2, :].rearrange("p b r -> p (b r)"), g.ident[:, :])
        last.then_inc(self.g_turned.sem, 1)
        pe.wait_ge(*self.hidden.at(1))
        for p in range(self.NP):
            last = nc.tensor.transpose(g.bank[5][:, p * P:(p + 1) * P], self.HN[:, p, :], g.ident[:, :])
        last.then_inc(self.h_turned.sem, 1)

    def select_scalar(self, act):
        g, nc = self.g, self.g.nc
        act.wait_ge(*self.gathered.at(1))
        nc.scalar.copy(self.XS[:, :, :], g.bank[4][:, :].rearrange("p (n d) -> p n d", d=D)).then_inc(self.taken.sem, 1)
        act.wait_ge(*self.g_turned.at(1))
        for n in range(2):
            last = nc.scalar.copy(self.GT[:, 2 * n:2 * n + 2, :, :],
                                  g.bank[n][:, :].rearrange("p (a k t) -> p a k t", a=2, k=2))
        last.then_inc(self.g_ready.sem, 1)
        act.wait_ge(*self.h_turned.at(1))
        nc.scalar.mul(self.HT[:, :], g.bank[5][:, :], g.col("f0_g1")).then_inc(self.h_ready.sem, 1)

    def rms(self, t, x, out):
        g, nc = self.g, self.g.nc
        for p in range(self.NP):
            last = nc.vector.scalar_tensor_tensor(self.junk2[:, p, :], x[:, p, :], 1.0, x[:, p, :], ALU.mult, ALU.mult,
                                                  accum_out=self.ss[:, p:p + 1])
        t.done(last)
        t.done(nc.vector.tensor_scalar(g.var[:, 0:self.NP], self.ss[:, :], 1.0 / D, 1e-6, ALU.mult, ALU.add))
        rsqrt(g, t, g.rstd, g.var, (g.half, g.square), self.NP)
        for p in range(self.NP):
            last = nc.vector.tensor_scalar(out[:, p, :], x[:, p, :], g.rstd[:, p:p + 1], None, ALU.mult)
        return last

    def select_vector(self, dve):
        g, nc = self.g, self.g.nc
        t = self.t = Tally(dve, self.chain)
        self.junk2 = g.Y
        for c in range(NC):
            dve.wait_ge(*self.scored.at(c + 1))
            for n in range(c * TC, (c + 1) * TC):
                b, k = n // 2, n % 2
                row = g.bank[c][:, (b % 2) * S:(b % 2) * S + S]
                t.done(nc.vector.scalar_tensor_tensor(self.junk[:, 0:P], row[:, k * P:(k + 1) * P], 1.0, g.ident[:, :],
                                                      ALU.mult, ALU.mult, accum_out=self.scol[:, n:n + 1]))
                nc.vector.tensor_scalar(self.junk[:, 0:S], row, self.scol[:, n:n + 1], None, ALU.is_gt, ALU.add,
                                        accum_out=self.above[:, n:n + 1]).then_inc(self.g_free.sem, 1)
                dve.wait_ge(*self.g_free.at(n + 1))
                t.done(nc.vector.scalar_tensor_tensor(self.junk[:, 0:S], row, self.scol[:, n:n + 1],
                                                      g.earlier[:, k, :], ALU.is_equal, ALU.mult,
                                                      accum_out=self.ties[:, n:n + 1]))
        t.done(nc.vector.tensor_tensor(self.rank[:, :], self.above[:, :], self.ties[:, :], ALU.add))
        rank = self.rank[:, :].rearrange("p (b k) -> p k b", k=2).unsqueeze(3)
        for k in range(2):
            last = nc.vector.tensor_tensor(self.G[:, k, :, :], g.iota[:, 0:SEL].unsqueeze(1).to_broadcast([P, B, SEL]),
                                           rank[:, k, :, :].to_broadcast([P, B, SEL]), ALU.is_equal)
        last.then_inc(self.ranked.sem, 1)
        dve.wait_ge(*self.taken.at(1))
        self.rms(t, self.XS, self.HN).then_inc(self.hidden.sem, 1)


    def feed_tensor(self, pe, ready):
        g, nc = self.g, self.g.nc
        ready()
        for p in range(self.NP):
            last = nc.tensor.transpose(g.bank[5][:, p * P:(p + 1) * P], g.CX[:, p, :], g.ident[:, :])
        last.then_inc(self.cx_turned.sem, 1)
        pe.wait_ge(*self.cx_ready.at(1))
        for p in range(self.NP):
            last = nc.tensor.matmul(g.bank[6][:, p * P:(p + 1) * P], g.CXT[:, 0, p * P:(p + 1) * P], g.w("f0_o"),
                                    start=True, stop=True)
        last.then_inc(self.attended.sem, 1)
        pe.wait_ge(*self.h2.at(1))
        for p in range(self.NP):
            last = nc.tensor.transpose(g.bank[7][:, p * P:(p + 1) * P], self.HN[:, p, :], g.ident[:, :])
        last.then_inc(self.h2_turned.sem, 1)
        pe.wait_ge(*self.h2_ready.at(1))
        for n, (lo, w) in enumerate(self.FC):
            for m in range(2):
                last = nc.tensor.matmul(g.bank[2 * n + m][0:w, :], g.f0_w12[:, m, lo:lo + w], self.HT[:, :],
                                        start=True, stop=True)
            last.then_inc(self.gate_up.sem, 1)
        pe.wait_ge(*self.mixed.at(3))
        for p in range(self.NP):
            for n, (lo, w) in enumerate(self.FC):
                last = nc.tensor.matmul(g.bank[6][:, p * P:(p + 1) * P], self.U[0:w, n, p * P:(p + 1) * P],
                                        g.f0_w3[0:w, n, :], start=n == 0, stop=n == 2)
        last.then_inc(self.down.sem, 1)
        pe.wait_ge(*self.delta.at(1))

        def scatter(c):
            if c >= 2:
                pe.wait_ge(*self.summed.at(c - 1))
            for half in range(2):
                rows = slice(SEL * half, SEL * half + SEL)
                for k in range(2):
                    last = nc.tensor.matmul(g.bank[2 * (c % 2) + half][:, k * P:(k + 1) * P], self.GT[rows, c, k, :],
                                            self.X1[rows, c, :], start=True, stop=True)
            last.then_inc(self.scattered.sem, 1)

        scatter(0)
        scatter(1)
        for c in range(NC):
            pe.wait_ge(*self.normed.at(c + 1))
            if c >= 1:
                pe.wait_ge(*self.xt_ready.at(c))
            for i in range(TC):
                last = nc.tensor.transpose(g.bank[7][:, i * P:(i + 1) * P], g.X[:, c * TC + i, :], g.ident[:, :])
            last.then_inc(self.xt_turned.sem, 1)
            if c + 2 < NC:
                scatter(c + 2)

    def feed_scalar(self, act):
        g, nc = self.g, self.g.nc
        act.wait_ge(*self.cx_turned.at(1))
        nc.scalar.copy(g.CXT[:, 0, :], g.bank[5][:, :]).then_inc(self.cx_ready.sem, 1)
        act.wait_ge(*self.h2_turned.at(1))
        nc.scalar.mul(self.HT[:, :], g.bank[7][:, :], g.col("f0_g2")).then_inc(self.h2_ready.sem, 1)
        for n, (lo, w) in enumerate(self.FC):
            act.wait_ge(*self.gate_up.at(n + 1))
            nc.scalar.activation(self.TH[0:w, n, :], g.bank[2 * n][0:w, :], ACT.Tanh, scale=0.5).then_inc(self.tanh.sem, 1)
        for c in range(NC):
            act.wait_ge(*self.xt_turned.at(c + 1))
            nc.scalar.copy(g.XT[:, c * CH:(c + 1) * CH], g.bank[7][:, :]).then_inc(self.xt_ready.sem, 1)

    def feed_vector(self, dve):
        g, nc = self.g, self.g.nc
        t = self.t
        tiles = lambda bank: bank[:, :].rearrange("p (n d) -> p n d", d=D)
        dve.wait_ge(*self.attended.at(1))
        t.done(nc.vector.tensor_copy(self.XA[:, :, :], tiles(g.bank[6])))
        t.done(nc.vector.tensor_tensor(self.X1[:, :, :], self.XA[:, :, :], self.XS[:, :, :], ALU.add))
        self.rms(t, self.X1, self.HN).then_inc(self.h2.sem, 1)
        for n, (lo, w) in enumerate(self.FC):
            dve.wait_ge(*self.tanh.at(n + 1))
            t.done(nc.vector.scalar_tensor_tensor(self.TH[0:w, n, :], self.TH[0:w, n, :], 1.0, g.bank[2 * n][0:w, :],
                                                  ALU.add, ALU.mult))
            nc.vector.scalar_tensor_tensor(self.U[0:w, n, :], self.TH[0:w, n, :], 0.5, g.bank[2 * n + 1][0:w, :],
                                           ALU.mult, ALU.mult).then_inc(self.mixed.sem, 1)
        dve.wait_ge(*self.down.at(1))
        nc.vector.tensor_tensor(self.X1[:, :, :], tiles(g.bank[6]), self.XA[:, :, :], ALU.add).then_inc(self.delta.sem, 1)
        for c in range(NC):
            dve.wait_ge(*self.scattered.at(c + 1))
            if c >= 1:
                dve.wait_ge(*self.normed.at(c))
            x = g.X[:, c * TC:(c + 1) * TC, :]
            for half in range(2):
                two = slice(2 * half, 2 * half + 2)
                last = nc.vector.scalar_tensor_tensor(g.Y[:, two, :], x[:, two, :], 2.0,
                                                      tiles(g.bank[2 * (c % 2) + half])[:, 0:2, :], ALU.mult, ALU.add)
            last.then_inc(self.summed.sem, 1)
            dve.wait_ge(*self.summed.at(c + 1))
            layernorm(g, t, g.Y[:, :, :], x).then_inc(self.normed.sem, 1)


class Gauss:

    def __init__(self, g, name):
        self.g = g
        self.summed = g.sem(f"{name}_summed")
        self.global_ = g.sem(f"{name}_global_")
        self.bias = g.sem(f"{name}_bias")
        self.c_in = g.sem(f"{name}_c_in")
        self.c_ready = g.sem(f"{name}_c_ready")
        self.pz = g.sem(f"{name}_pz")
        self.acted = g.sem(f"{name}_acted")
        self.rows_ready = g.sem(f"{name}_rows_ready")
        self.turned = g.sem(f"{name}_turned")
        self.copied = g.sem(f"{name}_copied")
        self.written = g.sem(f"{name}_written")
        self.chain = g.sem(f"{name}_chain")
        self.g1 = g.sem(f"{name}_g1")
        sb = g.sb
        self.glo = sb("glo", [P, B])
        self.cbias = sb("cbias", [P, B])
        self.MQ = g.CX[:, :, :].rearrange("p n d -> p (n d)")
        self.C = g.CXT
        free = g.PT[1][:, :, :].rearrange("p a b -> p (a b)")
        n = NT * H
        tiles = lambda ap: ap.rearrange("p (n h) -> p n h", h=H)
        self.ez, self.tp = tiles(free[:, 0:n]), tiles(free[:, n:2 * n])
        self.AB = free[:, 2 * n:4 * n].rearrange("p (a n h) -> p a n h", a=2, h=H)
        self.rem = free[:, 4 * n:6 * n].rearrange("p (a n h) -> p a n h", a=2, h=H)
        self.XR = g.PT[0][:, :, :].rearrange("p a b -> p (a b)").bitcast(BF16)[:, 0:6 * n]\
                   .rearrange("p (n r h) -> p n r h", n=NT, h=H)
        self.AR = g.OT[0][:, :, :].rearrange("p a b -> p (a b)").bitcast(BF16)[0:6 * H, :]

    def tensor(self, pe):
        g, nc = self.g, self.g.nc
        pe.wait_ge(*self.summed.at(1))
        nc.tensor.matmul(g.bank[5][:, 0:B], g.w("a1_fg"), self.glo[:, :], start=True, stop=True).then_inc(self.global_.sem, 1)
        for c in range(NC):
            if c >= 1:
                pe.wait_ge(*self.c_ready.at(c))
            nc.tensor.matmul(g.bank[6][:, :], g.w("a1_fq"), self.MQ[:, c * CH:(c + 1) * CH], start=True, stop=True)\
              .then_inc(self.c_in.sem, 1)
            pe.wait_ge(*self.c_ready.at(c + 1))
            for t in range(TC):
                n = c * TC + t
                last = nc.tensor.matmul(g.bank[7][:, n * 2 * H:(n + 1) * 2 * H], self.C[:, c % 2, t * P:(t + 1) * P],
                                        g.upz[:, :], start=True, stop=True)
            last.then_inc(self.pz.sem, 1)
        pe.wait_ge(*self.rows_ready.at(2))
        for n in range(NT):
            bank = g.bank[5 + n // 8].bitcast(BF16)
            last = nc.tensor.transpose(bank[0:6 * H, (n % 8) * P:(n % 8 + 1) * P],
                                       self.XR[:, n, :, :].rearrange("p r h -> p (r h)"), g.ident_bf[:, :])
            if n % 8 == 7:
                last.then_inc(self.turned.sem, 1)

    def scalar(self, act):
        g, nc = self.g, self.g.nc
        for c in range(NC):
            act.wait_ge(*self.c_in.at(c + 1))
            act.wait_ge(*self.bias.at(1))
            if c >= 2:
                act.wait_ge(*self.pz.at(c - 1))
            for k in range(2):
                b = 2 * c + k
                last = nc.scalar.activation(self.C[:, c % 2, k * S:(k + 1) * S], g.bank[6][:, k * S:(k + 1) * S], ACT.Tanh,
                                            bias=self.cbias[:, b:b + 1])
            last.then_inc(self.c_ready.sem, 1)
        act.wait_ge(*self.pz.at(NC))
        pz = g.bank[7][:, :].rearrange("p (n a h) -> p n a h", a=2, h=H)
        nc.scalar.activation(self.tp[:, :, :], pz[:, :, 0, :], ACT.Tanh, scale=0.5)
        nc.scalar.activation(self.ez[:, :, :], pz[:, :, 1, :], ACT.Exp, scale=-1.0).then_inc(self.acted.sem, 1)
        for n in range(2):
            act.wait_ge(*self.turned.at(n + 1))
            nc.scalar.copy(self.AR[:, n * 8 * P:(n + 1) * 8 * P], g.bank[5 + n].bitcast(BF16)[0:6 * H, :])\
              .then_inc(self.copied.sem, 1)

    def vector(self, dve, kept):
        g, nc = self.g, self.g.nc
        t = Tally(dve, self.chain)
        dve.wait_ge(*kept.at(NC))
        nc.vector.reduce_sum(self.glo[:, :], self.MQ[:, :].rearrange("p (b s) -> p b s", s=S), axis=AX_X)\
          .then_inc(self.summed.sem, 1)
        dve.wait_ge(*self.global_.at(1))
        t.done(nc.vector.tensor_scalar(self.cbias[:, :], g.bank[5][:, 0:B], 1.0 / S, g.col("a1_bfq"), ALU.mult, ALU.add))
        nc.vector.tensor_scalar(self.cbias[:, :], self.cbias[:, :], g.col("a1_bfg"), None, ALU.add).then_inc(self.bias.sem, 1)
        dve.wait_ge(*self.acted.at(1))
        ab, a, b = self.AB, self.AB[:, 0, :, :], self.AB[:, 1, :, :]
        t.done(nc.vector.tensor_scalar(self.ez[:, :, :], self.ez[:, :, :], 1.0, None, ALU.add))
        t.done(nc.vector.scalar_tensor_tensor(a, self.ez[:, :, :], -2.0 / (S * S * SCALE), self.ez[:, :, :],
                                              ALU.mult, ALU.mult))
        t.done(nc.vector.scalar_tensor_tensor(b, a, -float(S), self.tp[:, :, :], ALU.mult, ALU.mult))
        for part in range(3):
            src = ab if part == 0 else self.rem
            for m in range(2):
                last = nc.vector.tensor_copy(self.XR[:, :, 3 * m + part, :], src[:, m, :, :])
            if part == 2:
                last.then_inc(self.rows_ready.sem, 2)
                break
            t.done(last)
            for m in range(2):
                last = nc.vector.tensor_tensor(self.rem[:, m, :, :], src[:, m, :, :], self.XR[:, :, 3 * m + part, :],
                                               ALU.subtract)
            t.done(last)

    def sync(self, sp, rows):
        sp.wait_ge(*self.copied.at(2))
        for first, part in ((0, 0), (3, 0), (6, 1)):
            sp.dma_start(rows[first:first + 3, :, :].rearrange("r h t -> (r h) t"),
                         self.AR[3 * H * part:3 * H * part + 3 * H, :]).then_inc(self.written.sem, 16)


class Mask:

    def __init__(self, g):
        self.g = g
        self.loaded, self.made, self.turned, self.copied = (g.sem(f"mask_{w}") for w in ("loaded", "made", "turned", "copied"))

    def sync(self, sp):
        g = self.g
        for i in range(2):
            sp.dma_start(g.PT[i][:, :, :].rearrange("p a b -> p (a b)").bitcast(I32).rearrange("p (n k) -> p n k", k=S),
                         g.io["mask"].rearrange("(n p) k -> p n k", p=P)[:, 8 * i:8 * i + 8, :]).then_inc(self.loaded.sem, 16)

    def vector(self, dve):
        g, nc = self.g, self.g.nc
        dve.wait_ge(*self.loaded.at(32))
        for i in range(2):
            nc.vector.tensor_scalar(g.mask_q[:, i * 8 * S:(i + 1) * 8 * S],
                                    g.PT[i][:, :, :].rearrange("p a b -> p (a b)").bitcast(I32), 0.0, NEG_MASK,
                                    ALU.is_equal, ALU.mult).then_inc(self.made.sem, 1)

    def tensor(self, pe):
        g, nc = self.g, self.g.nc
        for i in range(4):
            pe.wait_ge(*self.made.at(i // 2 + 1))
            bank = g.bank[4 + i].bitcast(BF16)
            for n in range(8):
                b, kt, qt = 2 * i + n // 4, n // 2 % 2, n % 2
                last = nc.tensor.transpose(bank[:, n * P:(n + 1) * P],
                                           g.mask_q[:, b * 2 * S + qt * S + kt * P:b * 2 * S + qt * S + kt * P + P],
                                           g.ident_bf[:, :])
            last.then_inc(self.turned.sem, 1)

    def scalar(self, act):
        g, nc = self.g, self.g.nc
        for i in range(4):
            act.wait_ge(*self.turned.at(i + 1))
            nc.scalar.copy(g.mask_k[:, i * 4 * S:(i + 1) * 4 * S], g.bank[4 + i].bitcast(BF16)).then_inc(self.copied.sem, 1)


class Router:

    def __init__(self, g):
        self.g = g
        self.logits = g.sem(f"router_logits")
        self.chain = g.sem(f"router_chain")
        self.gap = g.sem(f"router_gap")
        self.gap_exp = g.sem(f"router_gap_exp")
        self.routed = g.sem(f"router_routed")
        sb = g.sb
        self.L = sb("router_L", [P, NT, EX])
        self.W1 = sb("router_W1", [P, NT, EX])
        self.W2 = sb("router_W2", [P, NT, EX])
        self.first = sb("router_first", [P, NT, EX])
        self.second = sb("router_second", [P, NT, EX])
        self.m1, self.m2, self.d = (sb(f"router_{n}", [P, NT]) for n in ("m1", "m2", "d"))
        self.gate = sb("router_gate", [P, 2, NT])

    def tensor(self, pe, ready):
        g, nc = self.g, self.g.nc
        bank = g.bank[0][:, 0:NT * EX].rearrange("p (n e) -> p n e", e=EX)
        for n in range(NT):
            if n % TC == 0:
                ready(n // TC)
            last = nc.tensor.matmul(bank[:, n, :], g.XT[:, n * P:(n + 1) * P], g.router_w[:, :], start=True, stop=True)
        last.then_inc(self.logits.sem, 1)

    def scalar(self, act):
        g, nc = self.g, self.g.nc
        act.wait_ge(*self.gap.at(1))
        nc.scalar.activation(self.d[:, :], self.d[:, :], ACT.Exp).then_inc(self.gap_exp.sem, 1)

    def vector(self, dve):
        g, nc = self.g, self.g.nc
        t = Tally(dve, self.chain)
        wide = lambda ap: ap.unsqueeze(2).to_broadcast([P, NT, EX])
        rows = lambda ap: ap.unsqueeze(1).to_broadcast([P, NT, EX])
        L, W1, W2 = self.L[:, :, :], self.W1[:, :, :], self.W2[:, :, :]
        dve.wait_ge(*self.logits.at(1))
        bank = g.bank[0][:, 0:NT * EX].rearrange("p (n e) -> p n e", e=EX)
        t.done(nc.vector.tensor_tensor(L, bank, rows(g.router_b[:, :]), ALU.add))
        for m, out in ((self.m1, self.first), (self.m2, self.second)):
            t.done(nc.vector.reduce_max(m[:, :], L, axis=AX_X))
            t.done(nc.vector.tensor_tensor(W1, L, wide(m[:, :]), ALU.is_equal))
            t.done(nc.vector.tensor_tensor(W1, W1, rows(g.descending[:, :]), ALU.mult))
            t.done(nc.vector.reduce_max(self.d[:, :], W1, axis=AX_X))
            t.done(nc.vector.tensor_tensor(out[:, :, :], W1, wide(self.d[:, :]), ALU.is_equal))
            if m is self.m1:
                t.done(nc.vector.tensor_scalar(W2, self.first[:, :, :], -1e30, None, ALU.mult))
                t.done(nc.vector.tensor_tensor(L, L, W2, ALU.add))
        nc.vector.tensor_tensor(self.d[:, :], self.m2[:, :], self.m1[:, :], ALU.subtract).then_inc(self.gap.sem, 1)
        dve.wait_ge(*self.gap_exp.at(1))
        t.done(nc.vector.tensor_scalar(self.m1[:, :], self.d[:, :], 1.0, None, ALU.add))
        t.done(nc.vector.reciprocal(self.gate[:, 0, :], self.m1[:, :]))
        nc.vector.tensor_tensor(self.gate[:, 1, :], self.d[:, :], self.gate[:, 0, :], ALU.mult)\
          .then_inc(self.routed.sem, 1)


class Experts:

    UNITS = 2 * NC
    TURNS = EX // 2
    FT = FE // P

    def __init__(self, g, router):
        self.g, self.router = g, router
        self.gate_up = g.sem(f"experts_gate_up")
        self.tanh = g.sem(f"experts_tanh")
        self.halved = g.sem(f"experts_halved")
        self.mixed = g.sem(f"experts_mixed")
        self.down = g.sem(f"experts_down")
        self.summed = g.sem(f"experts_summed")
        self.weights_used = g.sem(f"experts_weights_used")
        self.chain = g.sem(f"experts_chain")
        self.weighted = g.sem(f"experts_weighted")
        self.normed = g.sem(f"experts_normed")
        self.added = g.sem(f"experts_added")
        self.stored = g.sem(f"experts_stored")
        self.w_in = [g.sem(f"experts_w_in{i}") for i in range(2)]
        flat = lambda buf: buf[:, :, :].rearrange("p a b -> p (a b)")
        w = [flat(buf) for buf in g.PT]
        self.w12 = [x[:, 0:2 * FE].rearrange("p (a f) -> p a f", a=2) for x in w]
        self.w3 = [x[:, 2 * FE:3 * FE].rearrange("p (n d) -> p n d", d=D) for x in w]
        self.hid = [flat(g.CTX).rearrange("p (n t) -> p n t", n=self.FT), g.CTXT[:, :].rearrange("p (n t) -> p n t", n=self.FT)]
        self.acc = g.V
        self.weight = g.sb("experts_weight", [P, NT, EX])

    def sync(self, sp, out, ready):
        g = self.g

        def load(e, par):
            sp.dma_start(self.w12[par], g.io["ex_w12"][:, e, :, :]).then_inc(self.w_in[par].sem, 16)
            sp.dma_start(self.w3[par], g.io["ex_w3"][:, e, :, :]).then_inc(self.w_in[par].sem, 16)

        ready()
        for par in range(2):
            load(par, par)
        for i in range(1, self.TURNS):
            for par in range(2):
                sp.wait_ge(*self.weights_used.at(2 * i + par - 1))
                load(2 * i + par, par)
        for c in range(NC):
            sp.wait_ge(*self.normed.at(c + 1))
            sp.dma_start(out.rearrange("(t p) d -> p t d", p=P)[:, c * TC:(c + 1) * TC, :],
                         g.X[:, c * TC:(c + 1) * TC, :]).then_inc(self.stored.sem, 16)
        sp.wait_ge(*self.stored.at(16 * NC))

    def tensor(self, pe, ready):
        g, nc = self.g, self.g.nc
        ready()

        def gate_up(u, i):
            e, c = u // NC, u % NC
            if c == 0:
                pe.wait_ge(*self.w_in[e].at((i + 1) * 32))
            for f in range(self.FT):
                if u * self.FT + f >= 2:
                    pe.wait_ge(*self.mixed.at(i * 32 + u * 4 + f - 1))
                for a in range(2):
                    last = nc.tensor.matmul(g.bank[2 * a + f % 2], self.w12[e][:, a, f * P:(f + 1) * P],
                                            g.XT[:, c * CH:(c + 1) * CH], start=True, stop=True)
                last.then_inc(self.gate_up.sem, 1)

        def down(u, i):
            e = u // NC
            pe.wait_ge(*self.mixed.at(i * 32 + u * 4 + 4))
            if u >= 2:
                pe.wait_ge(*self.summed.at(i * 8 + u - 1))
            for t in range(TC):
                for f in range(self.FT):
                    last = nc.tensor.matmul(g.bank[4 + u % 2][:, t * P:(t + 1) * P],
                                            self.hid[u % 2][:, f, t * P:(t + 1) * P], self.w3[e][:, f, :],
                                            start=f == 0, stop=f == self.FT - 1)
            last.then_inc(self.down.sem, 1)
            if u % NC == NC - 1:
                pe.wait_ge(*self.down.at(i * 8 + u + 1))
                pe.sem_inc(self.weights_used.sem, 1)

        with pe.Fori(0, self.TURNS) as i:
            for u in range(self.UNITS + 1):
                if u < self.UNITS:
                    gate_up(u, i)
                if u >= 1:
                    down(u - 1, i)

    def scalar(self, act):
        g, nc = self.g, self.g.nc
        with act.Fori(0, self.TURNS) as i:
            for n in range(self.UNITS * self.FT):
                act.wait_ge(*self.gate_up.at(i * 32 + n + 1))
                if n >= 2:
                    act.wait_ge(*self.mixed.at(i * 32 + n - 1))
                nc.scalar.activation(g.fbuf[n % 2][:, :], g.bank[n % 2], ACT.Tanh, scale=0.5).then_inc(self.tanh.sem, 1)

    def vector(self, dve):
        g, nc = self.g, self.g.nc
        r = self.router
        t = Tally(dve, self.chain)
        w, w2 = self.weight[:, :, :], r.W1[:, :, :]
        gate = lambda k: r.gate[:, k, :].unsqueeze(2).to_broadcast([P, NT, EX])
        dve.wait_ge(*r.routed.at(1))
        t.done(nc.vector.tensor_tensor(w, r.first[:, :, :], gate(0), ALU.mult))
        t.done(nc.vector.tensor_tensor(w2, r.second[:, :, :], gate(1), ALU.mult))
        t.done(nc.vector.tensor_tensor(w, w, w2, ALU.add))
        t.done(nc.vector.tensor_copy(self.acc[:, :, :], g.X[:, :, :]))

        def add(u, i):
            e, c = u // NC, u % NC
            dve.wait_ge(*self.down.at(i * 8 + u + 1))
            if u >= NC:
                dve.wait_ge(*self.summed.at(i * 8 + u - NC + 1))
            for k in range(TC):
                n = c * TC + k
                last = nc.vector.scalar_tensor_tensor(self.acc[:, n, :], g.bank[4 + u % 2][:, k * P:(k + 1) * P],
                                                      self.weight[:, n, bass.ds(2 * i + e, 1)], self.acc[:, n, :],
                                                      ALU.mult, ALU.add)
            last.then_inc(self.summed.sem, 1)

        with dve.Fori(0, self.TURNS) as i:
            for u in range(self.UNITS + 1):
                if u < self.UNITS:
                    for f in range(self.FT):
                        n = u * self.FT + f
                        if f == 0 and u >= 2:
                            dve.wait_ge(*self.down.at(i * 8 + u - 1))
                        dve.wait_ge(*self.tanh.at(i * 32 + n + 1))
                        nc.vector.scalar_tensor_tensor(g.turn[n % 2][:, :], g.fbuf[n % 2][:, :], 1.0, g.bank[n % 2],
                                                       ALU.add, ALU.mult).then_inc(self.halved.sem, 1)
                        dve.wait_ge(*self.halved.at(i * 32 + n + 1))
                        nc.vector.scalar_tensor_tensor(self.hid[u % 2][:, f, :], g.turn[n % 2][:, :], 0.5,
                                                       g.bank[2 + n % 2], ALU.mult, ALU.mult)\
                          .then_inc(self.mixed.sem, 1)
                if u >= 1:
                    add(u - 1, i)
        dve.wait_ge(*self.summed.at(EX * NC))
        for c in range(NC):
            layernorm(g, t, self.acc[:, c * TC:(c + 1) * TC, :], g.X[:, c * TC:(c + 1) * TC, :]).then_inc(self.normed.sem, 1)


WEIGHTS = ["a0_qa", "a0_qb", "a0_ka", "a0_kb", "a0_v", "a0_o",
           "a1_q", "a1_k", "a1_v", "a1_o", "a1_fq", "a1_fg",
           "x1_q", "x1_k", "x1_v", "x1_o", "f0_q", "f0_k", "f0_v", "f0_o"]
COLUMNS = ["a1_bq", "a1_bk", "a1_bfq", "a1_bfg", "f0_g1", "f0_g2"]
ROWVECS = ["a1_bv", "a1_bo", "x1_bo"]


class Globals:

    def __init__(self, nc, ctx, io):
        self.nc, self.ctx, self.io = nc, ctx, io
        self.shared = {}

    def sem(self, name):
        return Signal(self.ctx.enter_context(self.nc.semaphore(name)), 0)

    def shared_sem(self, name, total):
        if name not in self.shared:
            self.shared[name] = [self.sem(name).sem, 0]
        sem, base = self.shared[name]
        self.shared[name][1] += total
        return Signal(sem, base)

    def sb(self, name, shape, dt=F32):
        return self.ctx.enter_context(self.nc.sbuf_tensor(name, shape, dt))

    def allocate(self):
        nc = self.nc
        sb = self.sb
        self.X = sb("X", [P, NT, D])
        self.XT = sb("XT", [P, T])
        self.CTX = sb("CTX", [P, NT, D])
        self.CTXT = sb("CTXT", [P, T])
        self.V = sb("V", [P, NT, D])
        self.CX = sb("CX", [P, NT, D])
        self.CXT = sb("CXT", [P, 2, CH])
        self.Q6 = [sb(f"Q6_{i}", [P, H, S], BF16) for i in range(2)]
        self.K6 = [sb(f"K6_{i}", [P, H, S], BF16) for i in range(2)]
        self.VA = [sb(f"VA_{i}", [P, 2, H, PVW]) for i in range(2)]
        self.PT = [sb(f"PT_{i}", [P, 4, 2 * S]) for i in range(2)]
        self.OT = [sb(f"OT_{i}", [P, 4, S]) for i in range(2)]
        self.MS = sb("MS", [P, 2, H])
        self.MB = [sb(f"MB_{i}", [P, 2, 16], BF16) for i in range(2)]
        self.MT = [sb(f"MT_{i}", [16, S], BF16) for i in range(2)]
        self.rsum = sb("rsum", [P, H])
        self.fbuf = [sb(f"fbuf{i}", [P, CH]) for i in range(2)]
        self.rbuf = [sb(f"rbuf{i}", [P, CH]) for i in range(2)]
        self.turn = [sb(f"turn{i}", [P, CH]) for i in range(2)]
        self.parts = [sb(f"parts{i}", [P, 3, CH], BF16) for i in range(2)]
        self.Y = sb("Y", [P, TC, D])
        self.stats = sb("stats", [P, TC, 6])
        self.meanvar = sb("meanvar", [P, TC, 2])
        self.var = sb("var", [P, TC])
        self.rstd = sb("rstd", [P, TC])
        self.half = sb("half", [P, TC])
        self.square = sb("square", [P, TC])
        self.ident = sb("ident", [P, P])
        self.ident_bf = sb("ident_bf", [P, P], BF16)
        self.cos = sb("cos", [P, S])
        self.sin = sb("sin", [P, S])
        self.W = sb("W", [P, len(WEIGHTS), P])
        self.cols = sb("cols", [P, len(COLUMNS)])
        self.rowvecs = sb("rowvecs", [1, len(ROWVECS), D])
        self.ones_row = sb("ones_row", [1, P])
        self.causal_q = sb("causal_q", [P, 2 * S], BF16)
        self.causal_k = sb("causal_k", [P, 2 * S], BF16)
        PS = self.ctx.enter_context(nc.psum_tensor("PS", [P, 8, CH], F32))
        self.bank = [PS[:, i, :] for i in range(8)]
        self.bank2 = [PS[:, 2 * i:2 * i + 2, :] for i in range(2)]
        self.aux_bf = PS[:, 7, :].bitcast(BF16)
        self.mask_q = sb("mask_q", [P, B * 2 * S], BF16)
        self.mask_k = sb("mask_k", [P, B * 2 * S], BF16)
        self.depth_q = sb("depth_q", [P, P], BF16)
        self.depth_k = sb("depth_k", [P, P], BF16)
        self.router = sb("router", [P, P])
        self.earlier = sb("earlier", [P, 2, S])
        self.iota = sb("iota", [P, P])
        self.f0_w12 = sb("f0_w12", [P, 2, F0])
        self.f0_w3 = sb("f0_w3", [P, 3, D])
        self.upz = sb("upz", [P, 2 * H])
        self.router_w = sb("router_w", [P, EX])
        self.router_b = sb("router_b", [P, EX])
        self.descending = sb("descending", [P, EX])

    def w(self, name):
        return self.W[:, WEIGHTS.index(name), :]

    def col(self, name):
        i = COLUMNS.index(name)
        return self.cols[:, i:i + 1]

    def row(self, name):
        return self.rowvecs[0:1, ROWVECS.index(name), :]


def program(nc, io, out):
    with ExitStack() as ctx:
        g = Globals(nc, ctx, io)
        g.allocate()
        sem = g.sem
        dram = lambda name, shape, dt: nc.dram_tensor(name, shape, dt, kind="Internal").ap()
        rows_q = [dram(f"rows_q{i}", (ROWS, H, T), BF16) for i in range(2)]
        rows_k = [dram(f"rows_k{i}", (ROWS, H, T), BF16) for i in range(2)]
        rows_x = dram("rows_x", (9, H, T), BF16)
        mask = Mask(g)

        weights_in = sem("weights_in")
        x_in, xt_in, ctx_in = sem("x_in"), sem("xt_in"), sem("ctx_in")
        zeroed = sem("zeroed")
        const_rows = [sem(f"const_rows{i}") for i in range(4)]

        def chunks(ap):
            return [ap[:, c * CH:(c + 1) * CH] for c in range(NC)]

        xt, ctxt = chunks(g.XT[:, :]), chunks(g.CTXT[:, :])

        jobs = []
        for c in range(NC):
            for wa, wb, to in (("a0_qa", "a0_qb", rows_q[0]), ("a0_ka", "a0_kb", rows_k[0])):
                jobs.append(dict(kind="rope", w=[g.w(wa), g.w(wb)], src=xt[c], to=to, query=to is rows_q[0]))
        split_a0 = Split(g, "sa0", jobs, (g.w("a0_v"), g.XT, None), NC)
        core_a0 = Core(g, "ca0", B, 2)
        post_a0 = Post(g, "pa0", g.w("a0_o"))

        jobs = []
        for c in range(NC):
            jobs.append(dict(kind="sbuf", src=xt[c], to=rows_q[1], query=True))
            jobs.append(dict(kind="sbuf", src=ctxt[c], to=rows_k[1], query=False))
        split_x0 = Split(g, "sx0", jobs, None, NC)
        core_x0 = Core(g, "cx0", B, 2, causal=True, bias=(g.causal_q[:, :], g.causal_k[:, :]))
        post_x0 = Post(g, "px0")

        depths = Depths(g, "f0")
        jobs = [dict(kind="psum", w=[g.w("f0_q")], src=depths.HT[:, :], to=rows_q[0], query=True),
                dict(kind="psum", w=[g.w("f0_k")], src=depths.HT[:, :], to=rows_k[0], query=False)]
        split_f0 = Split(g, "sf0", jobs, (g.w("f0_v"), depths.HT, None), 1)
        core_f0 = Core(g, "cf0", depths.NP, 1, bias=(g.depth_q[:, :], g.depth_k[:, :]))

        gauss = Gauss(g, "ga1")
        jobs = []
        for c in range(NC):
            jobs.append(dict(kind="keep", w=[g.w("a1_q")], src=xt[c], bias=g.col("a1_bq"),
                             keep=gauss.MQ[:, c * CH:(c + 1) * CH], to=rows_q[1], query=True))
            jobs.append(dict(kind="psum", w=[g.w("a1_k")], src=xt[c], bias=g.col("a1_bk"), to=rows_k[1], query=False))
        split_a1 = Split(g, "sa1", jobs, (g.w("a1_v"), g.XT, g.row("a1_bv")), NC)
        core_a1 = Core(g, "ca1", B, 2, xrows=9)
        post_a1 = Post(g, "pa1", g.w("a1_o"), g.row("a1_bo"))

        jobs = []
        for c in range(NC):
            jobs.append(dict(kind="psum", w=[g.w("x1_q")], src=xt[c], to=rows_q[0], query=True))
            jobs.append(dict(kind="psum", w=[g.w("x1_k")], src=ctxt[c], to=rows_k[0], query=False))
        split_x1 = Split(g, "sx1", jobs, (g.w("x1_v"), g.CTXT, None), NC)
        core_x1 = Core(g, "cx1", B, 2, bias="batch")
        post_x1 = Post(g, "px1", g.w("x1_o"), g.row("x1_bo"))
        router = Router(g)
        experts = Experts(g, router)

        block = ctx.enter_context(nc.Block())

        def const_rows_in(sp, n):
            for i in range(2):
                sp.dma_start(g.K6[i][XROW:XROW + 16, :, :], io["k_extra"][n % 3]).then_inc(const_rows[n].sem, 16)
                if n == 1:
                    sp.dma_start(g.Q6[i][XROW:XROW + 16, :, :], io["q_extra"]).then_inc(const_rows[n].sem, 16)

        @block.sync
        def _(sp):
            sp.dma_start(g.W[:, :, :], io["weights"]).then_inc(weights_in.sem, 16)
            sp.dma_start(g.XT[:, :], io["xt"]).then_inc(xt_in.sem, 16)
            for ap, name in ((g.ident, "ident"), (g.ident_bf, "ident_bf"), (g.cos, "cos"), (g.sin, "sin"),
                             (g.cols, "cols"), (g.causal_q, "causal_q"), (g.causal_k, "causal_k"), (g.ones_row, "ones_row"),
                             (g.depth_q, "depth_q"), (g.depth_k, "depth_k"), (g.router, "router"), (g.iota, "iota"),
                             (g.upz, "upz"), (g.router_w, "router_w"), (g.router_b, "router_b"),
                             (g.descending, "descending")):
                sp.dma_start(ap[:, :], io[name]).then_inc(weights_in.sem, 16)
            for ap, name in ((g.rowvecs, "rowvecs"), (g.earlier, "earlier"), (g.f0_w12, "f0_w12"), (g.f0_w3, "f0_w3")):
                sp.dma_start(ap[:, :, :], io[name]).then_inc(weights_in.sem, 16)
            mask.sync(sp)
            sp.dma_start(g.X[:, :, :], io["x"].rearrange("(t p) d -> p t d", p=P)).then_inc(x_in.sem, 16)
            sp.dma_start(g.CTX[:, :, :], io["ctx"].rearrange("(t p) d -> p t d", p=P)).then_inc(ctx_in.sem, 16)
            sp.dma_start(g.CTXT[:, :], io["ctxt"]).then_inc(ctx_in.sem, 16)
            split_a0.sync(sp)
            sp.wait_ge(*zeroed.at(5))
            split_a0.wait_written(sp)
            core_a0.sync(sp, rows_q[0], rows_k[0])
            split_x0.sync(sp)
            sp.wait_ge(*core_a0.st_ready.at(8 * B))
            const_rows_in(sp, 1)
            split_x0.wait_written(sp)
            core_x0.sync(sp, rows_q[1], rows_k[1])
            split_f0.sync(sp)
            sp.wait_ge(*core_x0.st_ready.at(8 * B))
            const_rows_in(sp, 0)
            split_f0.wait_written(sp)
            core_f0.sync(sp, rows_q[0], rows_k[0])
            split_a1.sync(sp)
            sp.wait_ge(*core_f0.st_ready.at(8 * depths.NP))
            const_rows_in(sp, 2)
            gauss.sync(sp, rows_x)
            split_a1.wait_written(sp)
            sp.wait_ge(*gauss.written.at(48))
            core_a1.sync(sp, rows_q[1], rows_k[1], rows_x)
            split_x1.sync(sp)
            sp.wait_ge(*core_a1.st_ready.at(8 * B))
            const_rows_in(sp, 3)
            split_x1.wait_written(sp)
            core_x1.sync(sp, rows_q[0], rows_k[0])

            def ready():
                sp.wait_ge(*core_x1.pv_done.at(4 * B))
            experts.sync(sp, out, ready)

        @block.tensor
        def _(pe):
            pe.wait_ge(*weights_in.at(16 * 21))

            def ready(c):
                if c == 0:
                    pe.wait_ge(*xt_in.at(16))
                    pe.wait_ge(*mask.copied.at(4))
            mask.tensor(pe)
            split_a0.tensor(pe, ready)

            def ready():
                pe.wait_ge(*split_a0.r1_ready.at(2 * NC))
                pe.wait_ge(*split_a0.v_ready.at(NC))
                pe.wait_ge(*zeroed.at(5))
            core_a0.tensor(pe, ready)

            def ready():
                pe.wait_ge(*core_a0.cx_done.at(NT))
                pe.wait_ge(*core_a0.ot_done.at(4 * B))
                pe.wait_ge(*core_a0.mx_done.at(16 * B))
            post_a0.tensor(pe, ready)
            split_x0.tensor(pe, lambda c: None)

            def ready():
                pe.wait_ge(*const_rows[1].at(64))
                pe.wait_ge(*post_a0.xt_ready.at(NC))
            core_x0.tensor(pe, ready)

            def ready():
                pe.wait_ge(*core_x0.cx_done.at(NT))
                pe.wait_ge(*core_x0.ot_done.at(4 * B))
                pe.wait_ge(*core_x0.mx_done.at(16 * B))
            post_x0.tensor(pe, ready)

            def ready(c):
                pe.wait_ge(*post_x0.xt_ready.at(c + 1))
            depths.select_tensor(pe, ready)

            def ready(c):
                pe.wait_ge(*depths.h_ready.at(1))
            split_f0.tensor(pe, ready)

            def ready():
                pe.wait_ge(*split_f0.r1_ready.at(2))
                pe.wait_ge(*split_f0.v_ready.at(1))
                pe.wait_ge(*const_rows[0].at(32))
            core_f0.tensor(pe, ready)

            def ready():
                pe.wait_ge(*core_f0.cx_done.at(depths.NP))
                pe.wait_ge(*core_f0.ot_done.at(4 * depths.NP))
                pe.wait_ge(*core_f0.mx_done.at(8 * depths.NP))
            depths.feed_tensor(pe, ready)

            def ready(c):
                pe.wait_ge(*depths.xt_ready.at(c + 1))
            split_a1.tensor(pe, ready)
            gauss.tensor(pe)

            def ready():
                pe.wait_ge(*split_a1.r1_ready.at(2 * NC))
                pe.wait_ge(*split_a1.v_ready.at(NC))
                pe.wait_ge(*gauss.copied.at(2))
                pe.wait_ge(*const_rows[2].at(32))
            core_a1.tensor(pe, ready)

            def ready():
                pe.wait_ge(*core_a1.cx_done.at(NT))
                pe.wait_ge(*core_a1.ot_done.at(4 * B))
                pe.wait_ge(*core_a1.mx_done.at(16 * B))
            post_a1.tensor(pe, ready)

            def ready(c):
                pe.wait_ge(*post_a1.xt_ready.at(c + 1))
            split_x1.tensor(pe, ready)

            def ready():
                pe.wait_ge(*split_x1.r1_ready.at(2 * NC))
                pe.wait_ge(*split_x1.v_ready.at(NC))
                pe.wait_ge(*const_rows[3].at(32))
            core_x1.tensor(pe, ready)

            def ready():
                pe.wait_ge(*core_x1.cx_done.at(NT))
                pe.wait_ge(*core_x1.ot_done.at(4 * B))
                pe.wait_ge(*core_x1.mx_done.at(16 * B))
            post_x1.tensor(pe, ready)

            def ready(c):
                pe.wait_ge(*post_x1.xt_ready.at(c + 1))
            router.tensor(pe, ready)

            def ready():
                pe.wait_ge(*router.chain.at(1))
            experts.tensor(pe, ready)

        @block.scalar
        def _(act):
            mask.scalar(act)
            split_a0.scalar(act)
            core_a0.scalar(act)
            post_a0.scalar(act)
            def ready(a, c):
                if c == 0:
                    a.wait_ge(*ctx_in.at(32))
                a.wait_ge(*post_a0.xt_ready.at(c + 1))
            split_x0.scalar(act, ready)
            core_x0.scalar(act)
            post_x0.scalar(act)
            depths.select_scalar(act)
            split_f0.scalar(act)
            core_f0.scalar(act)
            depths.feed_scalar(act)
            split_a1.scalar(act)
            gauss.scalar(act)
            core_a1.scalar(act)
            post_a1.scalar(act)
            split_x1.scalar(act)
            core_x1.scalar(act)
            post_x1.scalar(act)
            router.scalar(act)
            experts.scalar(act)

        @block.vector
        def _(dve):
            for buf in (*g.Q6, *g.K6):
                last = nc.vector.memset(buf[:, :, :], 0.0)
            last.then_inc(zeroed.sem, 1)
            dve.wait_ge(*zeroed.at(1))
            for buf in g.K6:
                last = nc.vector.memset(buf[MROW:MROW + 2, :, :], 1.0)
            last.then_inc(zeroed.sem, 1)
            for buf in g.VA:
                last = nc.vector.memset(buf[:, :, :, :], 0.0)
            last.then_inc(zeroed.sem, 1)
            dve.wait_ge(*zeroed.at(3))
            for buf in g.VA:
                last = nc.vector.memset(buf[:, :, :, DH:DH + 1], 1.0)
            last.then_inc(zeroed.sem, 2)
            dve.wait_ge(*weights_in.at(16 * 21))
            mask.vector(dve)
            split_a0.vector(dve)
            core_a0.vector(dve)
            dve.wait_ge(*x_in.at(16))
            post_a0.vector(dve)
            split_x0.vector(dve)
            core_x0.vector(dve)
            dve.wait_ge(*core_x0.cx_done.at(NT))
            post_x0.vector(dve)
            depths.select_vector(dve)
            split_f0.vector(dve)
            core_f0.vector(dve)
            depths.feed_vector(dve)
            split_a1.vector(dve)
            gauss.vector(dve, split_a1.kept)
            core_a1.vector(dve)
            post_a1.vector(dve)
            split_x1.vector(dve)
            core_x1.vector(dve)
            post_x1.vector(dve)
            router.vector(dve)
            experts.vector(dve)

        @block.gpsimd
        def _(pool):
            split_a0.gpsimd(pool)
            def ready():
                pool.wait_ge(*zeroed.at(5))
                pool.wait_ge(*split_a0.v_ready.at(NC))
            core_a0.gpsimd(pool, g.V, ready)
            split_x0.gpsimd(pool)
            def ready():
                pool.wait_ge(*ctx_in.at(32))
                pool.wait_ge(*core_a0.pv_done.at(4 * B))
            core_x0.gpsimd(pool, g.CTX, ready)
            split_f0.gpsimd(pool)
            def ready():
                pool.wait_ge(*split_f0.v_ready.at(1))
                pool.wait_ge(*core_x0.pv_done.at(4 * B))
            core_f0.gpsimd(pool, g.V, ready)
            split_a1.gpsimd(pool)
            def ready():
                pool.wait_ge(*split_a1.v_ready.at(NC))
                pool.wait_ge(*core_f0.pv_done.at(4 * depths.NP))
            core_a1.gpsimd(pool, g.V, ready)
            split_x1.gpsimd(pool)
            def ready():
                pool.wait_ge(*split_x1.v_ready.at(NC))
                pool.wait_ge(*core_a1.pv_done.at(4 * B))
            core_x1.gpsimd(pool, g.V, ready)


DFIRST = np.arange(D).reshape(H, DH).T.reshape(-1)


def rope_order(w, second):
    h, j = DFIRST // DH, DFIRST % DH
    i, high = j % (DH // 2), j >= DH // 2
    odd = high != second
    return w[h * DH + 2 * i + odd]


def constants():
    bf = mybir.dt.np(BF16)
    out = {}
    inv_freq = (np.float32(1.0) / np.float32(10000.0) ** (np.arange(0, DH, 2, dtype=np.float32) / np.float32(DH))).astype(np.float32)
    ang = (np.arange(S, dtype=np.float32)[None, :] * inv_freq[DFIRST % (DH // 2)][:, None]).astype(np.float32)
    sign = np.where(DFIRST % DH < DH // 2, -1.0, 1.0).astype(np.float32)[:, None]
    out["cos"] = np.cos(ang).astype(np.float32)
    out["sin"] = (np.sin(ang) * sign).astype(np.float32)
    out["ident"] = np.eye(P, dtype=np.float32)
    out["ident_bf"] = np.eye(P, dtype=np.float32).astype(bf)
    out["ones_row"] = np.ones((1, P), np.float32)
    q, k = np.arange(P)[:, None], np.arange(P)[None, :]
    cq = np.zeros((P, 2 * S), np.float32)
    cq[:, 0:P] = np.where(k > q, NEG_CAUSAL, 0.0)
    cq[:, 2 * P + P:4 * P] = cq[:, 0:P]
    ck = np.zeros((P, 2 * S), np.float32)
    ck[:, 0:P] = cq[:, 0:P].T
    ck[:, 2 * P:3 * P] = cq[:, 0:P].T
    out["causal_q"], out["causal_k"] = cq.astype(bf), ck.astype(bf)

    dq = np.where((q // SEL != k // SEL) | (k > q), NEG_CAUSAL, 0.0)
    out["depth_q"], out["depth_k"] = dq.astype(bf), np.ascontiguousarray(dq.T).astype(bf)
    tok = np.arange(S)
    out["earlier"] = (tok[None, None, :] < (q + P * np.arange(2)[None, :])[:, :, None]).astype(np.float32)
    out["descending"] = np.broadcast_to(np.arange(EX, 0, -1, dtype=np.float32)[None], (P, EX)).copy()
    out["iota"] = np.broadcast_to(np.arange(P, dtype=np.float32)[None], (P, P)).copy()

    def three(a):
        a = a.astype(np.float32)
        p1 = a.astype(bf)
        p2 = (a - p1.astype(np.float32)).astype(bf)
        p3 = (a - p1.astype(np.float32) - p2.astype(np.float32)).astype(bf)
        return [p1, p2, p3]

    kx = np.zeros((4, 16, H, S), bf)
    key = np.arange(S, dtype=np.float32)
    kx[1, 0:3] = key.astype(bf)
    j = key - S // 2
    sq1 = (j * j).astype(bf)
    sq2 = (j * j - sq1.astype(np.float32)).astype(bf)
    kx[2, 0:3], kx[2, 3:6], kx[2, 6:9] = sq1, sq2, j.astype(bf)
    out["k_extra"] = kx
    slopes = np.cumprod(np.full((H,), 2.0 ** (-8.0 / H), np.float32)).astype(np.float32)
    qx = np.zeros((16, H, S), bf)
    for n, part in enumerate(three(slopes * np.float32(DH ** 0.5))):
        qx[n] = part[:, None]
    out["q_extra"] = qx
    return out


def layout(a):
    io = {}
    w = {
        "a0_qa": rope_order(a["L0_attn_Wq"], False).T, "a0_qb": rope_order(a["L0_attn_Wq"], True).T,
        "a0_ka": rope_order(a["L0_attn_Wk"], False).T, "a0_kb": rope_order(a["L0_attn_Wk"], True).T,
        "a0_v": a["L0_attn_Wv"].T, "a0_o": a["L0_attn_Wo"].T,
        "a1_q": a["L1_attn_wq"], "a1_k": a["L1_attn_wk"], "a1_v": a["L1_attn_wv"], "a1_o": a["L1_attn_wo"],
        "a1_fq": a["L1_attn_wfq"], "a1_fg": a["L1_attn_wfg"],
        "x1_q": a["L1_xattn_Wq"].T, "x1_k": a["L1_xattn_Wk"].T, "x1_v": a["L1_xattn_Wv"].T, "x1_o": a["L1_xattn_Wo"].T,
        "f0_q": a["L0_ffn_W_qkv"][0:D].T, "f0_k": a["L0_ffn_W_qkv"][D:2 * D].T, "f0_v": a["L0_ffn_W_qkv"][2 * D:].T,
        "f0_o": a["L0_ffn_W_out"].T,
    }
    for n in w:
        w[n] = w[n][DFIRST] if n in ("a0_qa", "a0_qb", "a0_ka", "a0_kb") else w[n][DFIRST][:, DFIRST]
    io["weights"] = np.stack([w[n] for n in WEIGHTS], axis=1)
    cols = {"a1_bq": a["L1_attn_bq"], "a1_bk": a["L1_attn_bk"], "a1_bfq": a["L1_attn_bfq"], "a1_bfg": a["L1_attn_bfg"],
            "f0_g1": a["L0_ffn_g1"], "f0_g2": a["L0_ffn_g2"]}
    io["cols"] = np.stack([cols[n][DFIRST] for n in COLUMNS], axis=1)
    rows = {"a1_bv": a["L1_attn_bv"], "a1_bo": a["L1_attn_bo"], "x1_bo": a["L1_xattn_bo"]}
    io["rowvecs"] = np.stack([rows[n][DFIRST] for n in ROWVECS])[None]
    io["router"] = np.repeat(a["L0_ffn_w_router"][DFIRST][:, None], P, axis=1)
    io["f0_w12"] = np.stack([a["L0_ffn_W1"].T[DFIRST], a["L0_ffn_W2"].T[DFIRST]], axis=1)
    w3 = np.zeros((3 * P, D), np.float32)
    w3[0:F0] = a["L0_ffn_W3"].T[:, DFIRST]
    io["f0_w3"] = w3.reshape(3, P, D).transpose(1, 0, 2)
    upz = np.zeros((D, 2 * H), np.float32)
    for n, name in enumerate(("L1_attn_up", "L1_attn_uz")):
        for h in range(H):
            upz[np.arange(DH) * H + h, n * H + h] = a[name][h, 0]
    io["upz"] = upz
    io["router_w"] = a["L1_ffn_router_w"].T[DFIRST]
    io["router_b"] = np.repeat(a["L1_ffn_router_b"][None], P, axis=0)
    io["ex_w12"] = np.stack([a[f"L1_ffn_{n}_w"].transpose(2, 0, 1)[DFIRST] for n in ("gate", "up")], axis=2)
    io["ex_w3"] = a["L1_ffn_down_w"][:, DFIRST].reshape(EX, D, FE // P, P).transpose(3, 0, 2, 1)
    io["mask"] = a["mask_Bx1xSxS2_if1"].reshape(B * S, S)
    io["x"] = a["x"].reshape(T, D)[:, DFIRST]
    io["xt"] = io["x"].T
    io["ctx"] = a["ctx_1024"].reshape(T, D)[:, DFIRST]
    io["ctxt"] = io["ctx"].T
    return io


def kernel(**inputs):
    import concourse.bacc as _bacc
    from concourse.bass_utils import run_bass_kernel_spmd as _run

    arrays = {n: np.ascontiguousarray(v) for n, v in
              (layout({k: np.asarray(v) for k, v in inputs.items()}) | constants()).items()}
    nc = _bacc.Bacc("TRN2", target_bir_lowering=False, num_devices=1)
    io = {n: nc.dram_tensor(f"in_{n}", v.shape, mybir.dt.from_np(v.dtype), kind="ExternalInput").ap()
          for n, v in arrays.items()}
    out = nc.dram_tensor("out_0", (T, D), F32, kind="ExternalOutput").ap()
    program(nc, io, out)
    r = _run(nc, [{f"in_{n}": v for n, v in arrays.items()}], core_ids=[0])
    return r.results[0]["out_0"][:, np.argsort(DFIRST)].reshape(B, S, D)
```

```python
from contextlib import ExitStack

import numpy as np

import concourse.bass as bass
from concourse import mybir

F32 = mybir.dt.float32
BF16 = mybir.dt.bfloat16
I32 = mybir.dt.int32
U32 = mybir.dt.uint32
ALU = mybir.AluOpType
ACT = mybir.ActivationFunctionType
AX_X = mybir.AxisListType.X

P = 128
D = 128
H = 16
DH = D // H
B = 8
S = 256
T = B * S
NT = T // P
CH = 512
TC = CH // P
NC = T // CH
SCALE = float(DH) ** -0.5
EPS = 1e-5
PARTS = 6
ROWS = PARTS * DH
XROW = ROWS
MROW = 96
NEG_CAUSAL = -1e30
NEG_MASK = -1e20
PVW = 32
NPARTS = 4
SEL = 64
F0 = 341
EX = 8
FE = 512


class Batch:

    def __init__(self, c, i=None):
        self.no = c if i is None else 2 * i + c
        self.par = c % 2
        self.use = c // 2 if i is None else i + c // 2
        self.first = c if i is None else None


class Signal:

    def __init__(self, sem, base):
        self.sem, self.base = sem, base

    def at(self, n):
        return self.sem, self.base + n


class Tally:

    def __init__(self, eng, raised):
        self.eng, self.raised, self.n, self.base = eng, raised, 0, 0

    def done(self, ins):
        self.n += 1
        ins.then_inc(self.raised.sem, 1)
        self.eng.wait_ge(*self.raised.at(self.base + self.n))

    def loop(self, i, per):
        self.start, self.per, self.base = self.n, per, i * per

    def end(self, turns):
        assert self.n - self.start == self.per, (self.n - self.start, self.per)
        self.n += self.per * (turns - 1)
        self.base = 0



class Split:

    def __init__(self, g, name, jobs, values, nchunks):
        self.g, self.jobs, self.values, self.nchunks = g, jobs, values, nchunks
        self.has_pe = [j for j in jobs if j["kind"] != "sbuf"]
        kinds = [j["kind"] for j in jobs]
        n, n_v, n_rope = len(jobs), nchunks if values else 0, kinds.count("rope")
        self.projected = g.shared_sem("split_projected", len(self.has_pe))
        self.turned = g.shared_sem("split_turned", n_rope)
        self.rotated = g.shared_sem("split_rotated", n_rope)
        self.s1_ready = g.shared_sem("split_s1_ready", n)
        self.r1_ready = g.shared_sem("split_r1_ready", n)
        self.s2_ready = g.shared_sem("split_s2_ready", n)
        self.s3_ready = g.shared_sem("split_s3_ready", n)
        self.v_projected = g.shared_sem("split_v_projected", n_v)
        self.v_ready = g.shared_sem("split_v_ready", n_v)
        self.kept = g.shared_sem("split_kept", kinds.count("keep"))
        self.written = [g.shared_sem(f"split_written{i}", 48 * len(jobs[i::NPARTS])) for i in range(NPARTS)]
        for n, j in enumerate(self.has_pe):
            j["n_pe"] = n
        for n, j in enumerate(j for j in jobs if j["kind"] == "keep"):
            j["n_keep"] = n

        self.nbuf = 2 if n_rope else 4

    def bank(self, job):
        return 4 // self.nbuf * (job["n_pe"] % self.nbuf)

    def tensor(self, pe, ready):
        g, nc = self.g, self.g.nc
        per = len(self.jobs) // self.nchunks
        for c in range(self.nchunks):
            ready(c)
            for j in self.jobs[c * per:(c + 1) * per]:
                if j["kind"] == "sbuf":
                    continue
                n, b = j["n_pe"], self.bank(j)
                if n >= self.nbuf:
                    before = self.has_pe[n - self.nbuf]
                    if before["kind"] == "rope":
                        pe.wait_ge(*self.turned.at(before["n_pe"] + 1))
                    elif before["kind"] == "keep":
                        pe.wait_ge(*self.kept.at(before["n_keep"] + 1))
                    else:
                        pe.wait_ge(*self.r1_ready.at(self.jobs.index(before) + 1))
                for i, w in enumerate(j["w"]):
                    last = nc.tensor.matmul(g.bank[b + i][:, :], w, j["src"], start=True, stop=True)
                last.then_inc(self.projected.sem, 1)
            if self.values:
                w, src, bias = self.values
                if c >= 1:
                    pe.wait_ge(*self.v_ready.at(c))
                if bias is not None:
                    nc.tensor.matmul(g.bank[4][:, :].rearrange("p (t d) -> p t d", t=TC), g.ones_row[0:1, :],
                                     bias.unsqueeze(1).to_broadcast([1, TC, D]), start=True, stop=False)
                for t in range(TC):
                    last = nc.tensor.matmul(g.bank[4][:, t * P:(t + 1) * P], src[:, (c * TC + t) * P:(c * TC + t + 1) * P],
                                            w, start=bias is None, stop=bias is None or t == TC - 1)
                last.then_inc(self.v_projected.sem, 1)

    def scalar(self, act, ready=None):
        g, nc = self.g, self.g.nc
        per = len(self.jobs) // self.nchunks

        def first_part(n):
            j = self.jobs[n]
            if n % per == 0 and ready:
                ready(act, n // per)
            if n >= NPARTS:
                act.wait_ge(*self.written[n % NPARTS].at(48 * (n // NPARTS)))
            s1 = g.parts[n % NPARTS][:, 0, :]
            src = j.get("src")
            if j["kind"] == "rope":
                act.wait_ge(*self.rotated.at(j["n_pe"] + 1))
                src = g.fbuf[n % 2][:, :]
            elif j["kind"] == "psum":
                act.wait_ge(*self.projected.at(j["n_pe"] + 1))
                src = g.bank[self.bank(j)][:, :]
            elif j["kind"] == "keep":
                act.wait_ge(*self.projected.at(j["n_pe"] + 1))
                nc.scalar.activation(j["keep"], g.bank[self.bank(j)][:, :], ACT.Identity,
                                     bias=j["bias"]).then_inc(self.kept.sem, 1)
                act.wait_ge(*self.kept.at(j["n_keep"] + 1))
                src = j["keep"]
            if j["kind"] == "psum" and j.get("bias") is not None:
                nc.scalar.activation(s1, src, ACT.Identity, bias=j["bias"]).then_inc(self.s1_ready.sem, 1)
            else:
                nc.scalar.copy(s1, src).then_inc(self.s1_ready.sem, 1)

        def second_part(n):
            act.wait_ge(*self.r1_ready.at(n + 1))
            nc.scalar.copy(g.parts[n % NPARTS][:, 1, :], g.rbuf[n % 2][:, :]).then_inc(self.s2_ready.sem, 1)

        for n in range(len(self.jobs) + 1):
            if n < len(self.jobs):
                first_part(n)
            if n >= 1:
                second_part(n - 1)
            if self.values and n % per == 0 and n >= per:
                c = n // per - 1
                act.wait_ge(*self.v_projected.at(c + 1))
                nc.scalar.copy(g.V[:, c * TC:(c + 1) * TC, :], g.bank[4][:, :].rearrange("p (t d) -> p t d", t=TC))\
                   .then_inc(self.v_ready.sem, 1)

    def vector(self, dve):
        g, nc = self.g, self.g.nc
        for n, j in enumerate(self.jobs):
            if j["kind"] == "rope":
                dve.wait_ge(*self.projected.at(j["n_pe"] + 1))
                if j["n_pe"] >= 1:
                    dve.wait_ge(*self.rotated.at(j["n_pe"]))
                b = self.bank(j)
                for i, table in enumerate((g.cos, g.sin)):
                    last = nc.vector.tensor_tensor(
                        g.turn[i][:, :].rearrange("p (b s) -> p b s", s=S),
                        g.bank[b + i][:, :].rearrange("p (b s) -> p b s", s=S),
                        table[:, :].unsqueeze(1).to_broadcast([P, CH // S, S]), ALU.mult)
                last.then_inc(self.turned.sem, 1)
                src = g.fbuf[n % 2][:, :]
            elif j["kind"] == "psum":
                src = g.bank[self.bank(j)][:, :]
            else:
                src = j["keep"] if j["kind"] == "keep" else j["src"]
            dve.wait_ge(*self.s1_ready.at(n + 1))
            if n >= 2:
                dve.wait_ge(*self.s3_ready.at(n - 1))
            s1 = g.parts[n % NPARTS][:, 0, :]
            if j["kind"] == "psum" and j.get("bias") is not None:
                ins = nc.vector.scalar_tensor_tensor(g.rbuf[n % 2][:, :], src, j["bias"], s1, ALU.add, ALU.subtract)
            else:
                ins = nc.vector.tensor_tensor(g.rbuf[n % 2][:, :], src, s1, ALU.subtract)
            ins.then_inc(self.r1_ready.sem, 1)

    def gpsimd(self, pool):
        g, nc = self.g, self.g.nc
        for n in range(len(self.jobs) + 1):
            if n < len(self.jobs) and self.jobs[n]["kind"] == "rope":
                pool.wait_ge(*self.turned.at(self.jobs[n]["n_pe"] + 1))
                if n >= 2:
                    pool.wait_ge(*self.r1_ready.at(n - 1))
                nc.gpsimd.tensor_tensor(g.fbuf[n % 2][:, :], g.turn[0][:, :], g.turn[1][:, :], ALU.add)\
                  .then_inc(self.rotated.sem, 1)
            if n >= 1:
                m = n - 1
                pool.wait_ge(*self.s2_ready.at(m + 1))
                nc.gpsimd.tensor_tensor(g.parts[m % NPARTS][:, 2, :], g.rbuf[m % 2][:, :], g.parts[m % NPARTS][:, 1, :],
                                        ALU.subtract).then_inc(self.s3_ready.sem, 1)

    def sync(self, sp, first_loads):
        g = self.g
        per = len(self.jobs) // self.nchunks
        for n, j in enumerate(self.jobs):
            c = n // per
            s = g.parts[n % NPARTS]
            rows = j["to"].rearrange("(r d) h t -> (d h) r t", d=DH)[:, :, c * CH:(c + 1) * CH]
            sp.wait_ge(*self.s3_ready.at(n + 1))
            first = 0
            for k in (3, 2, 1):
                part = s[:, 3 - k, :].unsqueeze(1).to_broadcast([P, k, CH]) if j["query"] else s[:, 0:k, :]
                sp.dma_start(rows[:, first:first + k, :], part)\
                  .then_inc(self.written[n % NPARTS].sem, 16)
                first += k
            if n == min(NPARTS, len(self.jobs)) - 1:
                for i in range(per):
                    sp.wait_ge(*self.written[i].at(48))
                first_loads()

    def wait_written(self, eng):
        for i in range(NPARTS):
            uses = len(self.jobs[i::NPARTS])
            if uses:
                eng.wait_ge(*self.written[i].at(48 * uses))


class Core:

    def __init__(self, g, name, nb, nqt, causal=False, bias=None, xrows=0):
        self.g, self.nb, self.nqt, self.bias, self.xrows = g, nb, nqt, bias, xrows
        self.split = causal and nqt == 2
        self.queries = [(0, nqt * P)] + ([(P, P)] if self.split else [(0, nqt * P)]) * (nqt - 1)
        self.offset = [0, nqt * P][:nqt]
        self.width = sum(n for _, n in self.queries)
        self.keys = [P, 2 * P] if self.split else [nqt * P] * nqt
        self.nfeat = 2 + (1 if xrows else 0)
        self.tail = None
        self.st_ready = g.shared_sem("core_st_ready", 8 * nb)
        self.exp_done = g.shared_sem("core_exp_done", 8 * nb)
        self.mx_ready = g.shared_sem("core_mx_ready", 8 * nqt * nb)
        self.mx_done = g.shared_sem("core_mx_done", 8 * nqt * nb)
        self.mb_ready = g.shared_sem("core_mb_ready", 2 * nb)
        self.mt_ready = g.shared_sem("core_mt_ready", 2 * nb)
        self.mts_done = g.shared_sem("core_mts_done", 2 * nb)
        self.pv_done = g.shared_sem("core_pv_done", 4 * nb)
        self.ot_done = g.shared_sem("core_ot_done", 4 * nb)
        self.va_ready = g.shared_sem("core_va_ready", nb)
        self.cxt_ready = g.shared_sem("core_cxt_ready", nqt * nb)
        self.cx_done = g.shared_sem("core_cx_done", nqt * nb)
        self.chain = g.shared_sem("core_chain", (2 + nqt) * nb)
        self.feat = [[g.shared_sem(f"core_feat{p}{h}", 16 * self.nfeat * nb // 2) for h in range(2)] for p in range(2)]
        self.m_in = [[g.shared_sem(f"core_m_in{p}{h}", 32 * nb // 2) for h in range(2)] for p in range(2)]

    def steps(self, eng, body, last):
        body(0, None)
        body(1, None)
        turns = (last - 1) // 2
        if turns:
            with eng.Fori(0, turns) as i:
                body(2, i)
                body(3, i)
        for j in range(2 + 2 * turns, self.nb + 2):
            body(j, None)

    def batches(self, j, i):
        out = []
        for lag in range(3):
            c = j - lag
            out.append(None if c < 0 or c >= self.nb else Batch(c, i))
        return out

    def bias_for(self, b, transposed):
        g = self.g
        if self.bias == "batch":
            if transposed:
                return g.mask_k[:, bass.ts(b.no, 2 * S)]
            return g.mask_q[:, bass.ts(b.no, 2 * S)]
        return self.bias[1 if transposed else 0]

    def tensor(self, pe, ready):
        g, nc = self.g, self.g.nc
        ready()
        nqt = self.nqt

        def scores(b, u):
            if u % 4 == 0:
                pe.wait_ge(*self.m_in[b.par][u // 4].at((b.use + 1) * 32))
            if b.first is None or b.first * 8 + u >= 2:
                pe.wait_ge(*self.exp_done.at(b.no * 8 + u - 1))
            for hh in range(2):
                h = 2 * u + hh
                bank = g.bank[2 * (u % 2) + hh]
                if self.bias is not None:
                    nc.tensor.matmul(bank[:, 0:self.width], g.ident_bf[:, :],
                                     self.bias_for(b, True)[:, 0:self.width], start=True, stop=False)
                for kt in range(nqt):
                    lo, n = self.queries[kt]
                    last = nc.tensor.matmul(bank[:, self.offset[kt]:self.offset[kt] + n],
                                            g.K6[b.par][:, h, kt * P:(kt + 1) * P], g.Q6[b.par][:, h, lo:lo + n],
                                            start=self.bias is None, stop=self.bias is None or kt == nqt - 1)
            last.then_inc(self.st_ready.sem, 1)

        def maxima(b, pair, qt, v):
            if pair % 4 == 0 and qt == 0:
                pe.wait_ge(*self.feat[b.par][pair // 4].at((b.use + 1) * 16 * self.nfeat))
            if b.first is None or b.first * 8 * nqt + v >= 2:
                pe.wait_ge(*self.mx_done.at(b.no * (8 * nqt) + v - 1))
            kw = self.keys[qt]
            bank = g.bank[4 + v % 2][:, 0:2 * kw].rearrange("p (a k) -> p a k", a=2)
            if self.bias is not None:
                bias = self.bias_for(b, False)[:, qt * nqt * P:qt * nqt * P + kw]
                nc.tensor.matmul(bank, g.ident_bf[:, :], bias.unsqueeze(1).to_broadcast([P, 2, kw]), start=True, stop=False)
            for a in range(2):
                h = 2 * pair + a
                last = nc.tensor.matmul(bank[:, a, :], g.Q6[b.par][0:MROW, h, qt * P:(qt + 1) * P],
                                        g.K6[b.par][0:MROW, h, 0:kw], start=self.bias is None,
                                        stop=self.bias is None or a == 1)
            last.then_inc(self.mx_ready.sem, 1)

        def turn_m(b, half):
            pe.wait_ge(*self.mb_ready.at(b.no * 2 + half + 1))
            for qt in range(nqt):
                last = nc.tensor.transpose(g.aux_bf[0:16, qt * P:(qt + 1) * P], g.MB[half][:, qt, :], g.ident_bf[:, :])
            last.then_inc(self.mt_ready.sem, 1)

        def values(b, grp, kt):
            if kt == 0:
                if grp == 0:
                    pe.wait_ge(*self.va_ready.at(b.no + 1))
                pe.wait_ge(*self.exp_done.at(b.no * 8 + 2 * grp + 2))
                if b.first is None or b.first * 4 + grp >= 1:
                    pe.wait_ge(*self.ot_done.at(b.no * 4 + grp))
            lo, n = self.queries[kt]
            for hh in range(4):
                last = nc.tensor.matmul(
                    g.bank[6][PVW * hh:PVW * hh + PVW, lo:lo + n],
                    g.VA[b.par][:, kt, 4 * grp + hh, :],
                    g.PT[grp % 2][:, hh, self.offset[kt]:self.offset[kt] + n],
                    start=kt == 0, stop=kt == nqt - 1)
            if kt == nqt - 1:
                last.then_inc(self.pv_done.sem, 1)

        def turn_context(b, qt):
            pe.wait_ge(*self.ot_done.at(b.no * 4 + 4))
            for grp in range(4):
                last = nc.tensor.transpose(g.bank[7][:, grp * P:(grp + 1) * P], g.OT[b.par][:, grp, qt * P:(qt + 1) * P],
                                           g.ident[:, :])
            last.then_inc(self.cxt_ready.sem, 1)

        def step(j, i):
            bm, be, bc = self.batches(j, i)
            for grp in range(4):
                for slot in range(2 * nqt):
                    if bm:
                        maxima(bm, 2 * grp + slot // nqt, slot % nqt, grp * 2 * nqt + slot)
                    if be and slot % nqt == 0:
                        scores(be, 2 * grp + slot // nqt)
                    if slot % 2 == 1:
                        if be and grp >= 1:
                            values(be, grp - 1, slot // 2)
                        if bc and grp == 0:
                            values(bc, 3, slot // 2)
                    if slot == nqt:
                        if be and grp == 0:
                            if bc:
                                pe.wait_ge(*self.cx_done.at(bc.no * nqt))
                            pe.wait_ge(*self.mts_done.at(be.no * 2 + 1))
                            turn_m(be, 1)
                        if bm and grp == 2:
                            if bc:
                                pe.wait_ge(*self.cx_done.at(bc.no * nqt + 1))
                            if be:
                                pe.wait_ge(*self.mts_done.at(be.no * 2 + 2))
                            turn_m(bm, 0)
                if bc and grp % 2 == 1 and grp // 2 < nqt:
                    pe.wait_ge(*self.cx_done.at(bc.no * nqt + grp // 2))
                    if grp == 1 and be:
                        pe.wait_ge(*self.mts_done.at(be.no * 2 + 2))
                    if grp == 3 and bm:
                        pe.wait_ge(*self.mts_done.at(bm.no * 2 + 1))
                    turn_context(bc, grp // 2)
                if self.tail and i is None:
                    self.tail.run("tensor", pe, (j, grp))

        self.steps(pe, step, self.nb - 1)

    def scalar(self, act):
        g, nc = self.g, self.g.nc

        def evacuate(b, grp):
            act.wait_ge(*self.pv_done.at(b.no * 4 + grp + 1))
            if grp == 0 and (b.first is None or b.first >= 2):
                act.wait_ge(*self.cxt_ready.at((b.no - 1) * self.nqt))
            w = self.nqt * P
            nc.scalar.copy(g.OT[b.par][:, grp, 0:w], g.bank[6][:, 0:w])\
              .then_inc(self.ot_done.sem, 1)

        def m_rows(b, half):
            act.wait_ge(*self.mt_ready.at(b.no * 2 + half + 1))
            if b.first is None or b.first >= 1:
                act.wait_ge(*self.m_in[1 - b.par][half].at((b.use + b.par) * 32))
            w = self.nqt * P
            nc.scalar.copy(g.MT[half][:, 0:w], g.aux_bf[0:16, 0:w]).then_inc(self.mts_done.sem, 1)

        def step(j, i):
            bm, be, bc = self.batches(j, i)
            for grp in range(4):
                if bc and grp < 2:
                    evacuate(bc, 2 + grp)
                if be and grp >= 2:
                    evacuate(be, grp - 2)
                if be:
                    for u in (2 * grp, 2 * grp + 1):
                        act.wait_ge(*self.st_ready.at(be.no * 8 + u + 1))
                        if u % 2 == 0 and (be.first is None or be.first * 4 + grp >= 2):
                            act.wait_ge(*self.pv_done.at(be.no * 4 + grp - 1))
                        nc.scalar.activation(g.PT[grp % 2][:, 2 * (u % 2):2 * (u % 2) + 2, 0:self.width],
                                             g.bank2[u % 2][:, :, 0:self.width], ACT.Exp, scale=SCALE)\
                          .then_inc(self.exp_done.sem, 1)
                if be and grp == 0:
                    m_rows(be, 1)
                if bm and grp == 2:
                    m_rows(bm, 0)
                if self.tail and i is None:
                    self.tail.run("scalar", act, (j, grp))

        self.steps(act, step, self.nb - 1)

    def vector(self, dve):
        g, nc = self.g, self.g.nc
        nqt = self.nqt
        t = Tally(dve, self.chain)

        def parts_of_m(b, half):
            dve.wait_ge(*self.mx_done.at(b.no * 8 * nqt + (half + 1) * 4 * nqt))
            m = g.MS[:, 0:nqt, 8 * half:8 * half + 8]
            hi, lo = g.MB[half][:, 0:nqt, 0:8], g.MB[half][:, 0:nqt, 8:16]
            if b.first is None or b.first >= 1:
                dve.wait_ge(*self.mt_ready.at(b.no * 2 + half - 1))
            t.done(nc.vector.tensor_scalar(hi, m, -1.0, None, ALU.mult))
            nc.vector.scalar_tensor_tensor(lo, m, -1.0, hi, ALU.mult, ALU.subtract).then_inc(self.mb_ready.sem, 1)

        def context(b, qt):
            dve.wait_ge(*self.cxt_ready.at(b.no * nqt + qt + 1))
            sums = g.bank[7][:, :].rearrange("p (h w) -> p h w", w=PVW)
            t.done(nc.vector.reciprocal(g.rsum[:, :], sums[:, :, DH]))
            nc.vector.tensor_tensor(g.CX[:, bass.ds(b.no * nqt + qt, 1), :].rearrange("p o (d h) -> p (o h) d", d=DH),
                                    sums[:, :, 0:DH],
                                    g.rsum[:, :].unsqueeze(2).to_broadcast([P, H, DH]), ALU.mult)\
              .then_inc(self.cx_done.sem, 1)

        def step(j, i):
            bm, be, bc = self.batches(j, i)
            for grp in range(4):
                if bm:
                    for k in range(2 * nqt):
                        pair, qt, v = 2 * grp + k // nqt, k % nqt, grp * 2 * nqt + k
                        kw = self.keys[qt]
                        dve.wait_ge(*self.mx_ready.at(bm.no * (8 * nqt) + v + 1))
                        nc.vector.reduce_max(g.MS[:, qt, 2 * pair:2 * pair + 2],
                                             g.bank[4 + v % 2][:, 0:2 * kw].rearrange("p (a k) -> p a k", a=2),
                                             axis=AX_X).then_inc(self.mx_done.sem, 1)
                if bm and grp % 2 == 1:
                    parts_of_m(bm, grp // 2)
                if bc and grp % 2 == 1 and grp // 2 < nqt:
                    context(bc, grp // 2)
                if self.tail and i is None:
                    self.tail.run("vector", dve, (j, grp))

        body = self.steps
        per = 2 * (2 + nqt)

        def looped(j, i):
            if i is not None and j == 2:
                t.loop(i, per)
            step(j, i)
            if i is not None and j == 3:
                t.end((self.nb - 2) // 2)

        body(dve, looped, self.nb - 1)

    def gpsimd(self, pool, values, ready):
        g, nc = self.g, self.g.nc
        nqt = self.nqt
        ready()

        def step(j, i):
            bm, _, _ = self.batches(j, i)
            if not bm:
                return
            if bm.first is None or bm.first >= 2:
                pool.wait_ge(*self.pv_done.at(bm.no * 4 - 4))
            nc.gpsimd.tensor_copy(g.VA[bm.par][:, 0:nqt, :, 0:DH],
                                  values[:, bass.ds(bm.no * nqt, nqt), :].rearrange("p t (d h) -> p t h d", d=DH))\
              .then_inc(self.va_ready.sem, 1)

        self.steps(pool, step, self.nb - 1)

    def load(self, sp, b, half, rows, which="qkx"):
        g = self.g
        hs, w = slice(8 * half, 8 * half + 8), self.nqt * P
        to = {"q": g.Q6[b.par][0:ROWS, hs, 0:w], "k": g.K6[b.par][0:ROWS, hs, 0:w],
              "x": g.Q6[b.par][XROW:XROW + self.xrows, hs, 0:w]}
        for n, src in zip("qkx", rows):
            if n in which:
                sp.dma_start(to[n], src[:, hs, bass.ts(b.no, w)]).then_inc(self.feat[b.par][half].sem, 16)

    def first_loads(self, sp, rows, which="qkx"):
        for c in range(2):
            for half in range(2):
                self.load(sp, Batch(c), half, rows, which)

    def sync(self, sp, rows):
        g = self.g
        w = self.nqt * P

        def m_rows(b, half):
            sp.wait_ge(*self.mts_done.at(b.no * 2 + half + 1))
            for part in range(2):
                sp.dma_start(g.Q6[b.par][MROW + part:MROW + part + 1, 8 * half:8 * half + 8, 0:w],
                             g.MT[half][8 * part:8 * part + 8, 0:w]).then_inc(self.m_in[b.par][half].sem, 16)

        def step(j, i):
            bm, be, _ = self.batches(j, i)
            more = i is not None or j + 1 < self.nb
            for half in range(2):
                if be and half == 0:
                    m_rows(be, 1)
                if bm and half == 1:
                    m_rows(bm, 0)
                if more and be:
                    sp.wait_ge(*self.st_ready.at(be.no * 8 + 4 * half + 4))
                    self.load(sp, Batch(j + 1, i), half, rows)

        self.steps(sp, step, self.nb - 3)


def rsqrt(g, t, out, v, scratch, n):
    nc = g.nc
    out, v, sq = out[:, 0:n], v[:, 0:n], scratch[:, 0:n]
    t.done(nc.vector.tensor_scalar(out.bitcast(I32), v.bitcast(I32), -0.5, float(0x5F3759DF), ALU.mult, ALU.add))
    for _ in range(3):
        t.done(nc.vector.scalar_tensor_tensor(sq, out, -0.5, out, ALU.mult, ALU.mult))
        t.done(nc.vector.tensor_tensor(sq, sq, v, ALU.mult))
        t.done(nc.vector.scalar_tensor_tensor(out, sq, 1.5, out, ALU.add, ALU.mult))


def moments(g, t, tiles, rstd):
    nc = g.nc
    n = len(tiles)
    for i in range(n):
        last = nc.vector.bn_stats(g.stats[:, i, :], tiles[i])
    t.done(last)
    for i in range(n):
        last = nc.vector.bn_aggr(g.meanvar[:, i, :], g.stats[:, i, :])
    t.done(last)
    t.done(nc.vector.tensor_scalar(g.var[:, 0:n], g.meanvar[:, 0:n, 1], EPS, None, ALU.add))
    rsqrt(g, t, rstd, g.var, g.square, n)


def layernorm(g, t, y, out):
    moments(g, t, [y[:, i, :] for i in range(y.shape[1])], g.rstd)
    for i in range(y.shape[1]):
        last = g.nc.vector.tensor_scalar(out[:, i, :], y[:, i, :], g.meanvar[:, i, 0:1], g.rstd[:, i:i + 1],
                                         ALU.subtract, ALU.mult)
    return last


MOMENTS_CHAIN = 3 + 10


class Post:

    PLACES = {(0, 0): "T0 C0", (0, 1): "P0 T1 C1", (0, 2): "A0 P1 T2 C2", (0, 3): "A1 P2 M0", (1, 0): "A2",
              "after": "T3 C3 P3 A3 M1 N0 R0 Q0 N1 R1 Q1 N2 R2 Q2 N3 R3 Q3"}
    WHERE = {"tensor": "TPR", "scalar": "CNQ", "vector": "AM"}

    def __init__(self, g, name, core, w=None, bias=None):
        self.g, self.w, self.bias, self.core = g, w, bias, core
        core.tail = self
        n = NC if w is not None else 0
        self.turned = g.shared_sem("post_turned", n)
        self.ct_ready = g.shared_sem("post_ct_ready", n)
        self.projected = g.shared_sem("post_projected", n)
        self.added = g.shared_sem("post_added", NC)
        self.moments = g.shared_sem("post_moments", NC // 2)
        self.normed = g.shared_sem("post_normed", NC)
        self.xt_turned = g.shared_sem("post_xt_turned", NC)
        self.xt_ready = g.shared_sem("post_xt_ready", NC)
        self.chain = g.shared_sem("post_chain", NC // 2 * MOMENTS_CHAIN)
        self.tally = None
        self.Y = [y[:, :].rearrange("p (t d) -> p t d", t=TC) for y in (*g.turn, *g.fbuf)]

    def run(self, kind, eng, place):
        if place != "after":
            place = (place[0] - self.core.nb, place[1])
        pieces = {"T": self.turn, "C": self.copy, "P": self.project, "A": self.add,
                  "M": self.take_moments, "N": self.norm, "R": self.turn_x,
                  "Q": self.copy_x}
        for piece in self.PLACES.get(place, "").split():
            if piece[0] in self.WHERE[kind] and not (piece[0] in "TCP" and self.w is None):
                pieces[piece[0]](eng, int(piece[1]))

    def turn(self, pe, c):
        g, nc = self.g, self.g.nc
        pe.wait_ge(*self.core.cx_done.at((c + 1) * TC))
        if c == 0:
            pe.wait_ge(*self.core.mx_done.at(NT * H // 2))
        else:
            pe.wait_ge(*self.ct_ready.at(c))
        for t in range(TC):
            last = nc.tensor.transpose(g.bank[4][:, t * P:(t + 1) * P], g.CX[:, c * TC + t, :], g.ident[:, :])
        last.then_inc(self.turned.sem, 1)

    def copy(self, act, c):
        g, nc = self.g, self.g.nc
        act.wait_ge(*self.turned.at(c + 1))
        if c >= 2:
            act.wait_ge(*self.projected.at(c - 1))
        nc.scalar.copy(g.CXT[:, c % 2, :], g.bank[4][:, :]).then_inc(self.ct_ready.sem, 1)

    def project(self, pe, c):
        g, nc = self.g, self.g.nc
        pe.wait_ge(*self.ct_ready.at(c + 1))
        if c >= 1:
            pe.wait_ge(*self.added.at(c))
        if self.bias is not None:
            nc.tensor.matmul(g.bank[5][:, :].rearrange("p (t d) -> p t d", t=TC), g.ones_row[0:1, :],
                             self.bias.unsqueeze(1).to_broadcast([1, TC, D]), start=True, stop=False)
        for t in range(TC):
            last = nc.tensor.matmul(g.bank[5][:, t * P:(t + 1) * P], g.CXT[:, c % 2, t * P:(t + 1) * P], self.w,
                                    start=self.bias is None, stop=self.bias is None or t == TC - 1)
        last.then_inc(self.projected.sem, 1)

    def add(self, dve, c):
        g, nc = self.g, self.g.nc
        if self.w is not None:
            dve.wait_ge(*self.projected.at(c + 1))
            more = g.bank[5][:, :].rearrange("p (t d) -> p t d", t=TC)
        else:
            dve.wait_ge(*self.core.cx_done.at((c + 1) * TC))
            more = g.CX[:, c * TC:(c + 1) * TC, :]
        nc.vector.tensor_tensor(self.Y[c], more, g.X[:, c * TC:(c + 1) * TC, :], ALU.add).then_inc(self.added.sem, 1)

    def take_moments(self, dve, k):
        g, nc = self.g, self.g.nc
        self.tally = t = self.tally or Tally(dve, self.chain)
        dve.wait_ge(*self.added.at(2 * k + 2))
        moments(g, t, [self.Y[c][:, i, :] for c in (2 * k, 2 * k + 1) for i in range(TC)], g.scale[k])
        nc.vector.scalar_tensor_tensor(g.offset[k][:, :], g.meanvar[:, :, 0], -1.0, g.scale[k][:, :], ALU.mult, ALU.mult)\
          .then_inc(self.moments.sem, 1)

    def norm(self, act, c):
        g, nc = self.g, self.g.nc
        act.wait_ge(*self.moments.at(c // 2 + 1))
        for i in range(TC):
            n = c % 2 * TC + i
            last = nc.scalar.activation(g.X[:, c * TC + i, :], self.Y[c][:, i, :], ACT.Identity,
                                        scale=g.scale[c // 2][:, n:n + 1], bias=g.offset[c // 2][:, n:n + 1])
        last.then_inc(self.normed.sem, 1)

    def turn_x(self, pe, c):
        g, nc = self.g, self.g.nc
        pe.wait_ge(*self.normed.at(c + 1))
        if c == 0:
            pe.wait_ge(*self.core.cx_done.at(NT))
        else:
            pe.wait_ge(*self.xt_ready.at(c))
        for i in range(TC):
            last = nc.tensor.transpose(g.bank[7][:, i * P:(i + 1) * P], g.X[:, c * TC + i, :], g.ident[:, :])
        last.then_inc(self.xt_turned.sem, 1)

    def copy_x(self, act, c):
        g, nc = self.g, self.g.nc
        act.wait_ge(*self.xt_turned.at(c + 1))
        nc.scalar.copy(g.XT[:, c * CH:(c + 1) * CH], g.bank[7][:, :]).then_inc(self.xt_ready.sem, 1)




class Depths:

    NP = B // 2
    FC = [(0, P), (P, P), (2 * P, F0 - 2 * P)]

    def __init__(self, g, name):
        self.g = g
        self.scored = g.sem(f"{name}_scored")
        self.ranked = g.sem(f"{name}_ranked")
        self.gathered = g.sem(f"{name}_gathered")
        self.taken = g.sem(f"{name}_taken")
        self.hidden = g.sem(f"{name}_hidden")
        self.h_turned = g.sem(f"{name}_h_turned")
        self.h_ready = g.sem(f"{name}_h_ready")
        self.g_turned = g.sem(f"{name}_g_turned")
        self.g_ready = g.sem(f"{name}_g_ready")
        self.cx_turned = g.sem(f"{name}_cx_turned")
        self.cx_ready = g.sem(f"{name}_cx_ready")
        self.attended = g.sem(f"{name}_attended")
        self.added = g.sem(f"{name}_added")
        self.h2 = g.sem(f"{name}_h2")
        self.h2_turned = g.sem(f"{name}_h2_turned")
        self.h2_ready = g.sem(f"{name}_h2_ready")
        self.gate_up = g.sem(f"{name}_gate_up")
        self.tanh = g.sem(f"{name}_tanh")
        self.mixed = g.sem(f"{name}_mixed")
        self.down = g.sem(f"{name}_down")
        self.delta = g.sem(f"{name}_delta")
        self.scattered = g.sem(f"{name}_scattered")
        self.summed = g.sem(f"{name}_summed")
        self.normed = g.sem(f"{name}_normed")
        self.xt_turned = g.sem(f"{name}_xt_turned")
        self.xt_ready = g.sem(f"{name}_xt_ready")
        self.chain = g.sem(f"{name}_chain")
        self.g_free = g.sem(f"{name}_g_free")
        sb = g.sb
        self.scol = sb("scol", [P, NT])
        self.above = sb("above", [P, NT])
        self.ties = sb("ties", [P, NT])
        self.rank = sb("rank", [P, NT])
        self.junk = g.fbuf[0]
        free = [buf[:, :, :].rearrange("p a b -> p (a b)") for buf in g.PT]
        self.G = free[0][:, 0:2 * B * SEL].rearrange("p (k b r) -> p k b r", k=2, b=B)
        self.GT = sb("GT", [P, self.NP, 2, P])
        self.XS = sb("XS", [P, self.NP, D])
        self.X1 = sb("X1", [P, self.NP, D])
        self.XA = sb("XA", [P, self.NP, D])
        self.HN = sb("HN", [P, self.NP, D])
        self.HT = sb("HT", [P, CH])
        self.U = g.PT[0][:, 0:3, :]
        self.TH = g.PT[1][:, 0:3, :]
        self.ss = sb("ss", [P, self.NP])


    def select_tensor(self, pe, ready):
        g, nc = self.g, self.g.nc
        for c in range(NC):
            ready(c)
            nc.tensor.matmul(g.bank[c][:, :], g.router[:, :], g.XT[:, c * CH:(c + 1) * CH], start=True, stop=True)\
              .then_inc(self.scored.sem, 1)
        pe.wait_ge(*self.ranked.at(1))
        for p in range(self.NP):
            for half in range(2):
                b = 2 * p + half
                for k in range(2):
                    last = nc.tensor.matmul(g.bank[4][SEL * half:SEL * half + SEL, p * D:(p + 1) * D],
                                            self.G[:, k, b, :], g.X[:, 2 * b + k, :], start=k == 0, stop=k == 1)
        last.then_inc(self.gathered.sem, 1)
        for p in range(self.NP):
            for k in range(2):
                n = 2 * p + k
                last = nc.tensor.transpose(g.bank[n // 4][:, (n % 4) * P:(n % 4 + 1) * P],
                                           self.G[:, k, 2 * p:2 * p + 2, :].rearrange("p b r -> p (b r)"), g.ident[:, :])
        last.then_inc(self.g_turned.sem, 1)
        pe.wait_ge(*self.hidden.at(1))
        for p in range(self.NP):
            last = nc.tensor.transpose(g.bank[5][:, p * P:(p + 1) * P], self.HN[:, p, :], g.ident[:, :])
        last.then_inc(self.h_turned.sem, 1)

    def select_scalar(self, act):
        g, nc = self.g, self.g.nc
        act.wait_ge(*self.gathered.at(1))
        nc.scalar.copy(self.XS[:, :, :], g.bank[4][:, :].rearrange("p (n d) -> p n d", d=D)).then_inc(self.taken.sem, 1)
        act.wait_ge(*self.g_turned.at(1))
        for n in range(2):
            last = nc.scalar.copy(self.GT[:, 2 * n:2 * n + 2, :, :],
                                  g.bank[n][:, :].rearrange("p (a k t) -> p a k t", a=2, k=2))
        last.then_inc(self.g_ready.sem, 1)
        act.wait_ge(*self.h_turned.at(1))
        nc.scalar.mul(self.HT[:, :], g.bank[5][:, :], g.col("f0_g1")).then_inc(self.h_ready.sem, 1)

    def rms(self, t, x, out):
        g, nc = self.g, self.g.nc
        for p in range(self.NP):
            last = nc.vector.scalar_tensor_tensor(self.junk2[:, p, :], x[:, p, :], 1.0, x[:, p, :], ALU.mult, ALU.mult,
                                                  accum_out=self.ss[:, p:p + 1])
        t.done(last)
        t.done(nc.vector.tensor_scalar(g.var[:, 0:self.NP], self.ss[:, :], 1.0 / D, 1e-6, ALU.mult, ALU.add))
        rsqrt(g, t, g.rstd, g.var, g.square, self.NP)
        for p in range(self.NP):
            last = nc.vector.tensor_scalar(out[:, p, :], x[:, p, :], g.rstd[:, p:p + 1], None, ALU.mult)
        return last

    def select_vector(self, dve):
        g, nc = self.g, self.g.nc
        t = self.t = Tally(dve, self.chain)
        self.junk2 = g.Y
        for c in range(NC):
            dve.wait_ge(*self.scored.at(c + 1))
            for n in range(c * TC, (c + 1) * TC):
                b, k = n // 2, n % 2
                row = g.bank[c][:, (b % 2) * S:(b % 2) * S + S]
                t.done(nc.vector.scalar_tensor_tensor(self.junk[:, 0:P], row[:, k * P:(k + 1) * P], 1.0, g.ident[:, :],
                                                      ALU.mult, ALU.mult, accum_out=self.scol[:, n:n + 1]))
                nc.vector.tensor_scalar(self.junk[:, 0:S], row, self.scol[:, n:n + 1], None, ALU.is_gt, ALU.add,
                                        accum_out=self.above[:, n:n + 1]).then_inc(self.g_free.sem, 1)
                dve.wait_ge(*self.g_free.at(n + 1))
                t.done(nc.vector.scalar_tensor_tensor(self.junk[:, 0:S], row, self.scol[:, n:n + 1],
                                                      g.earlier[:, k, :], ALU.is_equal, ALU.mult,
                                                      accum_out=self.ties[:, n:n + 1]))
        t.done(nc.vector.tensor_tensor(self.rank[:, :], self.above[:, :], self.ties[:, :], ALU.add))
        rank = self.rank[:, :].rearrange("p (b k) -> p k b", k=2).unsqueeze(3)
        for k in range(2):
            last = nc.vector.tensor_tensor(self.G[:, k, :, :], g.iota[:, 0:SEL].unsqueeze(1).to_broadcast([P, B, SEL]),
                                           rank[:, k, :, :].to_broadcast([P, B, SEL]), ALU.is_equal)
        last.then_inc(self.ranked.sem, 1)
        dve.wait_ge(*self.taken.at(1))
        self.rms(t, self.XS, self.HN).then_inc(self.hidden.sem, 1)


    def feed_tensor(self, pe, ready):
        g, nc = self.g, self.g.nc
        ready()
        for p in range(self.NP):
            last = nc.tensor.transpose(g.bank[5][:, p * P:(p + 1) * P], g.CX[:, p, :], g.ident[:, :])
        last.then_inc(self.cx_turned.sem, 1)
        pe.wait_ge(*self.cx_ready.at(1))
        for p in range(self.NP):
            last = nc.tensor.matmul(g.bank[6][:, p * P:(p + 1) * P], g.CXT[:, 0, p * P:(p + 1) * P], g.w("f0_o"),
                                    start=True, stop=True)
        last.then_inc(self.attended.sem, 1)
        pe.wait_ge(*self.h2.at(1))
        for p in range(self.NP):
            last = nc.tensor.transpose(g.bank[7][:, p * P:(p + 1) * P], self.HN[:, p, :], g.ident[:, :])
        last.then_inc(self.h2_turned.sem, 1)
        pe.wait_ge(*self.h2_ready.at(1))
        for n, (lo, w) in enumerate(self.FC):
            for m in range(2):
                last = nc.tensor.matmul(g.bank[2 * n + m][0:w, :], g.f0_w12[:, m, lo:lo + w], self.HT[:, :],
                                        start=True, stop=True)
            last.then_inc(self.gate_up.sem, 1)
        pe.wait_ge(*self.mixed.at(3))
        for p in range(self.NP):
            for n, (lo, w) in enumerate(self.FC):
                last = nc.tensor.matmul(g.bank[6][:, p * P:(p + 1) * P], self.U[0:w, n, p * P:(p + 1) * P],
                                        g.f0_w3[0:w, n, :], start=n == 0, stop=n == 2)
        last.then_inc(self.down.sem, 1)
        pe.wait_ge(*self.delta.at(1))

        def scatter(c):
            if c >= 2:
                pe.wait_ge(*self.summed.at(c - 1))
            for half in range(2):
                rows = slice(SEL * half, SEL * half + SEL)
                for k in range(2):
                    last = nc.tensor.matmul(g.bank[2 * (c % 2) + half][:, k * P:(k + 1) * P], self.GT[rows, c, k, :],
                                            self.X1[rows, c, :], start=True, stop=True)
            last.then_inc(self.scattered.sem, 1)

        scatter(0)
        scatter(1)
        for c in range(NC):
            pe.wait_ge(*self.normed.at(c + 1))
            if c >= 1:
                pe.wait_ge(*self.xt_ready.at(c))
            for i in range(TC):
                last = nc.tensor.transpose(g.bank[7][:, i * P:(i + 1) * P], g.X[:, c * TC + i, :], g.ident[:, :])
            last.then_inc(self.xt_turned.sem, 1)
            if c + 2 < NC:
                scatter(c + 2)

    def feed_scalar(self, act):
        g, nc = self.g, self.g.nc
        act.wait_ge(*self.cx_turned.at(1))
        nc.scalar.copy(g.CXT[:, 0, :], g.bank[5][:, :]).then_inc(self.cx_ready.sem, 1)
        act.wait_ge(*self.h2_turned.at(1))
        nc.scalar.mul(self.HT[:, :], g.bank[7][:, :], g.col("f0_g2")).then_inc(self.h2_ready.sem, 1)
        for n, (lo, w) in enumerate(self.FC):
            act.wait_ge(*self.gate_up.at(n + 1))
            nc.scalar.activation(self.TH[0:w, n, :], g.bank[2 * n][0:w, :], ACT.Tanh, scale=0.5).then_inc(self.tanh.sem, 1)
        for c in range(NC):
            act.wait_ge(*self.xt_turned.at(c + 1))
            nc.scalar.copy(g.XT[:, c * CH:(c + 1) * CH], g.bank[7][:, :]).then_inc(self.xt_ready.sem, 1)

    def feed_vector(self, dve):
        g, nc = self.g, self.g.nc
        t = self.t
        tiles = lambda bank: bank[:, :].rearrange("p (n d) -> p n d", d=D)
        dve.wait_ge(*self.attended.at(1))
        t.done(nc.vector.tensor_copy(self.XA[:, :, :], tiles(g.bank[6])))
        t.done(nc.vector.tensor_tensor(self.X1[:, :, :], self.XA[:, :, :], self.XS[:, :, :], ALU.add))
        self.rms(t, self.X1, self.HN).then_inc(self.h2.sem, 1)
        for n, (lo, w) in enumerate(self.FC):
            dve.wait_ge(*self.tanh.at(n + 1))
            t.done(nc.vector.scalar_tensor_tensor(self.TH[0:w, n, :], self.TH[0:w, n, :], 1.0, g.bank[2 * n][0:w, :],
                                                  ALU.add, ALU.mult))
            nc.vector.scalar_tensor_tensor(self.U[0:w, n, :], self.TH[0:w, n, :], 0.5, g.bank[2 * n + 1][0:w, :],
                                           ALU.mult, ALU.mult).then_inc(self.mixed.sem, 1)
        dve.wait_ge(*self.down.at(1))
        nc.vector.tensor_tensor(self.X1[:, :, :], tiles(g.bank[6]), self.XA[:, :, :], ALU.add).then_inc(self.delta.sem, 1)
        for c in range(NC):
            dve.wait_ge(*self.scattered.at(c + 1))
            if c >= 1:
                dve.wait_ge(*self.normed.at(c))
            x = g.X[:, c * TC:(c + 1) * TC, :]
            for half in range(2):
                two = slice(2 * half, 2 * half + 2)
                last = nc.vector.scalar_tensor_tensor(g.Y[:, two, :], x[:, two, :], 2.0,
                                                      tiles(g.bank[2 * (c % 2) + half])[:, 0:2, :], ALU.mult, ALU.add)
            last.then_inc(self.summed.sem, 1)
            dve.wait_ge(*self.summed.at(c + 1))
            layernorm(g, t, g.Y[:, :, :], x).then_inc(self.normed.sem, 1)


class Gauss:

    def __init__(self, g, name):
        self.g = g
        self.summed = g.sem(f"{name}_summed")
        self.global_ = g.sem(f"{name}_global_")
        self.bias = g.sem(f"{name}_bias")
        self.c_in = g.sem(f"{name}_c_in")
        self.c_ready = g.sem(f"{name}_c_ready")
        self.pz = g.sem(f"{name}_pz")
        self.acted = g.sem(f"{name}_acted")
        self.rows_ready = g.sem(f"{name}_rows_ready")
        self.turned = g.sem(f"{name}_turned")
        self.copied = g.sem(f"{name}_copied")
        self.written = g.sem(f"{name}_written")
        self.chain = g.sem(f"{name}_chain")
        self.g1 = g.sem(f"{name}_g1")
        sb = g.sb
        self.glo = sb("glo", [P, B])
        self.cbias = sb("cbias", [P, B])
        self.MQ = g.CX[:, :, :].rearrange("p n d -> p (n d)")
        self.C = g.CXT
        free = g.PT[1][:, :, :].rearrange("p a b -> p (a b)")
        n = NT * H
        tiles = lambda ap: ap.rearrange("p (n h) -> p n h", h=H)
        self.ez, self.tp = tiles(free[:, 0:n]), tiles(free[:, n:2 * n])
        self.AB = free[:, 2 * n:4 * n].rearrange("p (a n h) -> p a n h", a=2, h=H)
        self.rem = free[:, 4 * n:6 * n].rearrange("p (a n h) -> p a n h", a=2, h=H)
        self.XR = g.PT[0][:, :, :].rearrange("p a b -> p (a b)").bitcast(BF16)[:, 0:6 * n]\
                   .rearrange("p (n r h) -> p n r h", n=NT, h=H)
        self.AR = g.OT[0][:, :, :].rearrange("p a b -> p (a b)").bitcast(BF16)[0:6 * H, :]

    def tensor(self, pe):
        g, nc = self.g, self.g.nc
        pe.wait_ge(*self.summed.at(1))
        nc.tensor.matmul(g.bank[5][:, 0:B], g.w("a1_fg"), self.glo[:, :], start=True, stop=True).then_inc(self.global_.sem, 1)
        for c in range(NC):
            if c >= 1:
                pe.wait_ge(*self.c_ready.at(c))
            nc.tensor.matmul(g.bank[6][:, :], g.w("a1_fq"), self.MQ[:, c * CH:(c + 1) * CH], start=True, stop=True)\
              .then_inc(self.c_in.sem, 1)
            pe.wait_ge(*self.c_ready.at(c + 1))
            for t in range(TC):
                n = c * TC + t
                last = nc.tensor.matmul(g.bank[7][:, n * 2 * H:(n + 1) * 2 * H], self.C[:, c % 2, t * P:(t + 1) * P],
                                        g.upz[:, :], start=True, stop=True)
            last.then_inc(self.pz.sem, 1)
        pe.wait_ge(*self.rows_ready.at(2))
        for n in range(NT):
            bank = g.bank[5 + n // 8].bitcast(BF16)
            last = nc.tensor.transpose(bank[0:6 * H, (n % 8) * P:(n % 8 + 1) * P],
                                       self.XR[:, n, :, :].rearrange("p r h -> p (r h)"), g.ident_bf[:, :])
            if n % 8 == 7:
                last.then_inc(self.turned.sem, 1)

    def scalar(self, act):
        g, nc = self.g, self.g.nc
        for c in range(NC):
            act.wait_ge(*self.c_in.at(c + 1))
            act.wait_ge(*self.bias.at(1))
            if c >= 2:
                act.wait_ge(*self.pz.at(c - 1))
            for k in range(2):
                b = 2 * c + k
                last = nc.scalar.activation(self.C[:, c % 2, k * S:(k + 1) * S], g.bank[6][:, k * S:(k + 1) * S], ACT.Tanh,
                                            bias=self.cbias[:, b:b + 1])
            last.then_inc(self.c_ready.sem, 1)
        act.wait_ge(*self.pz.at(NC))
        pz = g.bank[7][:, :].rearrange("p (n a h) -> p n a h", a=2, h=H)
        nc.scalar.activation(self.tp[:, :, :], pz[:, :, 0, :], ACT.Tanh, scale=0.5)
        nc.scalar.activation(self.ez[:, :, :], pz[:, :, 1, :], ACT.Exp, scale=-1.0).then_inc(self.acted.sem, 1)
        for n in range(2):
            act.wait_ge(*self.turned.at(n + 1))
            nc.scalar.copy(self.AR[:, n * 8 * P:(n + 1) * 8 * P], g.bank[5 + n].bitcast(BF16)[0:6 * H, :])\
              .then_inc(self.copied.sem, 1)

    def vector(self, dve, kept):
        g, nc = self.g, self.g.nc
        t = Tally(dve, self.chain)
        dve.wait_ge(*kept.at(NC))
        nc.vector.reduce_sum(self.glo[:, :], self.MQ[:, :].rearrange("p (b s) -> p b s", s=S), axis=AX_X)\
          .then_inc(self.summed.sem, 1)
        dve.wait_ge(*self.global_.at(1))
        t.done(nc.vector.tensor_scalar(self.cbias[:, :], g.bank[5][:, 0:B], 1.0 / S, g.col("a1_bfq"), ALU.mult, ALU.add))
        nc.vector.tensor_scalar(self.cbias[:, :], self.cbias[:, :], g.col("a1_bfg"), None, ALU.add).then_inc(self.bias.sem, 1)
        dve.wait_ge(*self.acted.at(1))
        ab, a, b = self.AB, self.AB[:, 0, :, :], self.AB[:, 1, :, :]
        t.done(nc.vector.tensor_scalar(self.ez[:, :, :], self.ez[:, :, :], 1.0, None, ALU.add))
        t.done(nc.vector.scalar_tensor_tensor(a, self.ez[:, :, :], -2.0 / (S * S * SCALE), self.ez[:, :, :],
                                              ALU.mult, ALU.mult))
        t.done(nc.vector.scalar_tensor_tensor(b, a, -float(S), self.tp[:, :, :], ALU.mult, ALU.mult))
        for part in range(3):
            src = ab if part == 0 else self.rem
            for m in range(2):
                last = nc.vector.tensor_copy(self.XR[:, :, 3 * m + part, :], src[:, m, :, :])
            if part == 2:
                last.then_inc(self.rows_ready.sem, 2)
                break
            t.done(last)
            for m in range(2):
                last = nc.vector.tensor_tensor(self.rem[:, m, :, :], src[:, m, :, :], self.XR[:, :, 3 * m + part, :],
                                               ALU.subtract)
            t.done(last)

    def sync(self, sp, rows):
        sp.wait_ge(*self.copied.at(2))
        for first, part in ((0, 0), (3, 0), (6, 1)):
            sp.dma_start(rows[first:first + 3, :, :].rearrange("r h t -> (r h) t"),
                         self.AR[3 * H * part:3 * H * part + 3 * H, :]).then_inc(self.written.sem, 16)


class Mask:

    def __init__(self, g):
        self.g = g
        self.loaded, self.made, self.turned, self.copied = (g.sem(f"mask_{w}") for w in ("loaded", "made", "turned", "copied"))

    def sync(self, sp):
        g = self.g
        for i in range(2):
            sp.dma_start(g.PT[i][:, :, :].rearrange("p a b -> p (a b)").bitcast(I32).rearrange("p (n k) -> p n k", k=S),
                         g.io["mask"].rearrange("(n p) k -> p n k", p=P)[:, 8 * i:8 * i + 8, :]).then_inc(self.loaded.sem, 16)

    def vector(self, dve):
        g, nc = self.g, self.g.nc
        dve.wait_ge(*self.loaded.at(32))
        for i in range(2):
            nc.vector.tensor_scalar(g.mask_q[:, i * 8 * S:(i + 1) * 8 * S],
                                    g.PT[i][:, :, :].rearrange("p a b -> p (a b)").bitcast(I32), 0.0, NEG_MASK,
                                    ALU.is_equal, ALU.mult).then_inc(self.made.sem, 1)

    def tensor(self, pe):
        g, nc = self.g, self.g.nc
        for i in range(4):
            pe.wait_ge(*self.made.at(i // 2 + 1))
            bank = g.bank[4 + i].bitcast(BF16)
            for n in range(8):
                b, kt, qt = 2 * i + n // 4, n // 2 % 2, n % 2
                last = nc.tensor.transpose(bank[:, n * P:(n + 1) * P],
                                           g.mask_q[:, b * 2 * S + qt * S + kt * P:b * 2 * S + qt * S + kt * P + P],
                                           g.ident_bf[:, :])
            last.then_inc(self.turned.sem, 1)

    def scalar(self, act):
        g, nc = self.g, self.g.nc
        for i in range(4):
            act.wait_ge(*self.turned.at(i + 1))
            nc.scalar.copy(g.mask_k[:, i * 4 * S:(i + 1) * 4 * S], g.bank[4 + i].bitcast(BF16)).then_inc(self.copied.sem, 1)


class Router:

    def __init__(self, g):
        self.g = g
        self.logits = g.sem(f"router_logits")
        self.chain = g.sem(f"router_chain")
        self.gap = g.sem(f"router_gap")
        self.gap_exp = g.sem(f"router_gap_exp")
        self.routed = g.sem(f"router_routed")
        sb = g.sb
        self.L = sb("router_L", [P, NT, EX])
        self.W1 = sb("router_W1", [P, NT, EX])
        self.W2 = sb("router_W2", [P, NT, EX])
        self.first = sb("router_first", [P, NT, EX])
        self.second = sb("router_second", [P, NT, EX])
        self.m1, self.m2, self.d = (sb(f"router_{n}", [P, NT]) for n in ("m1", "m2", "d"))
        self.gate = sb("router_gate", [P, 2, NT])

    def tensor(self, pe, ready):
        g, nc = self.g, self.g.nc
        bank = g.bank[0][:, 0:NT * EX].rearrange("p (n e) -> p n e", e=EX)
        for n in range(NT):
            if n % TC == 0:
                ready(n // TC)
            last = nc.tensor.matmul(bank[:, n, :], g.XT[:, n * P:(n + 1) * P], g.router_w[:, :], start=True, stop=True)
        last.then_inc(self.logits.sem, 1)

    def scalar(self, act):
        g, nc = self.g, self.g.nc
        act.wait_ge(*self.gap.at(1))
        nc.scalar.activation(self.d[:, :], self.d[:, :], ACT.Exp).then_inc(self.gap_exp.sem, 1)

    def vector(self, dve):
        g, nc = self.g, self.g.nc
        t = Tally(dve, self.chain)
        wide = lambda ap: ap.unsqueeze(2).to_broadcast([P, NT, EX])
        rows = lambda ap: ap.unsqueeze(1).to_broadcast([P, NT, EX])
        L, W1, W2 = self.L[:, :, :], self.W1[:, :, :], self.W2[:, :, :]
        dve.wait_ge(*self.logits.at(1))
        bank = g.bank[0][:, 0:NT * EX].rearrange("p (n e) -> p n e", e=EX)
        t.done(nc.vector.tensor_tensor(L, bank, rows(g.router_b[:, :]), ALU.add))
        for m, out in ((self.m1, self.first), (self.m2, self.second)):
            t.done(nc.vector.reduce_max(m[:, :], L, axis=AX_X))
            t.done(nc.vector.tensor_tensor(W1, L, wide(m[:, :]), ALU.is_equal))
            t.done(nc.vector.tensor_tensor(W1, W1, rows(g.descending[:, :]), ALU.mult))
            t.done(nc.vector.reduce_max(self.d[:, :], W1, axis=AX_X))
            t.done(nc.vector.tensor_tensor(out[:, :, :], W1, wide(self.d[:, :]), ALU.is_equal))
            if m is self.m1:
                t.done(nc.vector.tensor_scalar(W2, self.first[:, :, :], -1e30, None, ALU.mult))
                t.done(nc.vector.tensor_tensor(L, L, W2, ALU.add))
        nc.vector.tensor_tensor(self.d[:, :], self.m2[:, :], self.m1[:, :], ALU.subtract).then_inc(self.gap.sem, 1)
        dve.wait_ge(*self.gap_exp.at(1))
        t.done(nc.vector.tensor_scalar(self.m1[:, :], self.d[:, :], 1.0, None, ALU.add))
        t.done(nc.vector.reciprocal(self.gate[:, 0, :], self.m1[:, :]))
        nc.vector.tensor_tensor(self.gate[:, 1, :], self.d[:, :], self.gate[:, 0, :], ALU.mult)\
          .then_inc(self.routed.sem, 1)


class Experts:

    BLOCKS = 2 * T // P + EX
    FT = FE // P

    def __init__(self, g, router, xs, ys):
        self.g, self.router, self.xs, self.ys = g, router, xs, ys
        self.chosen = g.sem("experts_chosen")
        self.counted = g.sem("experts_counted")
        self.chain = g.sem("experts_chain")
        self.positions = g.sem("experts_positions")
        self.table = g.sem("experts_table")
        self.filled = g.sem("experts_filled")
        self.scattered = g.sem("experts_scattered")
        self.weights_in = g.sem("experts_weights_in")
        self.x_in = [g.sem(f"experts_x_in{i}") for i in range(2)]
        self.turned = g.sem("experts_turned")
        self.xt_ready = g.sem("experts_xt_ready")
        self.gate = g.sem("experts_gate")
        self.up = g.sem("experts_up")
        self.tanh = g.sem("experts_tanh")
        self.halved = g.sem("experts_halved")
        self.mixed = g.sem("experts_mixed")
        self.h_turned = g.sem("experts_h_turned")
        self.ht_ready = g.sem("experts_ht_ready")
        self.down = g.sem("experts_down")
        self.y_ready = g.sem("experts_y_ready")
        self.y_out = [g.sem(f"experts_y_out{i}") for i in range(2)]
        self.gathered = [g.sem(f"experts_gathered{c}") for c in range(NC)]
        self.normed = g.sem("experts_normed")
        self.stored = g.sem("experts_stored")
        sb = g.sb
        self.both = sb("experts_both", [P, NT, EX], BF16)
        self.place = sb("experts_place", [P, NT, EX])
        self.pos = sb("experts_pos", [P, 2, NT])
        self.row = sb("experts_row", [P, 2, NT], U32)
        self.full = sb("experts_full", [P, EX, T // P])
        self.nblocks = sb("experts_nblocks", [P, EX])
        self.before = sb("experts_before", [P, EX, EX])
        self.until = sb("experts_until", [P, EX])
        self.shift = sb("experts_shift", [P, EX])
        self.passed = sb("experts_passed", [1, self.BLOCKS, EX])
        self.lookup = sb("experts_lookup", [1, self.BLOCKS])
        self.lookup_int = sb("experts_lookup_int", [1, self.BLOCKS], I32)
        self.w12 = g.BIG[:, 0:2 * EX * FE].rearrange("p (a e f) -> p a e f", a=2, e=EX)
        self.w3 = g.BIG[:, 2 * EX * FE:3 * EX * FE].rearrange("p (e n d) -> p e n d", e=EX, n=self.FT)
        self.xb = [g.OT[0][:, i, 0:D] for i in range(2)]
        self.xt = [g.OT[1][:, i, 0:P] for i in range(2)]
        self.hid = g.rbuf
        self.ht = [g.CXT[:, i, :].rearrange("p (n t) -> p n t", n=self.FT) for i in range(2)]
        self.yb = [g.Y[:, i, :] for i in range(2)]


    FILLS = 5

    def fill(self, eng, pieces):
        g = self.g
        tiles = self.BLOCKS // self.FILLS
        for n in pieces:
            eng.dma_start(self.xs[n * tiles * P:(n + 1) * tiles * P, :].rearrange("(p t) d -> p t d", p=P),
                          g.CTX[:, 0:tiles, :]).then_inc(self.filled.sem, 16)

    def place_tensor(self, pe):
        g, nc = self.g, self.g.nc
        both = self.both
        pe.wait_ge(*self.chosen.at(1))
        bank = g.bank[1][:, 0:NT * EX].rearrange("p (n e) -> p n e", e=EX)
        nc.tensor.matmul(bank, g.upper_bf[:, :], both[:, :, :], start=True, stop=False)
        for n in range(NT - 1):
            nc.tensor.matmul(bank[:, n + 1:NT, :], g.ones_bf[:, :],
                             both[:, n:n + 1, :].to_broadcast([P, NT - 1 - n, EX]), start=False, stop=n == NT - 2)
        for n in range(NT):
            last = nc.tensor.matmul(g.bank[2][:, 0:EX], g.ones_bf[:, :], both[:, n, :], start=n == 0, stop=n == NT - 1)
        last.then_inc(self.counted.sem, 1)

    def place_vector(self, dve):
        g, nc, r = self.g, self.g.nc, self.router
        t = self.t = Tally(dve, self.chain)
        chosen = (r.first, r.second)
        dve.wait_ge(*r.routed.at(1))
        nc.vector.tensor_tensor(self.both[:, :, :], r.first[:, :, :], r.second[:, :, :], ALU.add)\
          .then_inc(self.chosen.sem, 1)
        dve.wait_ge(*self.counted.at(1))
        bank = g.bank[1][:, 0:NT * EX].rearrange("p (n e) -> p n e", e=EX)
        n_full = T // P
        t.done(nc.vector.tensor_tensor(self.full[:, :, :], g.bank[2][:, 0:EX].unsqueeze(2).to_broadcast([P, EX, n_full]),
                                       g.multiples[:, :].unsqueeze(1).to_broadcast([P, EX, n_full]), ALU.is_gt))
        t.done(nc.vector.reduce_sum(self.nblocks[:, :], self.full[:, :, :], axis=AX_X))
        t.done(nc.vector.tensor_tensor(self.before[:, :, :], self.nblocks[:, :].unsqueeze(1).to_broadcast([P, EX, EX]),
                                       g.up_to[:, :, :], ALU.mult))
        t.done(nc.vector.reduce_sum(self.until[:, :], self.before[:, :, :], axis=AX_X))
        t.done(nc.vector.tensor_tensor(self.shift[:, :], self.until[:, :], self.nblocks[:, :], ALU.subtract))
        t.done(nc.vector.tensor_scalar(self.shift[:, :], self.shift[:, :], float(P), None, ALU.mult))
        t.done(nc.vector.tensor_tensor(self.place[:, :, :], bank, self.shift[:, :].unsqueeze(1).to_broadcast([P, NT, EX]),
                                       ALU.add))
        for k, work in enumerate((r.W1, r.W2)):
            last = nc.vector.tensor_tensor(work[:, :, :], self.place[:, :, :], chosen[k][:, :, :], ALU.mult)
        t.done(last)
        for k, work in enumerate((r.W1, r.W2)):
            last = nc.vector.reduce_sum(self.pos[:, k, :], work[:, :, :], axis=AX_X)
        t.done(last)
        nc.vector.tensor_copy(self.row[:, :, :], self.pos[:, :, :]).then_inc(self.positions.sem, 1)
        t.done(nc.vector.tensor_tensor(self.passed[:, :, :], self.until[0:1, :].unsqueeze(1).to_broadcast([1, self.BLOCKS, EX]),
                                       g.iota[0:1, 0:self.BLOCKS].unsqueeze(2).to_broadcast([1, self.BLOCKS, EX]), ALU.is_le))
        t.done(nc.vector.reduce_sum(self.lookup[:, :], self.passed[:, :, :], axis=AX_X))
        t.done(nc.vector.tensor_scalar(self.lookup[:, :], self.lookup[:, :], float(EX - 1), None, ALU.min))
        nc.vector.tensor_copy(self.lookup_int[:, :], self.lookup[:, :]).then_inc(self.table.sem, 1)

    def scatter(self, pool):
        g, nc = self.g, self.g.nc
        pool.wait_ge(*self.filled.at(16 * self.FILLS))
        pool.wait_ge(*self.positions.at(1))
        for n in range(NT):
            for k in range(2):
                nc.gpsimd.indirect_dma_start(self.xs, bass.IndirectOffsetOnAxis(ap=self.row[:, k, n:n + 1], axis=0),
                                             g.X[:, n, :], None).then_inc(self.scattered.sem, 16)


    def steps(self, eng, body):
        def part(js, i):
            for j in js:
                body(j, i)

        part(range(2), None)
        turns = (self.BLOCKS - 4) // 4
        with eng.Fori(0, turns) as i:
            part(range(2, 6), 2 * i)
        part(range(2 + 4 * turns, self.BLOCKS + 1), None)

    def block(self, j, i):
        return None if j < 0 or j >= self.BLOCKS else Batch(j, i)

    def used(self, b, times):
        return b.first is None or b.first >= times

    def expert(self, eng, b):
        return eng.value_load(self.lookup_int[0:1, bass.ds(b.no, 1)], min_val=0, max_val=EX - 1)

    def load_weights(self, sp):
        g = self.g
        for a in range(2):
            sp.dma_start(self.w12[:, a, :, :], g.io["ex_w12"][:, a, :, :]).then_inc(self.weights_in.sem, 16)
        sp.dma_start(self.w3, g.io["ex_w3"]).then_inc(self.weights_in.sem, 16)

    def sync(self, sp, out):
        def load(b):
            sp.dma_start(self.xb[b.par], block_of(self.xs, b)).then_inc(self.x_in[b.par].sem, 16)

        g = self.g
        block_of = lambda dram, b: dram.rearrange("(n p) d -> p n d", p=P)[:, bass.ds(b.no, 1), :].rearrange("p n d -> p (n d)")
        sp.wait_ge(*self.scattered.at(16 * 2 * NT))
        load(Batch(0))
        load(Batch(1))

        def step(j, i):
            if self.block(j + 2, i) and (i is not None or j + 2 < self.BLOCKS):
                sp.wait_ge(*self.turned.at(Batch(j, i).no + 1))
                load(Batch(j + 2, i))
            if j >= 1:
                b = Batch(j - 1, i)
                sp.wait_ge(*self.y_ready.at(b.no + 1))
                sp.dma_start(block_of(self.ys, b), self.yb[b.par])\
                  .then_inc(self.y_out[b.par].sem, 16)

        self.steps(sp, step)
        for c in range(NC):
            sp.wait_ge(*self.normed.at(c + 1))
            sp.dma_start(out.rearrange("(t p) d -> p t d", p=P)[:, c * TC:(c + 1) * TC, :],
                         g.X[:, c * TC:(c + 1) * TC, :]).then_inc(self.stored.sem, 16)
        sp.wait_ge(*self.stored.at(16 * NC))

    def tensor(self, pe):
        g, nc = self.g, self.g.nc

        def turn_x(b):
            pe.wait_ge(*self.x_in[b.par].at((b.use + 1) * 16))
            if self.used(b, 1):
                pe.wait_ge(*self.xt_ready.at(b.no))
            nc.tensor.transpose(g.bank[7][:, 0:P], self.xb[b.par], g.ident[:, :]).then_inc(self.turned.sem, 1)

        def gate_or_up(b, a, e):
            nc.tensor.matmul(g.bank[2 * a + b.par], self.xt[b.par],
                             self.w12[:, a, bass.ds(e, 1), :].rearrange("p e f -> p (e f)"), start=True, stop=True)\
              .then_inc((self.up if a else self.gate).sem, 1)

        def turn_h(b):
            pe.wait_ge(*self.mixed.at(b.no + 1))
            if self.used(b, 2):
                pe.wait_ge(*self.ht_ready.at(b.no - 1))
            for f in range(self.FT):
                last = nc.tensor.transpose(g.bank[4 + b.par][:, f * P:(f + 1) * P], self.hid[b.par][:, f * P:(f + 1) * P],
                                           g.ident[:, :])
            last.then_inc(self.h_turned.sem, 1)

        def down(b, e):
            pe.wait_ge(*self.ht_ready.at(b.no + 1))
            if self.used(b, 1):
                pe.wait_ge(*self.y_ready.at(b.no))
            for f in range(self.FT):
                last = nc.tensor.matmul(g.bank[6][:, 0:D], self.ht[b.par][:, f, :],
                                        self.w3[:, bass.ds(e, 1), f, :].rearrange("p e d -> p (e d)"),
                                        start=f == 0, stop=f == self.FT - 1)
            last.then_inc(self.down.sem, 1)

        experts = {}

        def gate(b, j):
            pe.wait_ge(*self.xt_ready.at(b.no + 1))
            if self.used(b, 2):
                pe.wait_ge(*self.mixed.at(b.no - 1))
            gate_or_up(b, 0, experts[j])

        def step(j, i):
            b, before, after = self.block(j, i), self.block(j - 1, i), self.block(j + 1, i)
            turn_starts = i is not None and j == 2 or i is None and j == self.BLOCKS - 2
            if before:
                turn_h(before)
            if after:
                turn_x(after)
            if b:
                if turn_starts:
                    experts[j] = self.expert(nc.tensor, b)
                gate_or_up(b, 1, experts[j])
            if before:
                if turn_starts:
                    experts[j - 1] = self.expert(nc.tensor, before)
            if after:
                experts[j + 1] = self.expert(nc.tensor, after)
            if before:
                down(before, experts[j - 1])
            if after:
                gate(after, j + 1)

        pe.wait_ge(*self.table.at(1))
        pe.wait_ge(*self.weights_in.at(48))
        turn_x(Batch(0))
        experts[0] = self.expert(nc.tensor, Batch(0))
        gate(Batch(0), 0)
        self.steps(pe, step)

    def scalar(self, act):
        g, nc = self.g, self.g.nc

        def copy_x(b):
            act.wait_ge(*self.turned.at(b.no + 1))
            if self.used(b, 2):
                act.wait_ge(*self.up.at(b.no - 1))
            nc.scalar.copy(self.xt[b.par], g.bank[7][:, 0:P]).then_inc(self.xt_ready.sem, 1)

        def step(j, i):
            b, before, after = self.block(j, i), self.block(j - 1, i), self.block(j + 1, i)
            if b:
                act.wait_ge(*self.gate.at(b.no + 1))
                if self.used(b, 2):
                    act.wait_ge(*self.halved.at(b.no - 1))
                nc.scalar.activation(g.fbuf[b.par][:, :], g.bank[b.par], ACT.Tanh, scale=0.5).then_inc(self.tanh.sem, 1)
            if before:
                act.wait_ge(*self.h_turned.at(before.no + 1))
                if self.used(before, 2):
                    act.wait_ge(*self.down.at(before.no - 1))
                nc.scalar.copy(self.ht[before.par], g.bank[4 + before.par].rearrange("p (n t) -> p n t", t=P))\
                   .then_inc(self.ht_ready.sem, 1)
            if after:
                copy_x(after)

        copy_x(Batch(0))
        self.steps(act, step)

    def vector(self, dve):
        g, nc, r, t = self.g, self.g.nc, self.router, self.t

        def step(j, i):
            b, before = self.block(j, i), self.block(j - 1, i)
            if b:
                dve.wait_ge(*self.tanh.at(b.no + 1))
                if self.used(b, 2):
                    dve.wait_ge(*self.mixed.at(b.no - 1))
                nc.vector.scalar_tensor_tensor(g.turn[b.par][:, :], g.fbuf[b.par][:, :], 1.0, g.bank[b.par],
                                               ALU.add, ALU.mult).then_inc(self.halved.sem, 1)
            if b:
                dve.wait_ge(*self.up.at(b.no + 1))
                dve.wait_ge(*self.halved.at(b.no + 1))
                if self.used(b, 2):
                    dve.wait_ge(*self.h_turned.at(b.no - 1))
                nc.vector.scalar_tensor_tensor(self.hid[b.par][:, :], g.turn[b.par][:, :], 0.5, g.bank[2 + b.par],
                                               ALU.mult, ALU.mult).then_inc(self.mixed.sem, 1)
            if before:
                dve.wait_ge(*self.down.at(before.no + 1))
                if self.used(before, 2):
                    dve.wait_ge(*self.y_out[before.par].at(before.use * 16))
                nc.vector.tensor_copy(self.yb[before.par], g.bank[6][:, 0:D]).then_inc(self.y_ready.sem, 1)

        self.steps(dve, step)

        for c in range(NC):
            dve.wait_ge(*self.gathered[c].at(16 * 2 * TC))
            x = g.X[:, c * TC:(c + 1) * TC, :]
            for k, y in enumerate((g.V, g.CX)):
                for n in range(c * TC, (c + 1) * TC):
                    last = nc.vector.scalar_tensor_tensor(g.X[:, n, :], y[:, n, :], r.gate[:, k, n:n + 1], g.X[:, n, :],
                                                          ALU.mult, ALU.add)
                t.done(last)
            layernorm(g, t, x, x).then_inc(self.normed.sem, 1)

    def gather(self, pool):
        g, nc = self.g, self.g.nc
        for par in range(2):
            pool.wait_ge(*self.y_out[par].at(16 * self.BLOCKS // 2))
        for n in range(NT):
            for k, y in enumerate((g.V, g.CX)):
                nc.gpsimd.indirect_dma_start(y[:, n, :], None, self.ys,
                                             bass.IndirectOffsetOnAxis(ap=self.row[:, k, n:n + 1], axis=0))\
                  .then_inc(self.gathered[n // TC].sem, 16)


WEIGHTS = ["a0_qa", "a0_qb", "a0_ka", "a0_kb", "a0_v", "a0_o",
           "a1_q", "a1_k", "a1_v", "a1_o", "a1_fq", "a1_fg",
           "x1_q", "x1_k", "x1_v", "x1_o", "f0_q", "f0_k", "f0_v", "f0_o"]
COLUMNS = ["a1_bq", "a1_bk", "a1_bfq", "a1_bfg", "f0_g1", "f0_g2"]
ROWVECS = ["a1_bv", "a1_bo", "x1_bo"]


class Globals:

    def __init__(self, nc, ctx, io):
        self.nc, self.ctx, self.io = nc, ctx, io
        self.shared = {}

    def sem(self, name):
        return Signal(self.ctx.enter_context(self.nc.semaphore(name)), 0)

    def shared_sem(self, name, total):
        if name not in self.shared:
            self.shared[name] = [self.sem(name).sem, 0]
        sem, base = self.shared[name]
        self.shared[name][1] += total
        return Signal(sem, base)

    def sb(self, name, shape, dt=F32):
        return self.ctx.enter_context(self.nc.sbuf_tensor(name, shape, dt))

    def allocate(self):
        nc = self.nc
        sb = self.sb
        self.X = sb("X", [P, NT, D])
        self.XT = sb("XT", [P, T])
        self.CTX = sb("CTX", [P, NT, D])
        self.CTXT = sb("CTXT", [P, T])
        self.V = sb("V", [P, NT, D])
        self.CX = sb("CX", [P, NT, D])
        self.CXT = sb("CXT", [P, 2, CH])
        self.BIG = sb("BIG", [P, 3 * EX * FE])
        big = [self.BIG[:, i * H * S // 2:(i + 1) * H * S // 2] for i in range(6)]
        self.Q6 = [b.bitcast(BF16).rearrange("p (h s) -> p h s", h=H) for b in big[0:2]]
        self.K6 = [b.bitcast(BF16).rearrange("p (h s) -> p h s", h=H) for b in big[2:4]]
        self.PT = [b.rearrange("p (h q) -> p h q", h=4) for b in big[4:6]]
        self.VA = [sb(f"VA_{i}", [P, 2, H, PVW]) for i in range(2)]
        self.OT = [sb(f"OT_{i}", [P, 4, S]) for i in range(2)]
        self.MS = sb("MS", [P, 2, H])
        self.MB = [sb(f"MB_{i}", [P, 2, 16], BF16) for i in range(2)]
        self.MT = [sb(f"MT_{i}", [16, S], BF16) for i in range(2)]
        self.rsum = sb("rsum", [P, H])
        self.fbuf = [sb(f"fbuf{i}", [P, CH]) for i in range(2)]
        self.rbuf = [sb(f"rbuf{i}", [P, CH]) for i in range(2)]
        self.turn = [sb(f"turn{i}", [P, CH]) for i in range(2)]
        self.parts = [sb(f"parts{i}", [P, 3, CH], BF16) for i in range(NPARTS)]
        self.Y = sb("Y", [P, TC, D])
        self.stats = sb("stats", [P, 2 * TC, 6])
        self.meanvar = sb("meanvar", [P, 2 * TC, 2])
        self.var = sb("var", [P, 2 * TC])
        self.rstd = sb("rstd", [P, TC])
        self.scale = [sb(f"scale{i}", [P, 2 * TC]) for i in range(2)]
        self.offset = [sb(f"offset{i}", [P, 2 * TC]) for i in range(2)]
        self.square = sb("square", [P, 2 * TC])
        self.ident = sb("ident", [P, P])
        self.ident_bf = sb("ident_bf", [P, P], BF16)
        self.cos = sb("cos", [P, S])
        self.sin = sb("sin", [P, S])
        self.W = sb("W", [P, len(WEIGHTS), P])
        self.cols = sb("cols", [P, len(COLUMNS)])
        self.rowvecs = sb("rowvecs", [1, len(ROWVECS), D])
        self.ones_row = sb("ones_row", [1, P])
        self.causal_q = sb("causal_q", [P, 2 * S], BF16)
        self.causal_k = sb("causal_k", [P, 2 * S], BF16)
        PS = self.ctx.enter_context(nc.psum_tensor("PS", [P, 8, CH], F32))
        self.bank = [PS[:, i, :] for i in range(8)]
        self.bank2 = [PS[:, 2 * i:2 * i + 2, :] for i in range(2)]
        self.aux_bf = PS[:, 7, :].bitcast(BF16)
        self.mask_q = sb("mask_q", [P, B * 2 * S], BF16)
        self.mask_k = sb("mask_k", [P, B * 2 * S], BF16)
        self.depth_q = sb("depth_q", [P, P], BF16)
        self.depth_k = sb("depth_k", [P, P], BF16)
        self.router = sb("router", [P, P])
        self.earlier = sb("earlier", [P, 2, S])
        self.iota = sb("iota", [P, P])
        self.f0_w12 = sb("f0_w12", [P, 2, F0])
        self.f0_w3 = sb("f0_w3", [P, 3, D])
        self.upz = sb("upz", [P, 2 * H])
        self.router_w = sb("router_w", [P, EX])
        self.router_b = sb("router_b", [P, EX])
        self.descending = sb("descending", [P, EX])
        self.multiples = sb("multiples", [P, T // P])
        self.up_to = sb("up_to", [P, EX, EX])
        self.upper_bf = sb("upper_bf", [P, P], BF16)
        self.ones_bf = sb("ones_bf", [P, P], BF16)

    def w(self, name):
        return self.W[:, WEIGHTS.index(name), :]

    def col(self, name):
        i = COLUMNS.index(name)
        return self.cols[:, i:i + 1]

    def row(self, name):
        return self.rowvecs[0:1, ROWVECS.index(name), :]


def program(nc, io, out):
    with ExitStack() as ctx:
        g = Globals(nc, ctx, io)
        g.allocate()
        sem = g.sem
        dram = lambda name, shape, dt: nc.dram_tensor(name, shape, dt, kind="Internal").ap()
        rows_q = [dram(f"rows_q{i}", (ROWS, H, T), BF16) for i in range(2)]
        rows_k = [dram(f"rows_k{i}", (ROWS, H, T), BF16) for i in range(2)]
        rows_x = dram("rows_x", (9, H, T), BF16)
        mask = Mask(g)

        weights_in = sem("weights_in")
        first_in, x_in, ctx_in = sem("first_in"), sem("x_in"), sem("ctx_in")
        xt_in = [sem(f"xt_in{c}") for c in range(NC)]
        zeroed, k_zeroed, va_zeroed = sem("zeroed"), sem("k_zeroed"), sem("va_zeroed")
        const_rows = [sem(f"const_rows{i}") for i in range(4)]

        def chunks(ap):
            return [ap[:, c * CH:(c + 1) * CH] for c in range(NC)]

        xt, ctxt = chunks(g.XT[:, :]), chunks(g.CTXT[:, :])

        jobs = []
        for c in range(NC):
            for wa, wb, to in (("a0_qa", "a0_qb", rows_q[0]), ("a0_ka", "a0_kb", rows_k[0])):
                jobs.append(dict(kind="rope", w=[g.w(wa), g.w(wb)], src=xt[c], to=to, query=to is rows_q[0]))
        split_a0 = Split(g, "sa0", jobs, (g.w("a0_v"), g.XT, None), NC)
        core_a0 = Core(g, "ca0", B, 2)
        post_a0 = Post(g, "pa0", core_a0, g.w("a0_o"))

        jobs = []
        for c in range(NC):
            jobs.append(dict(kind="sbuf", src=xt[c], to=rows_q[1], query=True))
            jobs.append(dict(kind="sbuf", src=ctxt[c], to=rows_k[1], query=False))
        split_x0 = Split(g, "sx0", jobs, None, NC)
        core_x0 = Core(g, "cx0", B, 2, causal=True, bias=(g.causal_q[:, :], g.causal_k[:, :]))
        post_x0 = Post(g, "px0", core_x0)

        depths = Depths(g, "f0")
        jobs = [dict(kind="psum", w=[g.w("f0_q")], src=depths.HT[:, :], to=rows_q[0], query=True),
                dict(kind="psum", w=[g.w("f0_k")], src=depths.HT[:, :], to=rows_k[0], query=False)]
        split_f0 = Split(g, "sf0", jobs, (g.w("f0_v"), depths.HT, None), 1)
        core_f0 = Core(g, "cf0", depths.NP, 1, bias=(g.depth_q[:, :], g.depth_k[:, :]))

        gauss = Gauss(g, "ga1")
        jobs = []
        for c in range(NC):
            jobs.append(dict(kind="keep", w=[g.w("a1_q")], src=xt[c], bias=g.col("a1_bq"),
                             keep=gauss.MQ[:, c * CH:(c + 1) * CH], to=rows_q[1], query=True))
            jobs.append(dict(kind="psum", w=[g.w("a1_k")], src=xt[c], bias=g.col("a1_bk"), to=rows_k[1], query=False))
        split_a1 = Split(g, "sa1", jobs, (g.w("a1_v"), g.XT, g.row("a1_bv")), NC)
        core_a1 = Core(g, "ca1", B, 2, xrows=9)
        post_a1 = Post(g, "pa1", core_a1, g.w("a1_o"), g.row("a1_bo"))

        jobs = []
        for c in range(NC):
            jobs.append(dict(kind="psum", w=[g.w("x1_q")], src=xt[c], to=rows_q[0], query=True))
            jobs.append(dict(kind="psum", w=[g.w("x1_k")], src=ctxt[c], to=rows_k[0], query=False))
        split_x1 = Split(g, "sx1", jobs, (g.w("x1_v"), g.CTXT, None), NC)
        core_x1 = Core(g, "cx1", B, 2, bias="batch")
        post_x1 = Post(g, "px1", core_x1, g.w("x1_o"), g.row("x1_bo"))
        router = Router(g)
        experts = Experts(g, router, dram("experts_x", (Experts.BLOCKS * P, D), F32), dram("experts_y", (Experts.BLOCKS * P, D), F32))

        block = ctx.enter_context(nc.Block())

        def const_rows_in(sp, n):
            for i in range(2):
                sp.dma_start(g.K6[i][XROW:XROW + 16, :, :], io["k_extra"][n % 3]).then_inc(const_rows[n].sem, 16)
                if n == 1:
                    sp.dma_start(g.Q6[i][XROW:XROW + 16, :, :], io["q_extra"]).then_inc(const_rows[n].sem, 16)

        @block.sync
        def _(sp):
            n_a0 = WEIGHTS.index("a0_o")
            sp.dma_start(g.W[:, 0:n_a0, :], io["weights"][:, 0:n_a0, :]).then_inc(first_in.sem, 16)
            for c in range(NC):
                sp.dma_start(g.XT[:, c * CH:(c + 1) * CH], io["xt"][:, c * CH:(c + 1) * CH]).then_inc(xt_in[c].sem, 16)
                if c == 0:
                    sp.dma_start(g.cos[:, :], io["cos"]).then_inc(first_in.sem, 16)
                    sp.dma_start(g.sin[:, :], io["sin"]).then_inc(first_in.sem, 16)
            sp.dma_start(g.W[:, n_a0:, :], io["weights"][:, n_a0:, :]).then_inc(weights_in.sem, 16)
            mask.sync(sp)
            for ap, name in ((g.ident, "ident"), (g.ident_bf, "ident_bf"), (g.cols, "cols"), (g.causal_q, "causal_q"),
                             (g.causal_k, "causal_k"), (g.ones_row, "ones_row"), (g.depth_q, "depth_q"),
                             (g.depth_k, "depth_k"), (g.router, "router"), (g.iota, "iota"), (g.upz, "upz"),
                             (g.router_w, "router_w"), (g.router_b, "router_b"), (g.descending, "descending"),
                             (g.multiples, "multiples"), (g.upper_bf, "upper_bf"),
                             (g.ones_bf, "ones_bf")):
                sp.dma_start(ap[:, :], io[name]).then_inc(weights_in.sem, 16)
            for ap, name in ((g.rowvecs, "rowvecs"), (g.up_to, "up_to"), (g.earlier, "earlier"), (g.f0_w12, "f0_w12"), (g.f0_w3, "f0_w3")):
                sp.dma_start(ap[:, :, :], io[name]).then_inc(weights_in.sem, 16)
            sp.dma_start(g.X[:, :, :], io["x"].rearrange("(t p) d -> p t d", p=P)).then_inc(x_in.sem, 16)
            sp.dma_start(g.CTX[:, :, :], io["ctx"].rearrange("(t p) d -> p t d", p=P)).then_inc(ctx_in.sem, 16)
            sp.dma_start(g.CTXT[:, :], io["ctxt"]).then_inc(ctx_in.sem, 16)

            def first_loads():
                sp.wait_ge(*zeroed.at(4))
                core_a0.first_loads(sp, (rows_q[0], rows_k[0]))
            split_a0.sync(sp, first_loads)
            split_a0.wait_written(sp)
            core_a0.sync(sp, (rows_q[0], rows_k[0]))

            def first_loads():
                sp.wait_ge(*core_a0.st_ready.at(8 * B))
                const_rows_in(sp, 1)
                core_x0.first_loads(sp, (rows_q[1], rows_k[1]))
            split_x0.sync(sp, first_loads)
            split_x0.wait_written(sp)
            core_x0.sync(sp, (rows_q[1], rows_k[1]))

            def first_loads():
                sp.wait_ge(*core_x0.st_ready.at(8 * B))
                const_rows_in(sp, 0)
                core_f0.first_loads(sp, (rows_q[0], rows_k[0]))
            split_f0.sync(sp, first_loads)
            split_f0.wait_written(sp)
            core_f0.sync(sp, (rows_q[0], rows_k[0]))

            def first_loads():
                sp.wait_ge(*core_f0.st_ready.at(8 * depths.NP))
                const_rows_in(sp, 2)
                core_a1.first_loads(sp, (rows_q[1], rows_k[1], rows_x), "qk")
            split_a1.sync(sp, first_loads)
            gauss.sync(sp, rows_x)
            sp.wait_ge(*gauss.written.at(48))
            core_a1.first_loads(sp, (rows_q[1], rows_k[1], rows_x), "x")
            split_a1.wait_written(sp)
            core_a1.sync(sp, (rows_q[1], rows_k[1], rows_x))

            def first_loads():
                sp.wait_ge(*core_a1.st_ready.at(8 * B))
                const_rows_in(sp, 3)
                core_x1.first_loads(sp, (rows_q[0], rows_k[0]))
            split_x1.sync(sp, first_loads)
            split_x1.wait_written(sp)
            core_x1.sync(sp, (rows_q[0], rows_k[0]))

            sp.wait_ge(*core_x1.pv_done.at(4 * B))
            experts.load_weights(sp)
            experts.sync(sp, out)

        @block.tensor
        def _(pe):
            pe.wait_ge(*first_in.at(48))

            def ready(c):
                pe.wait_ge(*xt_in[c].at(16))
            split_a0.tensor(pe, ready)
            pe.wait_ge(*weights_in.at(16 * 23))
            pe.wait_ge(*split_a0.v_ready.at(NC))
            mask.tensor(pe)

            def ready():
                pe.wait_ge(*mask.copied.at(4))
                pe.wait_ge(*split_a0.r1_ready.at(2 * NC))
                pe.wait_ge(*split_a0.v_ready.at(NC))
                pe.wait_ge(*zeroed.at(4))
            core_a0.tensor(pe, ready)

            def ready():
                pe.wait_ge(*core_a0.cx_done.at(NT))
                pe.wait_ge(*core_a0.ot_done.at(4 * B))
                pe.wait_ge(*core_a0.mx_done.at(16 * B))
            ready()
            post_a0.run("tensor", pe, "after")
            split_x0.tensor(pe, lambda c: None)

            def ready():
                pe.wait_ge(*const_rows[1].at(64))
                pe.wait_ge(*post_a0.xt_ready.at(NC))
            core_x0.tensor(pe, ready)

            def ready():
                pe.wait_ge(*core_x0.cx_done.at(NT))
                pe.wait_ge(*core_x0.ot_done.at(4 * B))
                pe.wait_ge(*core_x0.mx_done.at(16 * B))
            ready()
            post_x0.run("tensor", pe, "after")

            def ready(c):
                pe.wait_ge(*post_x0.xt_ready.at(c + 1))
            depths.select_tensor(pe, ready)

            def ready(c):
                pe.wait_ge(*depths.h_ready.at(1))
            split_f0.tensor(pe, ready)

            def ready():
                pe.wait_ge(*split_f0.r1_ready.at(2))
                pe.wait_ge(*split_f0.v_ready.at(1))
                pe.wait_ge(*const_rows[0].at(32))
            core_f0.tensor(pe, ready)

            def ready():
                pe.wait_ge(*core_f0.cx_done.at(depths.NP))
                pe.wait_ge(*core_f0.ot_done.at(4 * depths.NP))
                pe.wait_ge(*core_f0.mx_done.at(8 * depths.NP))
            depths.feed_tensor(pe, ready)

            def ready(c):
                pe.wait_ge(*depths.xt_ready.at(c + 1))
            split_a1.tensor(pe, ready)
            gauss.tensor(pe)

            def ready():
                pe.wait_ge(*split_a1.r1_ready.at(2 * NC))
                pe.wait_ge(*split_a1.v_ready.at(NC))
                pe.wait_ge(*gauss.copied.at(2))
                pe.wait_ge(*const_rows[2].at(32))
            core_a1.tensor(pe, ready)

            def ready():
                pe.wait_ge(*core_a1.cx_done.at(NT))
                pe.wait_ge(*core_a1.ot_done.at(4 * B))
                pe.wait_ge(*core_a1.mx_done.at(16 * B))
            ready()
            post_a1.run("tensor", pe, "after")

            def ready(c):
                pe.wait_ge(*post_a1.xt_ready.at(c + 1))
            split_x1.tensor(pe, ready)

            def ready():
                pe.wait_ge(*split_x1.r1_ready.at(2 * NC))
                pe.wait_ge(*split_x1.v_ready.at(NC))
                pe.wait_ge(*const_rows[3].at(32))
            core_x1.tensor(pe, ready)

            def ready():
                pe.wait_ge(*core_x1.cx_done.at(NT))
                pe.wait_ge(*core_x1.ot_done.at(4 * B))
                pe.wait_ge(*core_x1.mx_done.at(16 * B))
            ready()
            post_x1.run("tensor", pe, "after")

            def ready(c):
                pe.wait_ge(*post_x1.xt_ready.at(c + 1))
            router.tensor(pe, ready)

            experts.place_tensor(pe)
            experts.tensor(pe)

        @block.scalar
        def _(act):
            split_a0.scalar(act)
            mask.scalar(act)
            core_a0.scalar(act)
            post_a0.run("scalar", act, "after")
            def ready(a, c):
                if c == 0:
                    a.wait_ge(*ctx_in.at(32))
                a.wait_ge(*post_a0.xt_ready.at(c + 1))
            split_x0.scalar(act, ready)
            core_x0.scalar(act)
            post_x0.run("scalar", act, "after")
            depths.select_scalar(act)
            split_f0.scalar(act)
            core_f0.scalar(act)
            depths.feed_scalar(act)
            split_a1.scalar(act)
            gauss.scalar(act)
            core_a1.scalar(act)
            post_a1.run("scalar", act, "after")
            split_x1.scalar(act)
            core_x1.scalar(act)
            post_x1.run("scalar", act, "after")
            router.scalar(act)
            experts.scalar(act)

        @block.vector
        def _(dve):
            for buf in g.K6:
                last = nc.vector.memset(buf[:, :, :].bitcast(F32), 0.0)
            last.then_inc(k_zeroed.sem, 1)
            dve.wait_ge(*k_zeroed.at(1))
            for buf in g.K6:
                last = nc.vector.memset(buf[MROW:MROW + 2, :, :], 1.0)
            last.then_inc(zeroed.sem, 2)
            dve.wait_ge(*first_in.at(48))
            split_a0.vector(dve)
            for buf in g.VA:
                last = nc.vector.memset(buf[:, :, :, :], 0.0)
            last.then_inc(va_zeroed.sem, 1)
            dve.wait_ge(*va_zeroed.at(1))
            for buf in g.VA:
                last = nc.vector.memset(buf[:, :, :, DH:DH + 1], 1.0)
            last.then_inc(va_zeroed.sem, 1)
            mask.vector(dve)
            dve.wait_ge(*x_in.at(16))
            core_a0.vector(dve)
            post_a0.run("vector", dve, "after")
            split_x0.vector(dve)
            core_x0.vector(dve)
            dve.wait_ge(*core_x0.cx_done.at(NT))
            post_x0.run("vector", dve, "after")
            depths.select_vector(dve)
            split_f0.vector(dve)
            core_f0.vector(dve)
            depths.feed_vector(dve)
            split_a1.vector(dve)
            gauss.vector(dve, split_a1.kept)
            core_a1.vector(dve)
            post_a1.run("vector", dve, "after")
            split_x1.vector(dve)
            core_x1.vector(dve)
            post_x1.run("vector", dve, "after")
            router.vector(dve)
            experts.place_vector(dve)
            experts.vector(dve)

        @block.gpsimd
        def _(pool):
            for buf in g.Q6:
                nc.gpsimd.memset(buf[:, :, :].bitcast(F32), 0.0).then_inc(zeroed.sem, 1)
            split_a0.gpsimd(pool)
            def ready():
                pool.wait_ge(*va_zeroed.at(2))
                pool.wait_ge(*split_a0.v_ready.at(NC))
            core_a0.gpsimd(pool, g.V, ready)
            pool.wait_ge(*ctx_in.at(32))
            experts.fill(pool, (0, 1))
            split_x0.gpsimd(pool)
            def ready():
                pool.wait_ge(*ctx_in.at(32))
                pool.wait_ge(*core_a0.pv_done.at(4 * B))
            core_x0.gpsimd(pool, g.CTX, ready)
            experts.fill(pool, (2, 3))
            split_f0.gpsimd(pool)
            def ready():
                pool.wait_ge(*split_f0.v_ready.at(1))
                pool.wait_ge(*core_x0.pv_done.at(4 * B))
            core_f0.gpsimd(pool, g.V, ready)
            split_a1.gpsimd(pool)
            def ready():
                pool.wait_ge(*split_a1.v_ready.at(NC))
                pool.wait_ge(*core_f0.pv_done.at(4 * depths.NP))
            core_a1.gpsimd(pool, g.V, ready)
            experts.fill(pool, (4,))
            split_x1.gpsimd(pool)
            def ready():
                pool.wait_ge(*split_x1.v_ready.at(NC))
                pool.wait_ge(*core_a1.pv_done.at(4 * B))
            core_x1.gpsimd(pool, g.V, ready)
            pool.wait_ge(*post_x1.normed.at(NC))
            experts.scatter(pool)
            experts.gather(pool)


DFIRST = np.arange(D).reshape(H, DH).T.reshape(-1)


def rope_order(w, second):
    h, j = DFIRST // DH, DFIRST % DH
    i, high = j % (DH // 2), j >= DH // 2
    odd = high != second
    return w[h * DH + 2 * i + odd]


def constants():
    bf = mybir.dt.np(BF16)
    out = {}
    inv_freq = (np.float32(1.0) / np.float32(10000.0) ** (np.arange(0, DH, 2, dtype=np.float32) / np.float32(DH))).astype(np.float32)
    ang = (np.arange(S, dtype=np.float32)[None, :] * inv_freq[DFIRST % (DH // 2)][:, None]).astype(np.float32)
    sign = np.where(DFIRST % DH < DH // 2, -1.0, 1.0).astype(np.float32)[:, None]
    out["cos"] = np.cos(ang).astype(np.float32)
    out["sin"] = (np.sin(ang) * sign).astype(np.float32)
    out["ident"] = np.eye(P, dtype=np.float32)
    out["ident_bf"] = np.eye(P, dtype=np.float32).astype(bf)
    out["ones_row"] = np.ones((1, P), np.float32)
    q, k = np.arange(P)[:, None], np.arange(P)[None, :]
    cq = np.zeros((P, 2 * S), np.float32)
    cq[:, 0:P] = np.where(k > q, NEG_CAUSAL, 0.0)
    cq[:, 2 * P + P:4 * P] = cq[:, 0:P]
    ck = np.zeros((P, 2 * S), np.float32)
    ck[:, 0:P] = cq[:, 0:P].T
    ck[:, 2 * P:3 * P] = cq[:, 0:P].T
    out["causal_q"], out["causal_k"] = cq.astype(bf), ck.astype(bf)

    dq = np.where((q // SEL != k // SEL) | (k > q), NEG_CAUSAL, 0.0)
    out["depth_q"], out["depth_k"] = dq.astype(bf), np.ascontiguousarray(dq.T).astype(bf)
    tok = np.arange(S)
    out["earlier"] = (tok[None, None, :] < (q + P * np.arange(2)[None, :])[:, :, None]).astype(np.float32)
    out["descending"] = np.broadcast_to(np.arange(EX, 0, -1, dtype=np.float32)[None], (P, EX)).copy()
    out["multiples"] = np.broadcast_to(P * np.arange(T // P, dtype=np.float32)[None], (P, T // P)).copy()
    out["up_to"] = np.broadcast_to(np.tril(np.ones((EX, EX), np.float32))[None], (P, EX, EX)).copy()
    out["upper_bf"] = np.triu(np.ones((P, P), np.float32), 1).astype(bf)
    out["ones_bf"] = np.ones((P, P), np.float32).astype(bf)
    out["iota"] = np.broadcast_to(np.arange(P, dtype=np.float32)[None], (P, P)).copy()

    def three(a):
        a = a.astype(np.float32)
        p1 = a.astype(bf)
        p2 = (a - p1.astype(np.float32)).astype(bf)
        p3 = (a - p1.astype(np.float32) - p2.astype(np.float32)).astype(bf)
        return [p1, p2, p3]

    kx = np.zeros((4, 16, H, S), bf)
    key = np.arange(S, dtype=np.float32)
    kx[1, 0:3] = key.astype(bf)
    j = key - S // 2
    sq1 = (j * j).astype(bf)
    sq2 = (j * j - sq1.astype(np.float32)).astype(bf)
    kx[2, 0:3], kx[2, 3:6], kx[2, 6:9] = sq1, sq2, j.astype(bf)
    out["k_extra"] = kx
    slopes = np.cumprod(np.full((H,), 2.0 ** (-8.0 / H), np.float32)).astype(np.float32)
    qx = np.zeros((16, H, S), bf)
    for n, part in enumerate(three(slopes * np.float32(DH ** 0.5))):
        qx[n] = part[:, None]
    out["q_extra"] = qx
    return out


def layout(a):
    io = {}
    w = {
        "a0_qa": rope_order(a["L0_attn_Wq"], False).T, "a0_qb": rope_order(a["L0_attn_Wq"], True).T,
        "a0_ka": rope_order(a["L0_attn_Wk"], False).T, "a0_kb": rope_order(a["L0_attn_Wk"], True).T,
        "a0_v": a["L0_attn_Wv"].T, "a0_o": a["L0_attn_Wo"].T,
        "a1_q": a["L1_attn_wq"], "a1_k": a["L1_attn_wk"], "a1_v": a["L1_attn_wv"], "a1_o": a["L1_attn_wo"],
        "a1_fq": a["L1_attn_wfq"], "a1_fg": a["L1_attn_wfg"],
        "x1_q": a["L1_xattn_Wq"].T, "x1_k": a["L1_xattn_Wk"].T, "x1_v": a["L1_xattn_Wv"].T, "x1_o": a["L1_xattn_Wo"].T,
        "f0_q": a["L0_ffn_W_qkv"][0:D].T, "f0_k": a["L0_ffn_W_qkv"][D:2 * D].T, "f0_v": a["L0_ffn_W_qkv"][2 * D:].T,
        "f0_o": a["L0_ffn_W_out"].T,
    }
    for n in w:
        w[n] = w[n][DFIRST] if n in ("a0_qa", "a0_qb", "a0_ka", "a0_kb") else w[n][DFIRST][:, DFIRST]
    io["weights"] = np.stack([w[n] for n in WEIGHTS], axis=1)
    cols = {"a1_bq": a["L1_attn_bq"], "a1_bk": a["L1_attn_bk"], "a1_bfq": a["L1_attn_bfq"], "a1_bfg": a["L1_attn_bfg"],
            "f0_g1": a["L0_ffn_g1"], "f0_g2": a["L0_ffn_g2"]}
    io["cols"] = np.stack([cols[n][DFIRST] for n in COLUMNS], axis=1)
    rows = {"a1_bv": a["L1_attn_bv"], "a1_bo": a["L1_attn_bo"], "x1_bo": a["L1_xattn_bo"]}
    io["rowvecs"] = np.stack([rows[n][DFIRST] for n in ROWVECS])[None]
    io["router"] = np.repeat(a["L0_ffn_w_router"][DFIRST][:, None], P, axis=1)
    io["f0_w12"] = np.stack([a["L0_ffn_W1"].T[DFIRST], a["L0_ffn_W2"].T[DFIRST]], axis=1)
    w3 = np.zeros((3 * P, D), np.float32)
    w3[0:F0] = a["L0_ffn_W3"].T[:, DFIRST]
    io["f0_w3"] = w3.reshape(3, P, D).transpose(1, 0, 2)
    upz = np.zeros((D, 2 * H), np.float32)
    for n, name in enumerate(("L1_attn_up", "L1_attn_uz")):
        for h in range(H):
            upz[np.arange(DH) * H + h, n * H + h] = a[name][h, 0]
    io["upz"] = upz
    io["router_w"] = a["L1_ffn_router_w"].T[DFIRST]
    io["router_b"] = np.repeat(a["L1_ffn_router_b"][None], P, axis=0)
    io["ex_w12"] = np.stack([a[f"L1_ffn_{n}_w"].transpose(2, 0, 1)[DFIRST] for n in ("gate", "up")], axis=1)
    io["ex_w3"] = a["L1_ffn_down_w"][:, DFIRST].reshape(EX, D, FE // P, P).transpose(3, 0, 2, 1)
    io["mask"] = a["mask_Bx1xSxS2_if1"].reshape(B * S, S)
    io["x"] = a["x"].reshape(T, D)[:, DFIRST]
    io["xt"] = io["x"].T
    io["ctx"] = a["ctx_1024"].reshape(T, D)[:, DFIRST]
    io["ctxt"] = io["ctx"].T
    return io


def kernel(**inputs):
    import concourse.bacc as _bacc
    from concourse.bass_utils import run_bass_kernel_spmd as _run

    arrays = {n: np.ascontiguousarray(v) for n, v in
              (layout({k: np.asarray(v) for k, v in inputs.items()}) | constants()).items()}
    nc = _bacc.Bacc("TRN2", target_bir_lowering=False, num_devices=1)
    io = {n: nc.dram_tensor(f"in_{n}", v.shape, mybir.dt.from_np(v.dtype), kind="ExternalInput").ap()
          for n, v in arrays.items()}
    out = nc.dram_tensor("out_0", (T, D), F32, kind="ExternalOutput").ap()
    program(nc, io, out)
    r = _run(nc, [{f"in_{n}": v for n, v in arrays.items()}], core_ids=[0])
    return r.results[0]["out_0"][:, np.argsort(DFIRST)].reshape(B, S, D)
```

```python
from contextlib import ExitStack

import numpy as np

import concourse.bass as bass
from concourse import mybir

F32 = mybir.dt.float32
BF16 = mybir.dt.bfloat16
I32 = mybir.dt.int32
U32 = mybir.dt.uint32
ALU = mybir.AluOpType
ACT = mybir.ActivationFunctionType
AX_X = mybir.AxisListType.X

P = 128
D = 128
H = 16
DH = D // H
B = 8
S = 256
T = B * S
NT = T // P
CH = 512
TC = CH // P
NC = T // CH
SCALE = float(DH) ** -0.5
EPS = 1e-5
PARTS = 6
ROWS = PARTS * DH
XROW = ROWS
MROW = 96
TWO_ONES = float(np.array([0x3F803F80], np.uint32).view(np.float32)[0])
NEG_CAUSAL = -1e30
NEG_MASK = -1e20
PVW = 32
NPARTS = 4
SEL = 64
F0 = 341
EX = 8
FE = 512


class Batch:

    def __init__(self, c, i=None):
        self.no = c if i is None else 2 * i + c
        self.par = c % 2
        self.use = c // 2 if i is None else i + c // 2
        self.first = c if i is None else None


class Signal:

    def __init__(self, sem, base):
        self.sem, self.base = sem, base

    def at(self, n):
        return self.sem, self.base + n


class Tally:

    def __init__(self, eng, raised):
        self.eng, self.raised, self.n, self.base = eng, raised, 0, 0

    def done(self, ins):
        self.n += 1
        ins.then_inc(self.raised.sem, 1)
        self.eng.wait_ge(*self.raised.at(self.base + self.n))

    def loop(self, i, per):
        self.start, self.per, self.base = self.n, per, i * per

    def end(self, turns):
        assert self.n - self.start == self.per, (self.n - self.start, self.per)
        self.n += self.per * (turns - 1)
        self.base = 0



class Split:

    def __init__(self, g, jobs, values, nchunks, banks=(0, 1, 2, 3)):
        self.g, self.jobs, self.values, self.nchunks = g, jobs, values, nchunks
        self.has_pe = [j for j in jobs if j["kind"] != "sbuf"]
        kinds = [j["kind"] for j in jobs]
        n, n_v, n_rope = len(jobs), nchunks if values else 0, kinds.count("rope")
        self.projected = g.shared_sem("split_projected", len(self.has_pe))
        self.turned = g.shared_sem("split_turned", n_rope)
        self.rotated = g.shared_sem("split_rotated", n_rope)
        self.s1_ready = g.shared_sem("split_s1_ready", n)
        self.r1_ready = g.shared_sem("split_r1_ready", n)
        self.s2_ready = g.shared_sem("split_s2_ready", n)
        self.s3_ready = g.shared_sem("split_s3_ready", n)
        self.v_projected = g.shared_sem("split_v_projected", n_v)
        self.v_ready = g.shared_sem("split_v_ready", n_v)
        self.kept = g.shared_sem("split_kept", kinds.count("keep"))
        self.written = [g.shared_sem(f"split_written{i}", self.writes(len(jobs) - 1, i)) for i in range(NPARTS)]
        for n, j in enumerate(self.has_pe):
            j["n_pe"] = n
        for n, j in enumerate(j for j in jobs if j["kind"] == "keep"):
            j["n_keep"] = n

        self.banks = banks[::2] if n_rope else banks

    def writes(self, n, i):
        return sum(48 if j["query"] else 16 for m, j in enumerate(self.jobs[:n + 1]) if m % NPARTS == i)

    def bank(self, job):
        return self.banks[job["n_pe"] % len(self.banks)]

    def turn(self, n, i):
        return self.g.CX[:, (n % 2 * 2 + i) * TC:(n % 2 * 2 + i + 1) * TC, :].rearrange("p n d -> p (n d)")

    def tensor(self, pe, ready):
        for _ in self.tensor_steps(pe, ready):
            pass

    def tensor_steps(self, pe, ready):
        g, nc = self.g, self.g.nc
        per = len(self.jobs) // self.nchunks
        for c in range(self.nchunks):
            ready(c)
            for j in self.jobs[c * per:(c + 1) * per]:
                if j["kind"] == "sbuf":
                    continue
                n, b = j["n_pe"], self.bank(j)
                if n >= len(self.banks):
                    before = self.has_pe[n - len(self.banks)]
                    if before["kind"] == "rope":
                        pe.wait_ge(*self.turned.at(before["n_pe"] + 1))
                    elif before["kind"] == "keep":
                        pe.wait_ge(*self.kept.at(before["n_keep"] + 1))
                    else:
                        pe.wait_ge(*self.r1_ready.at(self.jobs.index(before) + 1))
                for i, w in enumerate(j["w"]):
                    last = nc.tensor.matmul(g.bank[b + i][:, :], w, j["src"], start=True, stop=True)
                last.then_inc(self.projected.sem, 1)
            if self.values:
                w, src, _ = self.values
                sem, before = self.v_ready.at(c)
                if before > 0:
                    pe.wait_ge(sem, before)
                for t in range(TC):
                    last = nc.tensor.matmul(g.bank[4][:, t * P:(t + 1) * P], src[:, (c * TC + t) * P:(c * TC + t + 1) * P],
                                            w, start=True, stop=True)
                last.then_inc(self.v_projected.sem, 1)
            yield

    def scalar(self, act, ready=None):
        for _ in self.scalar_steps(act, ready):
            pass

    def scalar_steps(self, act, ready=None):
        g, nc = self.g, self.g.nc
        per = len(self.jobs) // self.nchunks

        def first_part(n):
            j = self.jobs[n]
            if n % per == 0 and ready:
                ready(act, n // per)
            sem, before = self.written[n % NPARTS].at(self.writes(n - 1, n % NPARTS))
            if before > 0:
                act.wait_ge(sem, before)
            s1 = g.parts[n % NPARTS][:, 0, :]
            src = j.get("src")
            if j["kind"] == "rope":
                act.wait_ge(*self.rotated.at(j["n_pe"] + 1))
                src = g.fbuf[n % 2][:, :]
            elif j["kind"] == "psum":
                act.wait_ge(*self.projected.at(j["n_pe"] + 1))
                src = g.bank[self.bank(j)][:, :]
            elif j["kind"] == "keep":
                act.wait_ge(*self.projected.at(j["n_pe"] + 1))
                nc.scalar.activation(j["keep"], g.bank[self.bank(j)][:, :], ACT.Identity,
                                     bias=j["bias"]).then_inc(self.kept.sem, 1)
                act.wait_ge(*self.kept.at(j["n_keep"] + 1))
                src = j["keep"]
            if j["kind"] == "psum" and j.get("bias") is not None:
                nc.scalar.activation(s1, src, ACT.Identity, bias=j["bias"]).then_inc(self.s1_ready.sem, 1)
            else:
                nc.scalar.copy(s1, src).then_inc(self.s1_ready.sem, 1)

        def second_part(n):
            act.wait_ge(*self.r1_ready.at(n + 1))
            nc.scalar.copy(g.parts[n % NPARTS][:, 1, :], g.rbuf[n % 2][:, :]).then_inc(self.s2_ready.sem, 1)

        for n in range(len(self.jobs) + 1):
            if self.values and n % per == 0 and n >= per:
                c = n // per - 1
                act.wait_ge(*self.v_projected.at(c + 1))
                nc.scalar.copy(self.values[2][:, c * TC:(c + 1) * TC, :], g.bank[4][:, :].rearrange("p (t d) -> p t d", t=TC))\
                   .then_inc(self.v_ready.sem, 1)
            if n < len(self.jobs):
                first_part(n)
            if n >= 1:
                second_part(n - 1)
            if n % per == per - 1:
                yield

    def vector(self, dve):
        for _ in self.vector_steps(dve):
            pass

    def vector_steps(self, dve):
        g, nc = self.g, self.g.nc
        per = len(self.jobs) // self.nchunks

        def rotate(n):
            j = self.jobs[n]
            dve.wait_ge(*self.projected.at(j["n_pe"] + 1))
            if j["n_pe"] >= 2:
                dve.wait_ge(*self.rotated.at(j["n_pe"] - 1))
            b = self.bank(j)
            for i, table in enumerate((g.cos, g.sin)):
                last = nc.vector.tensor_tensor(
                    self.turn(n, i).rearrange("p (b s) -> p b s", s=S),
                    g.bank[b + i][:, :].rearrange("p (b s) -> p b s", s=S),
                    table[:, :].unsqueeze(1).to_broadcast([P, CH // S, S]), ALU.mult)
            last.then_inc(self.turned.sem, 1)

        def remainder(n):
            j = self.jobs[n]
            src = {"rope": g.fbuf[n % 2][:, :], "keep": j.get("keep"), "sbuf": j.get("src")}.get(j["kind"])
            if j["kind"] == "psum":
                src = g.bank[self.bank(j)][:, :]
            dve.wait_ge(*self.s1_ready.at(n + 1))
            sem, before = self.s3_ready.at(n - 1)
            if before > 0:
                dve.wait_ge(sem, before)
            s1 = g.parts[n % NPARTS][:, 0, :]
            if j["kind"] == "psum" and j.get("bias") is not None:
                ins = nc.vector.scalar_tensor_tensor(g.rbuf[n % 2][:, :], src, j["bias"], s1, ALU.add, ALU.subtract)
            else:
                ins = nc.vector.tensor_tensor(g.rbuf[n % 2][:, :], src, s1, ALU.subtract)
            ins.then_inc(self.r1_ready.sem, 1)

        for n in range(len(self.jobs) + 1):
            if n < len(self.jobs) and self.jobs[n]["kind"] == "rope":
                rotate(n)
            if n >= 1:
                remainder(n - 1)
            if n % per == per - 1:
                yield

    def gpsimd(self, pool):
        g, nc = self.g, self.g.nc
        for n in range(len(self.jobs) + 1):
            if n < len(self.jobs) and self.jobs[n]["kind"] == "rope":
                pool.wait_ge(*self.turned.at(self.jobs[n]["n_pe"] + 1))
                if n >= 2:
                    pool.wait_ge(*self.r1_ready.at(n - 1))
                nc.gpsimd.tensor_tensor(g.fbuf[n % 2][:, :], self.turn(n, 0), self.turn(n, 1), ALU.add)\
                  .then_inc(self.rotated.sem, 1)
            if n >= 1:
                m = n - 1
                pool.wait_ge(*self.s2_ready.at(m + 1))
                nc.gpsimd.tensor_tensor(g.parts[m % NPARTS][:, 2, :], g.rbuf[m % 2][:, :], g.parts[m % NPARTS][:, 1, :],
                                        ALU.subtract).then_inc(self.s3_ready.sem, 1)

    def sync(self, sp, first_loads=None):
        g = self.g
        per = len(self.jobs) // self.nchunks
        for n, j in enumerate(self.jobs):
            c = n // per
            s = g.parts[n % NPARTS]
            rows = j["to"].rearrange("(r d) h t -> (d h) r t", d=DH)[:, :, c * CH:(c + 1) * CH]
            sp.wait_ge(*self.s3_ready.at(n + 1))
            if j["query"]:
                for first, k in ((0, 3), (3, 2), (5, 1)):
                    sp.dma_start(rows[:, first:first + k, :], s[:, 3 - k, :].unsqueeze(1).to_broadcast([P, k, CH]))\
                      .then_inc(self.written[n % NPARTS].sem, 16)
            else:
                sp.dma_start(rows, s[:, :, :]).then_inc(self.written[n % NPARTS].sem, 16)
            if first_loads and n == min(2 * per, len(self.jobs)) - 1:
                for i in range(per):
                    sp.wait_ge(*self.written[i].at(self.writes(i, i)))
                first_loads()

    def wait_written(self, eng):
        for i in range(NPARTS):
            if i < len(self.jobs):
                eng.wait_ge(*self.written[i].at(self.writes(len(self.jobs), i)))


class Core:

    def __init__(self, g, nb, nqt, causal=False, bias=None, xrows=0):
        self.g, self.nb, self.nqt, self.bias, self.xrows = g, nb, nqt, bias, xrows
        self.split = causal and nqt == 2
        self.queries = [(0, nqt * P)] + ([(P, P)] if self.split else [(0, nqt * P)]) * (nqt - 1)
        self.offset = [0, nqt * P][:nqt]
        self.width = sum(n for _, n in self.queries)
        self.keys = [P, 2 * P] if self.split else [nqt * P] * nqt
        self.nfeat = 4 + (1 if xrows else 0)
        self.tail = None
        self.st_ready = g.shared_sem("core_st_ready", 8 * nb)
        self.exp_done = g.shared_sem("core_exp_done", 8 * nb)
        self.mx_ready = g.shared_sem("core_mx_ready", 8 * nqt * nb)
        self.mx_done = g.shared_sem("core_mx_done", 8 * nqt * nb)
        self.mb_ready = g.shared_sem("core_mb_ready", 2 * nb)
        self.mt_ready = g.shared_sem("core_mt_ready", 2 * nb)
        self.mts_done = g.shared_sem("core_mts_done", 2 * nb)
        self.pv_done = g.shared_sem("core_pv_done", 4 * nb)
        self.ot_done = g.shared_sem("core_ot_done", 4 * nb)
        self.va_ready = g.shared_sem("core_va_ready", nb)
        self.cxt_ready = g.shared_sem("core_cxt_ready", nqt * nb)
        self.cx_done = g.shared_sem("core_cx_done", nqt * nb)
        self.chain = g.shared_sem("core_chain", (2 + nqt) * nb)
        self.feat = [[g.shared_sem(f"core_feat{p}{h}", 16 * self.nfeat * nb // 2) for h in range(2)] for p in range(2)]
        self.m_in = [[g.shared_sem(f"core_m_in{p}{h}", 32 * nb // 2) for h in range(2)] for p in range(2)]

    def steps(self, eng, body, last):
        body(0, None)
        body(1, None)
        turns = (last - 1) // 2
        if turns:
            with eng.Fori(0, turns) as i:
                body(2, i)
                body(3, i)
        for j in range(2 + 2 * turns, self.nb + 2):
            body(j, None)

    def batches(self, j, i):
        out = []
        for lag in range(3):
            c = j - lag
            out.append(None if c < 0 or c >= self.nb else Batch(c, i))
        return out

    def bias_for(self, b, transposed):
        g = self.g
        if self.bias == "batch":
            if transposed:
                return g.mask_k[:, bass.ts(b.no, 2 * S)]
            return g.mask_q[:, bass.ts(b.no, 2 * S)]
        return self.bias[1 if transposed else 0]

    def tensor(self, pe, ready):
        g, nc = self.g, self.g.nc
        ready()
        nqt = self.nqt

        def scores(b, u):
            if u % 4 == 0:
                pe.wait_ge(*self.m_in[b.par][u // 4].at((b.use + 1) * 32))
            if b.first is None or b.first * 8 + u >= 2:
                pe.wait_ge(*self.exp_done.at(b.no * 8 + u - 1))
            for hh in range(2):
                h = 2 * u + hh
                bank = g.bank[2 * (u % 2) + hh]
                if self.bias is not None:
                    nc.tensor.matmul(bank[:, 0:self.width], g.ident_bf[:, :],
                                     self.bias_for(b, True)[:, 0:self.width], start=True, stop=False)
                for kt in range(nqt):
                    lo, n = self.queries[kt]
                    last = nc.tensor.matmul(bank[:, self.offset[kt]:self.offset[kt] + n],
                                            g.K6[b.par][:, h, kt * P:(kt + 1) * P], g.Q6[b.par][:, h, lo:lo + n],
                                            start=self.bias is None, stop=self.bias is None or kt == nqt - 1)
            last.then_inc(self.st_ready.sem, 1)

        def maxima(b, pair, qt, v):
            if pair % 4 == 0 and qt == 0:
                pe.wait_ge(*self.feat[b.par][pair // 4].at((b.use + 1) * 16 * self.nfeat))
            if b.first is None or b.first * 8 * nqt + v >= 2:
                pe.wait_ge(*self.mx_done.at(b.no * (8 * nqt) + v - 1))
            kw = self.keys[qt]
            bank = g.bank[4 + v % 2][:, 0:2 * kw].rearrange("p (a k) -> p a k", a=2)
            if self.bias is not None:
                bias = self.bias_for(b, False)[:, qt * nqt * P:qt * nqt * P + kw]
                nc.tensor.matmul(bank, g.ident_bf[:, :], bias.unsqueeze(1).to_broadcast([P, 2, kw]), start=True, stop=False)
            for a in range(2):
                h = 2 * pair + a
                last = nc.tensor.matmul(bank[:, a, :], g.Q6[b.par][0:MROW, h, qt * P:(qt + 1) * P],
                                        g.K6[b.par][0:MROW, h, 0:kw], start=self.bias is None,
                                        stop=self.bias is None or a == 1)
            last.then_inc(self.mx_ready.sem, 1)

        def turn_m(b, half):
            pe.wait_ge(*self.mb_ready.at(b.no * 2 + half + 1))
            for qt in range(nqt):
                last = nc.tensor.transpose(g.aux_bf[0:16, qt * P:(qt + 1) * P], g.MB[half][:, qt, :], g.ident_bf[:, :])
            last.then_inc(self.mt_ready.sem, 1)

        def values(b, grp, kt):
            if kt == 0:
                if grp == 0:
                    pe.wait_ge(*self.va_ready.at(b.no + 1))
                pe.wait_ge(*self.exp_done.at(b.no * 8 + 2 * grp + 2))
                if b.first is None or b.first * 4 + grp >= 1:
                    pe.wait_ge(*self.ot_done.at(b.no * 4 + grp))
            lo, n = self.queries[kt]
            for hh in range(4):
                last = nc.tensor.matmul(
                    g.bank[6][PVW * hh:PVW * hh + PVW, lo:lo + n],
                    g.VA[b.par][:, kt, 4 * grp + hh, :],
                    g.PT[grp % 2][:, hh, self.offset[kt]:self.offset[kt] + n],
                    start=kt == 0, stop=kt == nqt - 1)
            if kt == nqt - 1:
                last.then_inc(self.pv_done.sem, 1)

        def turn_context(b, qt):
            pe.wait_ge(*self.ot_done.at(b.no * 4 + 4))
            for grp in range(4):
                last = nc.tensor.transpose(g.bank[7][:, grp * P:(grp + 1) * P], g.OT[b.par][:, grp, qt * P:(qt + 1) * P],
                                           g.ident[:, :])
            last.then_inc(self.cxt_ready.sem, 1)

        def step(j, i):
            bm, be, bc = self.batches(j, i)
            for grp in range(4):
                for slot in range(2 * nqt):
                    if bm:
                        maxima(bm, 2 * grp + slot // nqt, slot % nqt, grp * 2 * nqt + slot)
                    if be and slot % nqt == 0:
                        scores(be, 2 * grp + slot // nqt)
                    if slot % 2 == 1:
                        if be and grp >= 1:
                            values(be, grp - 1, slot // 2)
                        if bc and grp == 0:
                            values(bc, 3, slot // 2)
                    if slot == nqt:
                        if be and grp == 0:
                            if bc:
                                pe.wait_ge(*self.cx_done.at(bc.no * nqt))
                            pe.wait_ge(*self.mts_done.at(be.no * 2 + 1))
                            turn_m(be, 1)
                        if bm and grp == 2:
                            if bc:
                                pe.wait_ge(*self.cx_done.at(bc.no * nqt + 1))
                            if be:
                                pe.wait_ge(*self.mts_done.at(be.no * 2 + 2))
                            turn_m(bm, 0)
                if bc and grp % 2 == 1 and grp // 2 < nqt:
                    pe.wait_ge(*self.cx_done.at(bc.no * nqt + grp // 2))
                    if grp == 1 and be:
                        pe.wait_ge(*self.mts_done.at(be.no * 2 + 2))
                    if grp == 3 and bm:
                        pe.wait_ge(*self.mts_done.at(bm.no * 2 + 1))
                    turn_context(bc, grp // 2)
                if self.tail and i is None:
                    self.tail.run("tensor", pe, (j, grp))

        self.steps(pe, step, self.nb - 1)

    def scalar(self, act):
        g, nc = self.g, self.g.nc

        def evacuate(b, grp):
            act.wait_ge(*self.pv_done.at(b.no * 4 + grp + 1))
            if grp == 0 and (b.first is None or b.first >= 2):
                act.wait_ge(*self.cxt_ready.at((b.no - 1) * self.nqt))
            w = self.nqt * P
            nc.scalar.copy(g.OT[b.par][:, grp, 0:w], g.bank[6][:, 0:w])\
              .then_inc(self.ot_done.sem, 1)

        def m_rows(b, half):
            act.wait_ge(*self.mt_ready.at(b.no * 2 + half + 1))
            if b.first is None or b.first >= 1:
                act.wait_ge(*self.m_in[1 - b.par][half].at((b.use + b.par) * 32))
            w = self.nqt * P
            nc.scalar.copy(g.MT[half][:, 0:w], g.aux_bf[0:16, 0:w]).then_inc(self.mts_done.sem, 1)

        def step(j, i):
            bm, be, bc = self.batches(j, i)
            for grp in range(4):
                if bc and grp < 2:
                    evacuate(bc, 2 + grp)
                if be and grp >= 2:
                    evacuate(be, grp - 2)
                if be:
                    for u in (2 * grp, 2 * grp + 1):
                        act.wait_ge(*self.st_ready.at(be.no * 8 + u + 1))
                        if u % 2 == 0 and (be.first is None or be.first * 4 + grp >= 2):
                            act.wait_ge(*self.pv_done.at(be.no * 4 + grp - 1))
                        nc.scalar.activation(g.PT[grp % 2][:, 2 * (u % 2):2 * (u % 2) + 2, 0:self.width],
                                             g.bank2[u % 2][:, :, 0:self.width], ACT.Exp, scale=SCALE)\
                          .then_inc(self.exp_done.sem, 1)
                if be and grp == 0:
                    m_rows(be, 1)
                if bm and grp == 2:
                    m_rows(bm, 0)
                if self.tail and i is None:
                    self.tail.run("scalar", act, (j, grp))

        self.steps(act, step, self.nb - 1)

    def vector(self, dve):
        g, nc = self.g, self.g.nc
        nqt = self.nqt
        t = Tally(dve, self.chain)

        def parts_of_m(b, half):
            dve.wait_ge(*self.mx_done.at(b.no * 8 * nqt + (half + 1) * 4 * nqt))
            m = g.MS[:, 0:nqt, 8 * half:8 * half + 8]
            hi, lo = g.MB[half][:, 0:nqt, 0:8], g.MB[half][:, 0:nqt, 8:16]
            if b.first is None or b.first >= 1:
                dve.wait_ge(*self.mt_ready.at(b.no * 2 + half - 1))
            t.done(nc.vector.tensor_scalar(hi, m, -1.0, None, ALU.mult))
            nc.vector.scalar_tensor_tensor(lo, m, -1.0, hi, ALU.mult, ALU.subtract).then_inc(self.mb_ready.sem, 1)

        def context(b, qt):
            dve.wait_ge(*self.cxt_ready.at(b.no * nqt + qt + 1))
            sums = g.bank[7][:, :].rearrange("p (h w) -> p h w", w=PVW)
            t.done(nc.vector.reciprocal(g.rsum[:, :], sums[:, :, DH]))
            nc.vector.tensor_tensor(g.CX[:, bass.ds(b.no * nqt + qt, 1), :].rearrange("p o (d h) -> p (o h) d", d=DH),
                                    sums[:, :, 0:DH],
                                    g.rsum[:, :].unsqueeze(2).to_broadcast([P, H, DH]), ALU.mult)\
              .then_inc(self.cx_done.sem, 1)

        def step(j, i):
            bm, be, bc = self.batches(j, i)
            for grp in range(4):
                if bm:
                    for k in range(2 * nqt):
                        pair, qt, v = 2 * grp + k // nqt, k % nqt, grp * 2 * nqt + k
                        kw = self.keys[qt]
                        dve.wait_ge(*self.mx_ready.at(bm.no * (8 * nqt) + v + 1))
                        nc.vector.reduce_max(g.MS[:, qt, 2 * pair:2 * pair + 2],
                                             g.bank[4 + v % 2][:, 0:2 * kw].rearrange("p (a k) -> p a k", a=2),
                                             axis=AX_X).then_inc(self.mx_done.sem, 1)
                if bm and grp % 2 == 1:
                    parts_of_m(bm, grp // 2)
                if bc and grp % 2 == 1 and grp // 2 < nqt:
                    context(bc, grp // 2)
                if self.tail and i is None:
                    self.tail.run("vector", dve, (j, grp))

        body = self.steps
        per = 2 * (2 + nqt)

        def looped(j, i):
            if i is not None and j == 2:
                t.loop(i, per)
            step(j, i)
            if i is not None and j == 3:
                t.end((self.nb - 2) // 2)

        body(dve, looped, self.nb - 1)

    def gpsimd(self, pool, values, ready, bias=None):
        g, nc = self.g, self.g.nc
        nqt = self.nqt
        ready()

        def step(j, i):
            bm, _, _ = self.batches(j, i)
            if not bm:
                return
            if bm.first is None or bm.first >= 2:
                pool.wait_ge(*self.pv_done.at(bm.no * 4 - 4))
            to = g.VA[bm.par][:, 0:nqt, :, 0:DH]
            v = values[:, bass.ds(bm.no * nqt, nqt), :].rearrange("p t (d h) -> p t h d", d=DH)
            if bias is None:
                nc.gpsimd.tensor_copy(to, v).then_inc(self.va_ready.sem, 1)
            else:
                b = bias.rearrange("p (d h) -> p h d", d=DH)
                for t in range(nqt):
                    last = nc.gpsimd.tensor_tensor(to[:, t, :, :], v[:, t, :, :], b, ALU.add)
                last.then_inc(self.va_ready.sem, 1)

        self.steps(pool, step, self.nb - 1)

    def load(self, sp, b, half, rows, which="qkx"):
        g = self.g
        hs, w = slice(8 * half, 8 * half + 8), self.nqt * P
        q6, k6 = g.Q6[b.par], g.K6[b.par]
        for n, src in zip("qkx", rows):
            if n not in which:
                continue
            for first, k in {"q": [(0, ROWS)], "k": [(0, 3 * DH), (3 * DH, 2 * DH), (5 * DH, DH)],
                             "x": [(XROW, self.xrows)]}[n]:
                to = k6 if n == "k" else q6
                sp.dma_start(to[first:first + k, hs, 0:w], src[0:k, hs, bass.ts(b.no, w)])\
                  .then_inc(self.feat[b.par][half].sem, 16)

    def first_loads(self, sp, rows, which="qkx"):
        for c in range(2):
            for half in range(2):
                self.load(sp, Batch(c), half, rows, which)

    def sync(self, sp, rows):
        g = self.g
        w = self.nqt * P

        def m_rows(b, half):
            sp.wait_ge(*self.mts_done.at(b.no * 2 + half + 1))
            for part in range(2):
                sp.dma_start(g.Q6[b.par][MROW + part:MROW + part + 1, 8 * half:8 * half + 8, 0:w],
                             g.MT[half][8 * part:8 * part + 8, 0:w]).then_inc(self.m_in[b.par][half].sem, 16)

        def step(j, i):
            bm, be, _ = self.batches(j, i)
            more = i is not None or j + 1 < self.nb
            for half in range(2):
                if be and half == 0:
                    m_rows(be, 1)
                if bm and half == 1:
                    m_rows(bm, 0)
                if more and be:
                    sp.wait_ge(*self.st_ready.at(be.no * 8 + 4 * half + 4))
                    self.load(sp, Batch(j + 1, i), half, rows)

        self.steps(sp, step, self.nb - 3)


def rsqrt(g, t, out, v, scratch, n):
    nc = g.nc
    out, v, sq = out[:, 0:n], v[:, 0:n], scratch[:, 0:n]
    t.done(nc.vector.tensor_scalar(out.bitcast(I32), v.bitcast(I32), -0.5, float(0x5F3759DF), ALU.mult, ALU.add))
    for _ in range(3):
        t.done(nc.vector.scalar_tensor_tensor(sq, out, -0.5, out, ALU.mult, ALU.mult))
        t.done(nc.vector.tensor_tensor(sq, sq, v, ALU.mult))
        t.done(nc.vector.scalar_tensor_tensor(out, sq, 1.5, out, ALU.add, ALU.mult))


def moments(g, t, tiles, rstd):
    nc = g.nc
    n = len(tiles)
    for i in range(n):
        last = nc.vector.bn_stats(g.stats[:, i, :], tiles[i])
    t.done(last)
    for i in range(n):
        last = nc.vector.bn_aggr(g.meanvar[:, i, :], g.stats[:, i, :])
    t.done(last)
    t.done(nc.vector.tensor_scalar(g.var[:, 0:n], g.meanvar[:, 0:n, 1], EPS, None, ALU.add))
    rsqrt(g, t, rstd, g.var, g.square, n)


def layernorm(g, t, y, out):
    moments(g, t, [y[:, i, :] for i in range(y.shape[1])], g.rstd)
    for i in range(y.shape[1]):
        last = g.nc.vector.tensor_scalar(out[:, i, :], y[:, i, :], g.meanvar[:, i, 0:1], g.rstd[:, i:i + 1],
                                         ALU.subtract, ALU.mult)
    return last


MOMENTS_CHAIN = 3 + 10


class Post:

    PLACES = {(0, 0): "T0 C0", (0, 1): "P0 T1 C1", (0, 2): "A0 P1 T2 C2", (0, 3): "A1 P2 M0", (1, 0): "A2", (1, 3): "N0 N1",
              "after": "T3 C3 R0 P3 Q0 A3 R1 Q1 G0 G1 M1 I N2 R2 N3 Q2 I R3 Q3 G2 G3 I I"}
    PLACES_SCATTER = {"after": "S0 S1 S2 A0 A1 M0 S3 A2 A3 M1 N0 R0 N1 Q0 R1 Q1 I N2 R2 N3 Q2 I R3 Q3 I I"}
    WHERE = {"tensor": "STPRG", "scalar": "CNQ", "vector": "AM"}

    def __init__(self, g, name, core, w=None, bias=False, scatter=None, add=None, logits=None):
        self.g, self.w, self.core, self.scatter, self.logits = g, w, core, scatter, logits
        self.places = self.PLACES_SCATTER if scatter else self.PLACES
        if logits:
            self.places = self.PLACES | {"after": self.PLACES["after"].replace("M1 I", "I M1")}
        if add:
            self.add = add
        if core:
            core.tail = self
        n = NC if w is not None else 0
        self.turned = g.shared_sem("post_turned", n)
        self.ct_ready = g.shared_sem("post_ct_ready", n)
        self.projected = g.shared_sem("post_projected", n)
        self.added = g.shared_sem("post_added", NC)
        self.moments = g.shared_sem("post_moments", NC // 2)
        self.normed = g.shared_sem("post_normed", NC)
        self.xt_turned = g.shared_sem("post_xt_turned", NC)
        self.xt_ready = g.shared_sem("post_xt_ready", NC)
        self.chain = g.shared_sem("post_chain", NC // 2 * MOMENTS_CHAIN)
        self.biased = g.sem(f"{name}_biased")
        self.bias = bias
        self.tally = None
        self.Y = [y[:, :].rearrange("p (t d) -> p t d", t=TC) for y in (*g.turn, *g.fbuf)]

    def run(self, kind, eng, place, between=iter(())):
        if place != "after":
            place = (place[0] - self.core.nb, place[1])
        pieces = {"T": self.turn, "C": self.copy, "P": self.project, "A": self.add,
                  "M": self.take_moments, "N": self.norm, "R": self.turn_x,
                  "Q": self.copy_x, "S": self.scatter, "G": self.logits}
        for piece in self.places.get(place, "").split():
            if piece == "I":
                next(between, None)
            elif piece[0] in self.WHERE[kind] and not (piece[0] in "TCP" and self.w is None or
                                                       piece[0] == "G" and not self.logits):
                pieces[piece[0]](eng, int(piece[1]))
        for _ in between:
            pass

    def add_bias(self, pool, bias):
        g, nc = self.g, self.g.nc
        for c in range(NC):
            x = g.X[:, c * TC:(c + 1) * TC, :]
            last = nc.gpsimd.tensor_tensor(x, x, bias.unsqueeze(1).to_broadcast([P, TC, D]), ALU.add)
        last.then_inc(self.biased.sem, 1)

    def turn(self, pe, c):
        g, nc = self.g, self.g.nc
        pe.wait_ge(*self.core.cx_done.at((c + 1) * TC))
        if c == 0:
            pe.wait_ge(*self.core.mx_done.at(NT * H // 2))
        else:
            pe.wait_ge(*self.ct_ready.at(c))
        for t in range(TC):
            last = nc.tensor.transpose(g.bank[4][:, t * P:(t + 1) * P], g.CX[:, c * TC + t, :], g.ident[:, :])
        last.then_inc(self.turned.sem, 1)

    def copy(self, act, c):
        g, nc = self.g, self.g.nc
        act.wait_ge(*self.turned.at(c + 1))
        if c >= 2:
            act.wait_ge(*self.projected.at(c - 1))
        nc.scalar.copy(g.CXT[:, c % 2, :], g.bank[4][:, :]).then_inc(self.ct_ready.sem, 1)

    def project(self, pe, c):
        g, nc = self.g, self.g.nc
        pe.wait_ge(*self.ct_ready.at(c + 1))
        if c >= 1:
            pe.wait_ge(*self.added.at(c))
        for t in range(TC):
            last = nc.tensor.matmul(g.bank[5][:, t * P:(t + 1) * P], g.CXT[:, c % 2, t * P:(t + 1) * P], self.w,
                                    start=True, stop=True)
        last.then_inc(self.projected.sem, 1)

    def add(self, dve, c):
        g, nc = self.g, self.g.nc
        if self.bias and c == 0:
            dve.wait_ge(*self.biased.at(1))
        if self.w is not None:
            dve.wait_ge(*self.projected.at(c + 1))
            more = g.bank[5][:, :].rearrange("p (t d) -> p t d", t=TC)
        else:
            dve.wait_ge(*self.core.cx_done.at((c + 1) * TC))
            more = g.CX[:, c * TC:(c + 1) * TC, :]
        nc.vector.tensor_tensor(self.Y[c], more, g.X[:, c * TC:(c + 1) * TC, :], ALU.add).then_inc(self.added.sem, 1)

    def take_moments(self, dve, k):
        g, nc = self.g, self.g.nc
        self.tally = t = self.tally or Tally(dve, self.chain)
        dve.wait_ge(*self.added.at(2 * k + 2))
        moments(g, t, [self.Y[c][:, i, :] for c in (2 * k, 2 * k + 1) for i in range(TC)], g.scale[k])
        nc.vector.scalar_tensor_tensor(g.offset[k][:, :], g.meanvar[:, :, 0], -1.0, g.scale[k][:, :], ALU.mult, ALU.mult)\
          .then_inc(self.moments.sem, 1)

    def norm(self, act, c):
        g, nc = self.g, self.g.nc
        act.wait_ge(*self.moments.at(c // 2 + 1))
        for i in range(TC):
            n = c % 2 * TC + i
            last = nc.scalar.activation(g.X[:, c * TC + i, :], self.Y[c][:, i, :], ACT.Identity,
                                        scale=g.scale[c // 2][:, n:n + 1], bias=g.offset[c // 2][:, n:n + 1])
        last.then_inc(self.normed.sem, 1)

    def turn_x(self, pe, c):
        g, nc = self.g, self.g.nc
        pe.wait_ge(*self.normed.at(c + 1))
        if c == 0 and self.core:
            pe.wait_ge(*self.core.cx_done.at(NT))
        if c >= 1:
            pe.wait_ge(*self.xt_ready.at(c))
        for i in range(TC):
            last = nc.tensor.transpose(g.bank[7][:, i * P:(i + 1) * P], g.X[:, c * TC + i, :], g.ident[:, :])
        last.then_inc(self.xt_turned.sem, 1)

    def copy_x(self, act, c):
        g, nc = self.g, self.g.nc
        act.wait_ge(*self.xt_turned.at(c + 1))
        nc.scalar.copy(g.XT[:, c * CH:(c + 1) * CH], g.bank[7][:, :]).then_inc(self.xt_ready.sem, 1)




class Depths:

    NP = B // 2
    FC = [(0, P), (P, P), (2 * P, F0 - 2 * P)]

    def __init__(self, g, name):
        self.g = g
        self.scored = g.sem(f"{name}_scored")
        self.ranked = g.sem(f"{name}_ranked")
        self.gathered = g.sem(f"{name}_gathered")
        self.taken = g.sem(f"{name}_taken")
        self.hidden = g.sem(f"{name}_hidden")
        self.h_turned = g.sem(f"{name}_h_turned")
        self.h_ready = g.sem(f"{name}_h_ready")
        self.g_turned = g.sem(f"{name}_g_turned")
        self.g_ready = g.sem(f"{name}_g_ready")
        self.cx_turned = g.sem(f"{name}_cx_turned")
        self.cx_ready = g.sem(f"{name}_cx_ready")
        self.attended = g.sem(f"{name}_attended")
        self.added = g.sem(f"{name}_added")
        self.h2 = g.sem(f"{name}_h2")
        self.h2_turned = g.sem(f"{name}_h2_turned")
        self.h2_ready = g.sem(f"{name}_h2_ready")
        self.gate_up = g.sem(f"{name}_gate_up")
        self.tanh = g.sem(f"{name}_tanh")
        self.mixed = g.sem(f"{name}_mixed")
        self.down = g.sem(f"{name}_down")
        self.delta = g.sem(f"{name}_delta")
        self.scattered = g.sem(f"{name}_scattered")
        self.chain = g.sem(f"{name}_chain")
        self.post = Post(g, name, None, scatter=self.scatter, add=self.add)
        sb = g.sb
        self.scol = sb("scol", [P, NT])
        self.above = sb("above", [P, NT])
        self.ties = sb("ties", [P, NT])
        self.rank = sb("rank", [P, NT])
        free = [buf[:, :, :].rearrange("p a b -> p (a b)") for buf in g.PT]
        self.G = free[0][:, 0:2 * B * SEL].rearrange("p (k b r) -> p k b r", k=2, b=B)
        self.GT = sb("GT", [P, self.NP, 2, P])
        self.XS = sb("XS", [P, self.NP, D])
        self.X1 = sb("X1", [P, self.NP, D])
        self.XA = sb("XA", [P, self.NP, D])
        self.HN = sb("HN", [P, self.NP, D])
        self.HT = sb("HT", [P, CH])
        self.U = g.PT[0][:, 0:3, :]
        self.TH = g.PT[1][:, 0:3, :]
        self.ss = sb("ss", [P, self.NP])


    def select_tensor(self, pe, ready, keys):
        g, nc = self.g, self.g.nc
        for c in range(NC):
            ready(c)
            nc.tensor.matmul(g.bank[c][:, :], g.router[:, :], g.XT[:, c * CH:(c + 1) * CH], start=True, stop=True)\
              .then_inc(self.scored.sem, 1)
        keys.tensor(pe, lambda c: None)
        pe.wait_ge(*self.ranked.at(1))
        pe.wait_ge(*keys.v_ready.at(NC))
        pe.wait_ge(*keys.r1_ready.at(NC))
        for p in range(self.NP):
            for half in range(2):
                b = 2 * p + half
                for k in range(2):
                    last = nc.tensor.matmul(g.bank[4][SEL * half:SEL * half + SEL, p * D:(p + 1) * D],
                                            self.G[:, k, b, :], g.X[:, 2 * b + k, :], start=k == 0, stop=k == 1)
        last.then_inc(self.gathered.sem, 1)
        for p in range(self.NP):
            for k in range(2):
                n = 2 * p + k
                last = nc.tensor.transpose(g.bank[n // 4][:, (n % 4) * P:(n % 4 + 1) * P],
                                           self.G[:, k, 2 * p:2 * p + 2, :].rearrange("p b r -> p (b r)"), g.ident[:, :])
        last.then_inc(self.g_turned.sem, 1)
        pe.wait_ge(*self.hidden.at(1))
        for p in range(self.NP):
            last = nc.tensor.transpose(g.bank[5][:, p * P:(p + 1) * P], self.HN[:, p, :], g.ident[:, :])
        last.then_inc(self.h_turned.sem, 1)

    def select_scalar(self, act):
        g, nc = self.g, self.g.nc
        act.wait_ge(*self.gathered.at(1))
        nc.scalar.copy(self.XS[:, :, :], g.bank[4][:, :].rearrange("p (n d) -> p n d", d=D)).then_inc(self.taken.sem, 1)
        act.wait_ge(*self.g_turned.at(1))
        for n in range(2):
            last = nc.scalar.copy(self.GT[:, 2 * n:2 * n + 2, :, :],
                                  g.bank[n][:, :].rearrange("p (a k t) -> p a k t", a=2, k=2))
        last.then_inc(self.g_ready.sem, 1)
        act.wait_ge(*self.h_turned.at(1))
        nc.scalar.mul(self.HT[:, :], g.bank[5][:, :], g.col("f0_g1")).then_inc(self.h_ready.sem, 1)

    def rms(self, t, x, out):
        g, nc = self.g, self.g.nc
        for p in range(self.NP):
            last = nc.vector.scalar_tensor_tensor(self.junk2[:, p, :], x[:, p, :], 1.0, x[:, p, :], ALU.mult, ALU.mult,
                                                  accum_out=self.ss[:, p:p + 1])
        t.done(last)
        t.done(nc.vector.tensor_scalar(g.var[:, 0:self.NP], self.ss[:, :], 1.0 / D, 1e-6, ALU.mult, ALU.add))
        rsqrt(g, t, g.rstd, g.var, g.square, self.NP)
        for p in range(self.NP):
            last = nc.vector.tensor_scalar(out[:, p, :], x[:, p, :], g.rstd[:, p:p + 1], None, ALU.mult)
        return last

    def select_vector(self, dve, keys):
        g, nc = self.g, self.g.nc
        t = self.t = Tally(dve, self.chain)
        self.junk2 = g.Y
        junk_own = g.CX
        halves = [g.V[:, :, :].rearrange("p a b -> p (a b)"), g.PT[1].rearrange("p a b -> p (a b)")]
        junk = lambda n: halves[n // 8][:, n % 8 * S:(n % 8 + 1) * S]
        row = lambda n: g.bank[n // TC][:, n % TC // 2 * S:(n % TC // 2 + 1) * S]
        for c in range(NC):
            dve.wait_ge(*self.scored.at(c + 1))
            for n in range(c * TC, (c + 1) * TC):
                last = nc.vector.scalar_tensor_tensor(junk_own[:, n, :], row(n)[:, n % 2 * P:(n % 2 + 1) * P], 1.0,
                                                      g.ident[:, :], ALU.mult, ALU.mult, accum_out=self.scol[:, n:n + 1])
        t.done(last)
        for n in range(NT):
            last = nc.vector.tensor_scalar(junk(n), row(n), self.scol[:, n:n + 1], None, ALU.is_gt, ALU.add,
                                           accum_out=self.above[:, n:n + 1])
        t.done(last)
        steps = keys.vector_steps(dve)
        next(steps)
        next(steps)
        next(steps)
        for n in range(NT):
            last = nc.vector.scalar_tensor_tensor(junk(n), row(n), self.scol[:, n:n + 1], g.earlier[:, n % 2, :],
                                                  ALU.is_equal, ALU.mult, accum_out=self.ties[:, n:n + 1])
        t.done(last)
        for _ in steps:
            pass
        t.done(nc.vector.tensor_tensor(self.rank[:, :], self.above[:, :], self.ties[:, :], ALU.add))
        rank = self.rank[:, :].rearrange("p (b k) -> p k b", k=2).unsqueeze(3)
        for k in range(2):
            last = nc.vector.tensor_tensor(self.G[:, k, :, :], g.iota[:, 0:SEL].unsqueeze(1).to_broadcast([P, B, SEL]),
                                           rank[:, k, :, :].to_broadcast([P, B, SEL]), ALU.is_equal)
        last.then_inc(self.ranked.sem, 1)
        dve.wait_ge(*self.taken.at(1))
        self.rms(t, self.XS, self.HN).then_inc(self.hidden.sem, 1)


    def feed_tensor(self, pe, ready, between):
        g, nc = self.g, self.g.nc
        ready()
        for p in range(self.NP):
            last = nc.tensor.transpose(g.bank[5][:, p * P:(p + 1) * P], g.CX[:, p, :], g.ident[:, :])
        last.then_inc(self.cx_turned.sem, 1)
        pe.wait_ge(*self.cx_ready.at(1))
        for p in range(self.NP):
            last = nc.tensor.matmul(g.bank[6][:, p * P:(p + 1) * P], g.CXT[:, 0, p * P:(p + 1) * P], g.w("f0_o"),
                                    start=True, stop=True)
        last.then_inc(self.attended.sem, 1)
        pe.wait_ge(*self.h2.at(1))
        for p in range(self.NP):
            last = nc.tensor.transpose(g.bank[7][:, p * P:(p + 1) * P], self.HN[:, p, :], g.ident[:, :])
        last.then_inc(self.h2_turned.sem, 1)
        pe.wait_ge(*self.h2_ready.at(1))
        for n, (lo, w) in enumerate(self.FC):
            for m in range(2):
                last = nc.tensor.matmul(g.bank[2 * n + m][0:w, :], g.f0_w12[:, m, lo:lo + w], self.HT[:, :],
                                        start=True, stop=True)
            last.then_inc(self.gate_up.sem, 1)
        pe.wait_ge(*self.mixed.at(3))
        for p in range(self.NP):
            for n, (lo, w) in enumerate(self.FC):
                last = nc.tensor.matmul(g.bank[6][:, p * P:(p + 1) * P], self.U[0:w, n, p * P:(p + 1) * P],
                                        g.f0_w3[0:w, n, :], start=n == 0, stop=n == 2)
        last.then_inc(self.down.sem, 1)
        pe.wait_ge(*self.delta.at(1))

        self.post.run("tensor", pe, "after", between)

    def scatter(self, pe, c):
        g, nc = self.g, self.g.nc
        if c == 0:
            pe.wait_ge(*self.delta.at(1))
        if c >= 3:
            pe.wait_ge(*self.post.added.at(c - 2))
        for half in range(2):
            rows = slice(SEL * half, SEL * half + SEL)
            for k in range(2):
                last = nc.tensor.matmul(self.bank_of(c, half)[:, k * P:(k + 1) * P], self.GT[rows, c, k, :],
                                        self.X1[rows, c, :], start=True, stop=True)
        last.then_inc(self.scattered.sem, 1)

    def bank_of(self, c, half):
        return self.g.bank[2 * (c % 3) + half]

    def add(self, dve, c):
        g, nc = self.g, self.g.nc
        dve.wait_ge(*self.scattered.at(c + 1))
        for half in range(2):
            two = slice(2 * half, 2 * half + 2)
            last = nc.vector.scalar_tensor_tensor(self.post.Y[c][:, two, :], g.X[:, c * TC + 2 * half:c * TC + 2 * half + 2, :],
                                                  2.0, self.bank_of(c, half)[:, 0:2 * P].rearrange("p (n d) -> p n d", d=D),
                                                  ALU.mult, ALU.add)
        last.then_inc(self.post.added.sem, 1)

    def feed_scalar(self, act, between):
        g, nc = self.g, self.g.nc
        act.wait_ge(*self.cx_turned.at(1))
        nc.scalar.copy(g.CXT[:, 0, :], g.bank[5][:, :]).then_inc(self.cx_ready.sem, 1)
        act.wait_ge(*self.h2_turned.at(1))
        nc.scalar.mul(self.HT[:, :], g.bank[7][:, :], g.col("f0_g2")).then_inc(self.h2_ready.sem, 1)
        for n, (lo, w) in enumerate(self.FC):
            act.wait_ge(*self.gate_up.at(n + 1))
            nc.scalar.activation(self.TH[0:w, n, :], g.bank[2 * n][0:w, :], ACT.Tanh, scale=0.5).then_inc(self.tanh.sem, 1)
        self.post.run("scalar", act, "after", between)

    def feed_vector(self, dve, between):
        g, nc = self.g, self.g.nc
        t = self.t
        tiles = lambda bank: bank[:, :].rearrange("p (n d) -> p n d", d=D)
        dve.wait_ge(*self.attended.at(1))
        t.done(nc.vector.tensor_copy(self.XA[:, :, :], tiles(g.bank[6])))
        t.done(nc.vector.tensor_tensor(self.X1[:, :, :], self.XA[:, :, :], self.XS[:, :, :], ALU.add))
        self.rms(t, self.X1, self.HN).then_inc(self.h2.sem, 1)
        for n, (lo, w) in enumerate(self.FC):
            dve.wait_ge(*self.tanh.at(n + 1))
            t.done(nc.vector.scalar_tensor_tensor(self.TH[0:w, n, :], self.TH[0:w, n, :], 1.0, g.bank[2 * n][0:w, :],
                                                  ALU.add, ALU.mult))
            nc.vector.scalar_tensor_tensor(self.U[0:w, n, :], self.TH[0:w, n, :], 0.5, g.bank[2 * n + 1][0:w, :],
                                           ALU.mult, ALU.mult).then_inc(self.mixed.sem, 1)
        dve.wait_ge(*self.down.at(1))
        nc.vector.tensor_tensor(self.X1[:, :, :], tiles(g.bank[6]), self.XA[:, :, :], ALU.add).then_inc(self.delta.sem, 1)
        self.post.run("vector", dve, "after", between)


class Gauss:

    def __init__(self, g, name):
        self.g = g
        self.summed = g.sem(f"{name}_summed")
        self.global_ = g.sem(f"{name}_global_")
        self.bias = g.sem(f"{name}_bias")
        self.c_in = g.sem(f"{name}_c_in")
        self.c_ready = g.sem(f"{name}_c_ready")
        self.pz = g.sem(f"{name}_pz")
        self.acted = g.sem(f"{name}_acted")
        self.rows_ready = g.sem(f"{name}_rows_ready")
        self.turned = g.sem(f"{name}_turned")
        self.copied = g.sem(f"{name}_copied")
        self.written = g.sem(f"{name}_written")
        self.chain = g.sem(f"{name}_chain")
        sb = g.sb
        self.glo = sb("glo", [P, B])
        self.cbias = sb("cbias", [P, B])
        self.MQ = g.CX[:, :, :].rearrange("p n d -> p (n d)")
        self.C = g.CXT
        free = g.PT[1][:, :, :].rearrange("p a b -> p (a b)")
        n = NT * H
        tiles = lambda ap: ap.rearrange("p (n h) -> p n h", h=H)
        self.ez, self.tp = tiles(free[:, 0:n]), tiles(free[:, n:2 * n])
        self.AB = free[:, 2 * n:4 * n].rearrange("p (a n h) -> p a n h", a=2, h=H)
        self.rem = free[:, 4 * n:6 * n].rearrange("p (a n h) -> p a n h", a=2, h=H)
        self.XR = g.PT[0][:, :, :].rearrange("p a b -> p (a b)").bitcast(BF16)[:, 0:6 * n]\
                   .rearrange("p (n r h) -> p n r h", n=NT, h=H)
        self.AR = g.OT[0][:, :, :].rearrange("p a b -> p (a b)").bitcast(BF16)[0:6 * H, :]

    def tensor(self, pe):
        g, nc = self.g, self.g.nc
        pe.wait_ge(*self.summed.at(NC))
        nc.tensor.matmul(g.bank[5][:, 0:B], g.w("a1_fg"), self.glo[:, :], start=True, stop=True).then_inc(self.global_.sem, 1)

        def c_in(c):
            if c == 1:
                pe.wait_ge(*self.bias.at(1))
            if c >= 2:
                pe.wait_ge(*self.c_ready.at(c - 1))
            nc.tensor.matmul(g.bank[6 - c % 2][:, :], g.w("a1_fq"), self.MQ[:, c * CH:(c + 1) * CH], start=True, stop=True)\
              .then_inc(self.c_in.sem, 1)

        c_in(0)
        for c in range(NC):
            if c + 1 < NC:
                c_in(c + 1)
            pe.wait_ge(*self.c_ready.at(c + 1))
            for t in range(TC):
                n = c * TC + t
                last = nc.tensor.matmul(g.bank[7][:, n * 2 * H:(n + 1) * 2 * H], self.C[:, c % 2, t * P:(t + 1) * P],
                                        g.upz[:, :], start=True, stop=True)
            last.then_inc(self.pz.sem, 1)
        pe.wait_ge(*self.rows_ready.at(2))
        for n in range(NT):
            bank = g.bank[5 + n // 8].bitcast(BF16)
            last = nc.tensor.transpose(bank[0:6 * H, (n % 8) * P:(n % 8 + 1) * P],
                                       self.XR[:, n, :, :].rearrange("p r h -> p (r h)"), g.ident_bf[:, :])
            if n % 8 == 7:
                last.then_inc(self.turned.sem, 1)

    def scalar(self, act):
        g, nc = self.g, self.g.nc
        for c in range(NC):
            act.wait_ge(*self.c_in.at(c + 1))
            act.wait_ge(*self.bias.at(1))
            if c >= 2:
                act.wait_ge(*self.pz.at(c - 1))
            for k in range(2):
                b = 2 * c + k
                last = nc.scalar.activation(self.C[:, c % 2, k * S:(k + 1) * S], g.bank[6 - c % 2][:, k * S:(k + 1) * S], ACT.Tanh,
                                            bias=self.cbias[:, b:b + 1])
            last.then_inc(self.c_ready.sem, 1)
        act.wait_ge(*self.pz.at(NC))
        pz = g.bank[7][:, :].rearrange("p (n a h) -> p n a h", a=2, h=H)
        nc.scalar.activation(self.tp[:, :, :], pz[:, :, 0, :], ACT.Tanh, scale=0.5)
        nc.scalar.activation(self.ez[:, :, :], pz[:, :, 1, :], ACT.Exp, scale=-1.0).then_inc(self.acted.sem, 1)
        for n in range(2):
            act.wait_ge(*self.turned.at(n + 1))
            nc.scalar.copy(self.AR[:, n * 8 * P:(n + 1) * 8 * P], g.bank[5 + n].bitcast(BF16)[0:6 * H, :])\
              .then_inc(self.copied.sem, 1)

    def sums(self, dve, c, kept):
        dve.wait_ge(*kept.at(c + 1))
        n = CH // S
        self.g.nc.vector.reduce_sum(self.glo[:, c * n:(c + 1) * n],
                                    self.MQ[:, c * CH:(c + 1) * CH].rearrange("p (b s) -> p b s", s=S), axis=AX_X)\
            .then_inc(self.summed.sem, 1)

    def vector(self, dve):
        g, nc = self.g, self.g.nc
        t = Tally(dve, self.chain)
        dve.wait_ge(*self.global_.at(1))
        t.done(nc.vector.tensor_scalar(self.cbias[:, :], g.bank[5][:, 0:B], 1.0 / S, g.col("a1_bfq"), ALU.mult, ALU.add))
        nc.vector.tensor_scalar(self.cbias[:, :], self.cbias[:, :], g.col("a1_bfg"), None, ALU.add).then_inc(self.bias.sem, 1)
        dve.wait_ge(*self.acted.at(1))
        ab, a, b = self.AB, self.AB[:, 0, :, :], self.AB[:, 1, :, :]
        t.done(nc.vector.tensor_scalar(self.ez[:, :, :], self.ez[:, :, :], 1.0, None, ALU.add))
        t.done(nc.vector.scalar_tensor_tensor(a, self.ez[:, :, :], -2.0 / (S * S * SCALE), self.ez[:, :, :],
                                              ALU.mult, ALU.mult))
        t.done(nc.vector.scalar_tensor_tensor(b, a, -float(S), self.tp[:, :, :], ALU.mult, ALU.mult))
        for part in range(3):
            src = ab if part == 0 else self.rem
            for m in range(2):
                last = nc.vector.tensor_copy(self.XR[:, :, 3 * m + part, :], src[:, m, :, :])
            if part == 2:
                last.then_inc(self.rows_ready.sem, 2)
                break
            t.done(last)
            for m in range(2):
                last = nc.vector.tensor_tensor(self.rem[:, m, :, :], src[:, m, :, :], self.XR[:, :, 3 * m + part, :],
                                               ALU.subtract)
            t.done(last)

    def sync(self, sp, rows):
        sp.wait_ge(*self.copied.at(2))
        for first, part in ((0, 0), (3, 0), (6, 1)):
            sp.dma_start(rows[first:first + 3, :, :].rearrange("r h t -> (r h) t"),
                         self.AR[3 * H * part:3 * H * part + 3 * H, :]).then_inc(self.written.sem, 16)


class Mask:

    def __init__(self, g):
        self.g = g
        self.loaded, self.made, self.turned, self.copied = (g.sem(f"mask_{w}") for w in ("loaded", "made", "turned", "copied"))

    def sync(self, sp):
        g = self.g
        for i in range(2):
            sp.dma_start(g.PT[i][:, :, :].rearrange("p a b -> p (a b)").bitcast(I32).rearrange("p (n k) -> p n k", k=S),
                         g.io["mask"].rearrange("(n p) k -> p n k", p=P)[:, 8 * i:8 * i + 8, :]).then_inc(self.loaded.sem, 16)

    def vector(self, dve):
        g, nc = self.g, self.g.nc
        dve.wait_ge(*self.loaded.at(32))
        for i in range(2):
            nc.vector.tensor_scalar(g.mask_q[:, i * 8 * S:(i + 1) * 8 * S],
                                    g.PT[i][:, :, :].rearrange("p a b -> p (a b)").bitcast(I32), 0.0, NEG_MASK,
                                    ALU.is_equal, ALU.mult).then_inc(self.made.sem, 1)

    def tensor(self, pe):
        g, nc = self.g, self.g.nc
        for i in range(4):
            pe.wait_ge(*self.made.at(i // 2 + 1))
            bank = g.bank[4 + i].bitcast(BF16)
            for n in range(8):
                b, kt, qt = 2 * i + n // 4, n // 2 % 2, n % 2
                last = nc.tensor.transpose(bank[:, n * P:(n + 1) * P],
                                           g.mask_q[:, b * 2 * S + qt * S + kt * P:b * 2 * S + qt * S + kt * P + P],
                                           g.ident_bf[:, :])
            last.then_inc(self.turned.sem, 1)

    def scalar(self, act):
        g, nc = self.g, self.g.nc
        for i in range(4):
            act.wait_ge(*self.turned.at(i + 1))
            nc.scalar.copy(g.mask_k[:, i * 4 * S:(i + 1) * 4 * S], g.bank[4 + i].bitcast(BF16)).then_inc(self.copied.sem, 1)


class Router:

    NH = NT // 2

    def __init__(self, g):
        self.g = g
        self.logits = g.sem("router_logits")
        self.chain = g.sem("router_chain")
        self.gap = g.sem("router_gap")
        self.gap_exp = g.sem("router_gap_exp")
        self.routed = g.sem("router_routed")
        sb = g.sb
        self.L = sb("router_L", [P, NT, EX])
        self.W1 = sb("router_W1", [P, NT, EX])
        self.W2 = sb("router_W2", [P, NT, EX])
        self.first = sb("router_first", [P, NT, EX])
        self.second = sb("router_second", [P, NT, EX])
        self.m1, self.m2, self.d = (sb(f"router_{n}", [P, NT]) for n in ("m1", "m2", "d"))
        self.gate = sb("router_gate", [P, 2, NT])

    def chunk(self, pe, c):
        g, nc = self.g, self.g.nc
        pe.wait_ge(*self.stream.xt_ready.at(c + 1))
        half, first = divmod(c, NC // 2)
        for n in range(TC):
            t = c * TC + n
            last = nc.tensor.matmul(self.bank(half)[:, first * TC + n, :], g.XT[:, t * P:(t + 1) * P], g.router_w[:, :],
                                    start=True, stop=True)
        if first == NC // 2 - 1:
            last.then_inc(self.logits.sem, 1)

    def bank(self, half):
        return self.g.bank[3 * half][:, 0:self.NH * EX].rearrange("p (n e) -> p n e", e=EX)

    def half(self, ap, half):
        return ap[:, half * self.NH:(half + 1) * self.NH]

    def scalar(self, act):
        g, nc = self.g, self.g.nc
        act.wait_ge(*self.gap.at(2))
        nc.scalar.activation(self.d[:, :], self.d[:, :], ACT.Exp).then_inc(self.gap_exp.sem, 1)

    def vector(self, dve, half):
        g, nc = self.g, self.g.nc
        if half == 0:
            self.tally = Tally(dve, self.chain)
        t = self.tally
        wide = lambda ap: ap.unsqueeze(2).to_broadcast([P, self.NH, EX])
        rows = lambda ap: ap.unsqueeze(1).to_broadcast([P, self.NH, EX])
        L, W1, W2, d, first, second = (self.half(ap, half) for ap in (self.L, self.W1, self.W2, self.d, self.first, self.second))
        dve.wait_ge(*self.logits.at(half + 1))
        t.done(nc.vector.tensor_tensor(L, self.bank(half), rows(g.router_b[:, :]), ALU.add))
        for m, out in ((self.half(self.m1, half), first), (self.half(self.m2, half), second)):
            t.done(nc.vector.reduce_max(m, L, axis=AX_X))
            t.done(nc.vector.tensor_tensor(W1, L, wide(m), ALU.is_equal))
            t.done(nc.vector.tensor_tensor(W1, W1, rows(g.descending[:, :]), ALU.mult))
            t.done(nc.vector.reduce_max(d, W1, axis=AX_X))
            t.done(nc.vector.tensor_tensor(out, W1, wide(d), ALU.is_equal))
            if out is first:
                t.done(nc.vector.tensor_scalar(W2, first, -1e30, None, ALU.mult))
                t.done(nc.vector.tensor_tensor(L, L, W2, ALU.add))
        nc.vector.tensor_tensor(d, self.half(self.m2, half), self.half(self.m1, half), ALU.subtract).then_inc(self.gap.sem, 1)

    def weigh(self, dve):
        nc, t = self.g.nc, self.tally
        dve.wait_ge(*self.gap_exp.at(1))
        t.done(nc.vector.tensor_scalar(self.m1[:, :], self.d[:, :], 1.0, None, ALU.add))
        t.done(nc.vector.reciprocal(self.gate[:, 0, :], self.m1[:, :]))
        nc.vector.tensor_tensor(self.gate[:, 1, :], self.d[:, :], self.gate[:, 0, :], ALU.mult)\
          .then_inc(self.routed.sem, 1)


class Experts:

    HB = T // P - 1 + EX
    BLOCKS = 2 * HB
    FT = FE // P

    def __init__(self, g, router, xs, ys):
        self.g, self.router, self.xs, self.ys = g, router, xs, ys
        self.chosen = g.sem("experts_chosen")
        self.counted = g.sem("experts_counted")
        self.chain = g.sem("experts_chain")
        self.positions = g.sem("experts_positions")
        self.result_rows = g.sem("experts_result_rows")
        self.table = g.sem("experts_table")
        self.filled = g.sem("experts_filled")
        self.scattered = [g.sem(f"experts_scattered{i}") for i in range(2)]
        self.weights_in = g.sem("experts_weights_in")
        self.x_in = [g.sem(f"experts_x_in{i}") for i in range(2)]
        self.turned = g.sem("experts_turned")
        self.xt_ready = g.sem("experts_xt_ready")
        self.gate = g.sem("experts_gate")
        self.up = g.sem("experts_up")
        self.tanh = g.sem("experts_tanh")
        self.halved = g.sem("experts_halved")
        self.mixed = g.sem("experts_mixed")
        self.down = g.sem("experts_down")
        self.y_ready = g.sem("experts_y_ready")
        self.y_out = [g.sem(f"experts_y_out{i}") for i in range(2)]
        self.gathered = [g.sem(f"experts_gathered{c}") for c in range(NC)]
        self.normed = g.sem("experts_normed")
        self.stored = g.sem("experts_stored")
        sb = g.sb
        self.both = sb("experts_both", [P, NT, EX], BF16)
        self.place = sb("experts_place", [P, NT, EX])
        self.pos = sb("experts_pos", [P, 2, NT])
        self.row = sb("experts_row", [P, 2, NT], U32)
        self.result_row = sb("experts_result_row", [P, 2, NT], U32)
        self.full = sb("experts_full", [P, EX, T // 2 // P])
        self.nblocks = sb("experts_nblocks", [P, EX])
        self.before = sb("experts_before", [P, EX, EX])
        self.until = sb("experts_until", [P, EX])
        self.shift = sb("experts_shift", [P, EX])
        self.passed = sb("experts_passed", [1, self.HB, EX])
        self.lookup = sb("experts_lookup", [1, self.BLOCKS])
        self.lookup_int = sb("experts_lookup_int", [1, self.BLOCKS], I32)
        self.w12 = g.BIG[:, 0:2 * EX * FE].rearrange("p (a e f) -> p a e f", a=2, e=EX)
        self.w3 = g.BIG[:, 2 * EX * FE:3 * EX * FE].rearrange("p (e n d) -> p e n d", e=EX, n=self.FT)
        self.xb = [g.OT[0][:, i, 0:D] for i in range(2)]
        self.xt = [g.OT[1][:, i, 0:P] for i in range(2)]
        self.hid = g.rbuf
        self.wb = [v[:, :, :, :].rearrange("p a h w -> p (a h w)").rearrange("p (a f) -> p a f", a=2) for v in g.VA]
        self.yb = [g.Y[:, i, :] for i in range(2)]


    FILLS = -(-BLOCKS // NT)

    def fill(self, eng, pieces):
        g = self.g
        for n in pieces:
            first, tiles = n * NT, min(NT, self.BLOCKS - n * NT)
            eng.dma_start(self.xs[first * P:(first + tiles) * P, :].rearrange("(p t) d -> p t d", p=P),
                          g.CTX[:, 0:tiles, :]).then_inc(self.filled.sem, 16)

    def place_tensor(self, pe, half):
        g, nc, n_half = self.g, self.g.nc, self.router.NH
        both = self.router.half(self.both, half)
        pe.wait_ge(*self.chosen.at(half + 1))
        bank = g.bank[1][:, 0:n_half * EX].rearrange("p (n e) -> p n e", e=EX)
        nc.tensor.matmul(bank, g.upper_bf[:, :], both, start=True, stop=False)
        for n in range(n_half - 1):
            nc.tensor.matmul(bank[:, n + 1:n_half, :], g.ones_bf[:, :],
                             both[:, n:n + 1, :].to_broadcast([P, n_half - 1 - n, EX]), start=False, stop=n == n_half - 2)
        for n in range(n_half):
            last = nc.tensor.matmul(g.bank[2][:, 0:EX], g.ones_bf[:, :], both[:, n, :], start=n == 0, stop=n == n_half - 1)
        last.then_inc(self.counted.sem, 1)

    def place_vector(self, dve, half):
        g, nc, r = self.g, self.g.nc, self.router
        if half == 0:
            self.t = Tally(dve, self.chain)
        t = self.t
        chosen = [r.half(ap, half) for ap in (r.first, r.second)]
        both, place, *work = (r.half(ap, half) for ap in (self.both, self.place, r.W1, r.W2))
        nc.vector.tensor_tensor(both, chosen[0], chosen[1], ALU.add).then_inc(self.chosen.sem, 1)
        dve.wait_ge(*self.counted.at(half + 1))
        bank = g.bank[1][:, 0:r.NH * EX].rearrange("p (n e) -> p n e", e=EX)
        n_full = T // 2 // P
        t.done(nc.vector.tensor_tensor(self.full[:, :, :], g.bank[2][:, 0:EX].unsqueeze(2).to_broadcast([P, EX, n_full]),
                                       g.multiples[:, 0:n_full].unsqueeze(1).to_broadcast([P, EX, n_full]), ALU.is_gt))
        t.done(nc.vector.reduce_sum(self.nblocks[:, :], self.full[:, :, :], axis=AX_X))
        t.done(nc.vector.tensor_tensor(self.before[:, :, :], self.nblocks[:, :].unsqueeze(1).to_broadcast([P, EX, EX]),
                                       g.up_to[:, :, :], ALU.mult))
        t.done(nc.vector.reduce_sum(self.until[:, :], self.before[:, :, :], axis=AX_X))
        t.done(nc.vector.tensor_tensor(self.shift[:, :], self.until[:, :], self.nblocks[:, :], ALU.subtract))
        t.done(nc.vector.tensor_scalar(self.shift[:, :], self.shift[:, :], float(P), float(half * self.HB * P),
                                       ALU.mult, ALU.add))
        t.done(nc.vector.tensor_tensor(place, bank, self.shift[:, :].unsqueeze(1).to_broadcast([P, r.NH, EX]), ALU.add))
        for k in range(2):
            last = nc.vector.tensor_tensor(work[k], place, chosen[k], ALU.mult)
        t.done(last)
        mine = slice(half * r.NH, (half + 1) * r.NH)
        for k in range(2):
            last = nc.vector.reduce_sum(self.pos[:, k, mine], work[k], axis=AX_X)
        t.done(last)
        nc.vector.tensor_copy(self.row[:, :, mine], self.pos[:, :, mine]).then_inc(self.positions.sem, 1)
        nc.vector.tensor_scalar(self.result_row[:, :, mine], self.pos[:, :, mine], float(-half * self.HB * P), None, ALU.add)\
          .then_inc(self.result_rows.sem, 1)
        mine = slice(half * self.HB, (half + 1) * self.HB)
        t.done(nc.vector.tensor_tensor(self.passed[:, :, :], self.until[0:1, :].unsqueeze(1).to_broadcast([1, self.HB, EX]),
                                       g.iota[0:1, 0:self.HB].unsqueeze(2).to_broadcast([1, self.HB, EX]), ALU.is_le))
        t.done(nc.vector.reduce_sum(self.lookup[:, mine], self.passed[:, :, :], axis=AX_X))
        t.done(nc.vector.tensor_scalar(self.lookup[:, mine], self.lookup[:, mine], float(EX - 1), None, ALU.min))
        nc.vector.tensor_copy(self.lookup_int[:, mine], self.lookup[:, mine]).then_inc(self.table.sem, 1)

    def scatter(self, pool, normed):
        g, nc = self.g, self.g.nc
        pool.wait_ge(*self.filled.at(16 * self.FILLS))
        for half in range(2):
            pool.wait_ge(*normed.at(NC // 2 * (half + 1)))
            pool.wait_ge(*self.positions.at(half + 1))
            for n in range(half * NT // 2, (half + 1) * NT // 2):
                for k in range(2):
                    nc.gpsimd.indirect_dma_start(self.xs, bass.IndirectOffsetOnAxis(ap=self.row[:, k, n:n + 1], axis=0),
                                                 g.X[:, n, :], None).then_inc(self.scattered[half].sem, 16)


    LOOPS = ((0, (HB - 4) // 4), ((HB - 4) // 4 + 2, (BLOCKS - 4) // 4))

    def steps(self, eng, body, second_half=None):
        def part(js, i):
            for j in js:
                body(j, i)

        done = 0
        for half, (first, end) in enumerate(self.LOOPS):
            self.loop_half = half
            if half and second_half:
                second_half()
            part(range(done, 2 + 4 * first), None)
            with eng.Fori(first, end) as i:
                part(range(2, 6), 2 * i)
            done = 2 + 4 * end
        part(range(done, self.BLOCKS + 1), None)

    def half_of(self, b):
        return self.loop_half if b.first is None else int(b.no >= self.HB)

    def block(self, j, i):
        return None if j < 0 or j >= self.BLOCKS else Batch(j, i)

    def used(self, b, times):
        return b.first is None or b.first >= times

    def expert(self, eng, b):
        return eng.value_load(self.lookup_int[0:1, bass.ds(b.no, 1)], min_val=0, max_val=EX - 1)

    def load_weights(self, sp):
        g = self.g
        for a in range(2):
            sp.dma_start(self.w12[:, a, :, :], g.io["ex_w12"][:, a, :, :]).then_inc(self.weights_in.sem, 16)
        sp.dma_start(self.w3, g.io["ex_w3"]).then_inc(self.weights_in.sem, 16)

    def sync(self, sp, out):
        def load(b):
            sp.dma_start(self.xb[b.par], block_of(self.xs, b.no)).then_inc(self.x_in[b.par].sem, 16)

        g = self.g
        block_of = lambda dram, n: dram.rearrange("(n p) d -> p n d", p=P)[:, bass.ds(n, 1), :].rearrange("p n d -> p (n d)")
        sp.wait_ge(*self.scattered[0].at(16 * NT))
        load(Batch(0))
        load(Batch(1))

        def step(j, i):
            if self.block(j + 2, i) and (i is not None or j + 2 < self.BLOCKS):
                sp.wait_ge(*self.turned.at(Batch(j, i).no + 1))
                load(Batch(j + 2, i))
            if j >= 1:
                b = Batch(j - 1, i)
                sp.wait_ge(*self.y_ready.at(b.no + 1))
                half = self.half_of(b)
                sp.dma_start(block_of(self.ys[half], b.no - half * self.HB), self.yb[b.par])\
                  .then_inc(self.y_out[b.par].sem, 16)

        def second_half():
            sp.wait_ge(*self.scattered[1].at(16 * NT))
        self.steps(sp, step, second_half)
        for c in range(NC):
            sp.wait_ge(*self.normed.at(c + 1))
            sp.dma_start(out.rearrange("(t p) d -> p t d", p=P)[:, c * TC:(c + 1) * TC, :],
                         g.X[:, c * TC:(c + 1) * TC, :]).then_inc(self.stored.sem, 16)
        sp.wait_ge(*self.stored.at(16 * NC))

    def tensor(self, pe):
        g, nc = self.g, self.g.nc

        def turn_x(b):
            pe.wait_ge(*self.x_in[b.par].at((b.use + 1) * 16))
            if self.used(b, 1):
                pe.wait_ge(*self.xt_ready.at(b.no))
            nc.tensor.transpose(g.bank[7][:, 0:P], self.xb[b.par], g.ident[:, :]).then_inc(self.turned.sem, 1)

        def gate_or_up(b, a):
            for f in range(self.FT):
                last = nc.tensor.matmul(g.bank[2 * a + b.par][:, f * P:(f + 1) * P],
                                        self.wb[b.par][:, a, f * P:(f + 1) * P],
                                        self.xt[b.par], start=True, stop=True)
            last.then_inc((self.up if a else self.gate).sem, 1)

        def down(b, e):
            pe.wait_ge(*self.mixed.at(b.no + 1))
            if self.used(b, 1):
                pe.wait_ge(*self.y_ready.at(b.no))
            for f in range(self.FT):
                last = nc.tensor.matmul(g.bank[6][:, 0:D], self.hid[b.par][:, f * P:(f + 1) * P],
                                        self.w3[:, bass.ds(e, 1), f, :].rearrange("p e d -> p (e d)"),
                                        start=f == 0, stop=f == self.FT - 1)
            last.then_inc(self.down.sem, 1)

        def gate(b):
            pe.wait_ge(*self.xt_ready.at(b.no + 1))
            if self.used(b, 2):
                pe.wait_ge(*self.mixed.at(b.no - 1))
            gate_or_up(b, 0)

        def step(j, i):
            b, before, after = self.block(j, i), self.block(j - 1, i), self.block(j + 1, i)
            if after:
                turn_x(after)
            if b:
                gate_or_up(b, 1)
            if before:
                down(before, self.expert(nc.tensor, before))
            if after:
                gate(after)

        pe.wait_ge(*self.table.at(1))
        pe.wait_ge(*self.weights_in.at(48))
        turn_x(Batch(0))
        gate(Batch(0))
        pe.wait_ge(*self.positions.at(2))

        def second_half():
            pe.wait_ge(*self.table.at(2))
        self.steps(pe, step, second_half)

    def scalar(self, act):
        g, nc = self.g, self.g.nc

        def copy_weights(b):
            if self.used(b, 2):
                act.wait_ge(*self.up.at(b.no - 1))
            nc.scalar.copy(self.wb[b.par], self.w12[:, :, bass.ds(self.expert(nc.scalar, b), 1), :]
                           .rearrange("p a e f -> p a (e f)"))

        def copy_x(b):
            act.wait_ge(*self.turned.at(b.no + 1))
            nc.scalar.copy(self.xt[b.par], g.bank[7][:, 0:P]).then_inc(self.xt_ready.sem, 1)

        def step(j, i):
            b, after = self.block(j, i), self.block(j + 1, i)
            if after:
                copy_weights(after)
            if b:
                act.wait_ge(*self.gate.at(b.no + 1))
                if self.used(b, 2):
                    act.wait_ge(*self.halved.at(b.no - 1))
                nc.scalar.activation(g.fbuf[b.par][:, :], g.bank[b.par], ACT.Tanh, scale=0.5).then_inc(self.tanh.sem, 1)
            if after:
                copy_x(after)

        def second_half():
            act.wait_ge(*self.table.at(2))

        act.wait_ge(*self.table.at(1))
        act.wait_ge(*self.weights_in.at(48))
        copy_weights(Batch(0))
        copy_x(Batch(0))
        self.steps(act, step, second_half)

    def vector(self, dve):
        g, nc, r, t = self.g, self.g.nc, self.router, self.t

        def step(j, i):
            b, before = self.block(j, i), self.block(j - 1, i)
            if b:
                dve.wait_ge(*self.tanh.at(b.no + 1))
                if self.used(b, 2):
                    dve.wait_ge(*self.mixed.at(b.no - 1))
                nc.vector.scalar_tensor_tensor(g.turn[b.par][:, :], g.fbuf[b.par][:, :], 1.0, g.bank[b.par],
                                               ALU.add, ALU.mult).then_inc(self.halved.sem, 1)
            if b:
                dve.wait_ge(*self.up.at(b.no + 1))
                dve.wait_ge(*self.halved.at(b.no + 1))
                if self.used(b, 2):
                    dve.wait_ge(*self.down.at(b.no - 1))
                nc.vector.scalar_tensor_tensor(self.hid[b.par][:, :], g.turn[b.par][:, :], 0.5, g.bank[2 + b.par],
                                               ALU.mult, ALU.mult).then_inc(self.mixed.sem, 1)
            if before:
                dve.wait_ge(*self.down.at(before.no + 1))
                if self.used(before, 2):
                    dve.wait_ge(*self.y_out[before.par].at(before.use * 16))
                nc.vector.tensor_copy(self.yb[before.par], g.bank[6][:, 0:D]).then_inc(self.y_ready.sem, 1)

        self.steps(dve, step)

        dve.wait_ge(*r.routed.at(1))
        for c in range(NC):
            dve.wait_ge(*self.gathered[c].at(16 * 2 * TC))
            x = g.X[:, c * TC:(c + 1) * TC, :]
            for k, y in enumerate((g.V, g.CX)):
                for n in range(c * TC, (c + 1) * TC):
                    last = nc.vector.scalar_tensor_tensor(g.X[:, n, :], y[:, n, :], r.gate[:, k, n:n + 1], g.X[:, n, :],
                                                          ALU.mult, ALU.add)
                t.done(last)
            layernorm(g, t, x, x).then_inc(self.normed.sem, 1)

    def gather(self, pool):
        g, nc = self.g, self.g.nc
        for half in range(2):
            pool.wait_ge(*self.result_rows.at(half + 1))
            for par in range(2):
                pool.wait_ge(*self.y_out[par].at(16 * (((half + 1) * self.HB + 1 - par) // 2)))
            for n in range(half * NT // 2, (half + 1) * NT // 2):
                for k, y in enumerate((g.V, g.CX)):
                    nc.gpsimd.indirect_dma_start(y[:, n, :], None, self.ys[half],
                                                 bass.IndirectOffsetOnAxis(ap=self.result_row[:, k, n:n + 1], axis=0))\
                      .then_inc(self.gathered[n // TC].sem, 16)


WEIGHTS = ["a0_qa", "a0_qb", "a0_ka", "a0_kb", "a0_v", "a0_o",
           "a1_q", "a1_k", "a1_v", "a1_o", "a1_fq", "a1_fg",
           "x1_q", "x1_k", "x1_v", "x1_o", "f0_q", "f0_k", "f0_v", "f0_o"]
COLUMNS = ["a1_bq", "a1_bk", "a1_bfq", "a1_bfg", "f0_g1", "f0_g2"]
ROWVECS = ["a1_bv", "a1_bo", "x1_bo"]


class Globals:

    def __init__(self, nc, ctx, io):
        self.nc, self.ctx, self.io = nc, ctx, io
        self.shared = {}

    def sem(self, name):
        return Signal(self.ctx.enter_context(self.nc.semaphore(name)), 0)

    def shared_sem(self, name, total):
        if name not in self.shared:
            self.shared[name] = [self.sem(name).sem, 0]
        sem, base = self.shared[name]
        self.shared[name][1] += total
        return Signal(sem, base)

    def sb(self, name, shape, dt=F32):
        return self.ctx.enter_context(self.nc.sbuf_tensor(name, shape, dt))

    def allocate(self):
        nc = self.nc
        sb = self.sb
        self.X = sb("X", [P, NT, D])
        self.XT = sb("XT", [P, T])
        self.CTX = sb("CTX", [P, NT, D])
        self.CTXT = sb("CTXT", [P, T])
        self.V = sb("V", [P, NT, D])
        self.CX = sb("CX", [P, NT, D])
        self.CXT = sb("CXT", [P, 2, CH])
        self.BIG = sb("BIG", [P, 3 * EX * FE])
        big = [self.BIG[:, i * H * S // 2:(i + 1) * H * S // 2] for i in range(6)]
        self.Q6 = [b.bitcast(BF16).rearrange("p (h s) -> p h s", h=H) for b in big[0:2]]
        self.K6 = [b.bitcast(BF16).rearrange("p (h s) -> p h s", h=H) for b in big[2:4]]
        self.PT = [b.rearrange("p (h q) -> p h q", h=4) for b in big[4:6]]
        self.VA = [sb(f"VA_{i}", [P, 2, H, PVW]) for i in range(2)]
        self.OT = [sb(f"OT_{i}", [P, 4, S]) for i in range(2)]
        self.MS = sb("MS", [P, 2, H])
        self.MB = [sb(f"MB_{i}", [P, 2, 16], BF16) for i in range(2)]
        self.MT = [sb(f"MT_{i}", [16, S], BF16) for i in range(2)]
        self.rsum = sb("rsum", [P, H])
        self.fbuf = [sb(f"fbuf{i}", [P, CH]) for i in range(2)]
        self.rbuf = [sb(f"rbuf{i}", [P, CH]) for i in range(2)]
        self.turn = [sb(f"turn{i}", [P, CH]) for i in range(2)]
        self.parts = [sb(f"parts{i}", [P, 3, CH], BF16) for i in range(NPARTS)]
        self.Y = sb("Y", [P, TC, D])
        self.stats = sb("stats", [P, 2 * TC, 6])
        self.meanvar = sb("meanvar", [P, 2 * TC, 2])
        self.var = sb("var", [P, 2 * TC])
        self.rstd = sb("rstd", [P, TC])
        self.scale = [sb(f"scale{i}", [P, 2 * TC]) for i in range(2)]
        self.offset = [sb(f"offset{i}", [P, 2 * TC]) for i in range(2)]
        self.square = sb("square", [P, 2 * TC])
        self.ident = sb("ident", [P, P])
        self.ident_bf = sb("ident_bf", [P, P], BF16)
        self.cos = sb("cos", [P, S])
        self.sin = sb("sin", [P, S])
        self.W = sb("W", [P, len(WEIGHTS), P])
        self.cols = sb("cols", [P, len(COLUMNS)])
        self.rowvecs = sb("rowvecs", [P, len(ROWVECS), D])
        self.causal_q = sb("causal_q", [P, 2 * S], BF16)
        self.causal_k = sb("causal_k", [P, 2 * S], BF16)
        PS = self.ctx.enter_context(nc.psum_tensor("PS", [P, 8, CH], F32))
        self.bank = [PS[:, i, :] for i in range(8)]
        self.bank2 = [PS[:, 2 * i:2 * i + 2, :] for i in range(2)]
        self.aux_bf = PS[:, 7, :].bitcast(BF16)
        self.mask_q = sb("mask_q", [P, B * 2 * S], BF16)
        self.mask_k = sb("mask_k", [P, B * 2 * S], BF16)
        self.depth_q = sb("depth_q", [P, P], BF16)
        self.depth_k = sb("depth_k", [P, P], BF16)
        self.router = sb("router", [P, P])
        self.earlier = sb("earlier", [P, 2, S])
        self.iota = sb("iota", [P, P])
        self.f0_w12 = sb("f0_w12", [P, 2, F0])
        self.f0_w3 = sb("f0_w3", [P, 3, D])
        self.upz = sb("upz", [P, 2 * H])
        self.router_w = sb("router_w", [P, EX])
        self.router_b = sb("router_b", [P, EX])
        self.descending = sb("descending", [P, EX])
        self.multiples = sb("multiples", [P, T // P])
        self.up_to = sb("up_to", [P, EX, EX])
        self.upper_bf = sb("upper_bf", [P, P], BF16)
        self.ones_bf = sb("ones_bf", [P, P], BF16)

    def w(self, name):
        return self.W[:, WEIGHTS.index(name), :]

    def col(self, name):
        i = COLUMNS.index(name)
        return self.cols[:, i:i + 1]

    def row(self, name):
        return self.rowvecs[:, ROWVECS.index(name), :]


def program(nc, io, out):
    with ExitStack() as ctx:
        g = Globals(nc, ctx, io)
        g.allocate()
        sem = g.sem
        dram = lambda name, shape, dt: nc.dram_tensor(name, shape, dt, kind="Internal").ap()
        rows_q = [dram(f"rows_q{i}", (ROWS, H, T), BF16) for i in range(2)]
        rows_k = [dram(f"rows_k{i}", (3 * DH, H, T), BF16) for i in range(3)]
        rows_x = dram("rows_x", (9, H, T), BF16)
        mask = Mask(g)

        weights_in, ident_in, tables_in = sem("weights_in"), sem("ident_in"), sem("tables_in")
        first_in, x_in, ctx_in, ctxt_in = sem("first_in"), sem("x_in"), sem("ctx_in"), sem("ctxt_in")
        xt_in = [sem(f"xt_in{c}") for c in range(NC)]
        zeroed, va_zeroed, ones_set = sem("zeroed"), sem("va_zeroed"), sem("ones_set")
        const_rows = [sem(f"const_rows{i}") for i in range(4)]

        def chunks(ap):
            return [ap[:, c * CH:(c + 1) * CH] for c in range(NC)]

        xt, ctxt = chunks(g.XT[:, :]), chunks(g.CTXT[:, :])

        jobs = []
        for c in range(NC):
            for wa, wb, to in (("a0_qa", "a0_qb", rows_q[0]), ("a0_ka", "a0_kb", rows_k[0])):
                jobs.append(dict(kind="rope", w=[g.w(wa), g.w(wb)], src=xt[c], to=to, query=to is rows_q[0]))
        split_a0 = Split(g, jobs, (g.w("a0_v"), g.XT, g.V), NC)
        core_a0 = Core(g, B, 2)
        post_a0 = Post(g, "pa0", core_a0, g.w("a0_o"))

        split_x0_keys = Split(g, [dict(kind="sbuf", src=ctxt[c], to=rows_k[1], query=False) for c in range(NC)],
                              None, NC)
        split_x0 = Split(g, [dict(kind="sbuf", src=xt[c], to=rows_q[1], query=True) for c in range(NC)], None, NC)
        core_x0 = Core(g, B, 2, causal=True, bias=(g.causal_q[:, :], g.causal_k[:, :]))
        post_x0 = Post(g, "px0", core_x0)

        split_x1_keys = Split(g, [dict(kind="psum", w=[g.w("x1_k")], src=ctxt[c], to=rows_k[2], query=False)
                                          for c in range(NC)], (g.w("x1_v"), g.CTXT, g.CTX), NC, (5, 6))
        depths = Depths(g, "f0")
        jobs = [dict(kind="psum", w=[g.w("f0_q")], src=depths.HT[:, :], to=rows_q[0], query=True),
                dict(kind="psum", w=[g.w("f0_k")], src=depths.HT[:, :], to=rows_k[0], query=False)]
        split_f0 = Split(g, jobs, (g.w("f0_v"), depths.HT, g.V), 1)
        core_f0 = Core(g, depths.NP, 1, bias=(g.depth_q[:, :], g.depth_k[:, :]))

        gauss = Gauss(g, "ga1")
        jobs = []
        for c in range(NC):
            jobs.append(dict(kind="keep", w=[g.w("a1_q")], src=xt[c], bias=g.col("a1_bq"),
                             keep=gauss.MQ[:, c * CH:(c + 1) * CH], to=rows_q[1], query=True))
            jobs.append(dict(kind="psum", w=[g.w("a1_k")], src=xt[c], bias=g.col("a1_bk"), to=rows_k[1], query=False))
        split_a1 = Split(g, jobs, (g.w("a1_v"), g.XT, g.V), NC)
        core_a1 = Core(g, B, 2, xrows=9)
        post_a1 = Post(g, "pa1", core_a1, g.w("a1_o"), bias=True)

        split_x1 = Split(g, [dict(kind="psum", w=[g.w("x1_q")], src=xt[c], to=rows_q[0], query=True)
                                    for c in range(NC)], None, NC)
        core_x1 = Core(g, B, 2, bias="batch")
        router = Router(g)
        post_x1 = Post(g, "px1", core_x1, g.w("x1_o"), bias=True, logits=router.chunk)
        router.stream = post_x1
        experts = Experts(g, router, dram("experts_x", (Experts.BLOCKS * P, D), F32), 
                          [dram(f"experts_y{i}", (Experts.HB * P, D), F32) for i in range(2)])

        block = ctx.enter_context(nc.Block())

        def const_rows_in(sp, n):
            for i in range(2):
                sp.dma_start(g.K6[i][XROW:XROW + 16, :, :], io["k_extra"][n % 3]).then_inc(const_rows[n].sem, 16)
                if n == 1:
                    sp.dma_start(g.Q6[i][XROW:XROW + 16, :, :], io["q_extra"]).then_inc(const_rows[n].sem, 16)

        @block.sync
        def _(sp):
            n_a0 = WEIGHTS.index("a0_o")
            sp.dma_start(g.W[:, 0:n_a0, :], io["weights"][:, 0:n_a0, :]).then_inc(first_in.sem, 16)
            for c in range(NC):
                sp.dma_start(g.XT[:, c * CH:(c + 1) * CH], io["xt"][:, c * CH:(c + 1) * CH]).then_inc(xt_in[c].sem, 16)
                if c == 0:
                    sp.dma_start(g.cos[:, :], io["cos"]).then_inc(first_in.sem, 16)
                    sp.dma_start(g.sin[:, :], io["sin"]).then_inc(first_in.sem, 16)
            sp.dma_start(g.CTXT[:, :], io["ctxt"]).then_inc(ctxt_in.sem, 16)
            sp.dma_start(g.ident[:, :], io["ident"]).then_inc(ident_in.sem, 16)
            sp.dma_start(g.ident_bf[:, :], io["ident_bf"]).then_inc(ident_in.sem, 16)

            def first_loads():
                sp.wait_ge(*zeroed.at(3))
                core_a0.first_loads(sp, (rows_q[0], rows_k[0]))
            split_a0.sync(sp, first_loads)
            split_a0.wait_written(sp)
            split_x0_keys.sync(sp)
            core_a0.sync(sp, (rows_q[0], rows_k[0]))
            for ap, name in ((g.cols, "cols"), (g.causal_q, "causal_q"), (g.causal_k, "causal_k"),
                             (g.depth_q, "depth_q"), (g.depth_k, "depth_k"), (g.router, "router"), (g.iota, "iota"),
                             (g.upz, "upz"), (g.router_w, "router_w"), (g.router_b, "router_b"),
                             (g.descending, "descending"), (g.multiples, "multiples"), (g.upper_bf, "upper_bf"),
                             (g.ones_bf, "ones_bf")):
                sp.dma_start(ap[:, :], io[name]).then_inc(tables_in.sem, 16)
            for ap, name in ((g.rowvecs, "rowvecs"), (g.up_to, "up_to"), (g.earlier, "earlier"), (g.f0_w12, "f0_w12"),
                             (g.f0_w3, "f0_w3")):
                sp.dma_start(ap[:, :, :], io[name]).then_inc(tables_in.sem, 16)
            sp.wait_ge(*core_a0.pv_done.at(4 * B))
            mask.sync(sp)

            def first_loads():
                sp.wait_ge(*core_a0.st_ready.at(8 * B))
                const_rows_in(sp, 1)
                core_x0.first_loads(sp, (rows_q[1], rows_k[1]))
            split_x0_keys.wait_written(sp)
            split_x0.sync(sp, first_loads)
            split_x0.wait_written(sp)
            core_x0.sync(sp, (rows_q[1], rows_k[1]))
            split_x1_keys.sync(sp)

            def first_loads():
                sp.wait_ge(*core_x0.st_ready.at(8 * B))
                const_rows_in(sp, 0)
                core_f0.first_loads(sp, (rows_q[0], rows_k[0]))
            split_x1_keys.wait_written(sp)
            split_f0.sync(sp, first_loads)
            split_f0.wait_written(sp)
            core_f0.sync(sp, (rows_q[0], rows_k[0]))

            def first_loads():
                sp.wait_ge(*core_f0.st_ready.at(8 * depths.NP))
                const_rows_in(sp, 2)
                core_a1.first_loads(sp, (rows_q[1], rows_k[1], rows_x), "qk")
            split_a1.sync(sp, first_loads)
            gauss.sync(sp, rows_x)
            sp.wait_ge(*gauss.written.at(48))
            core_a1.first_loads(sp, (rows_q[1], rows_k[1], rows_x), "x")
            split_a1.wait_written(sp)
            core_a1.sync(sp, (rows_q[1], rows_k[1], rows_x))

            def first_loads():
                sp.wait_ge(*core_a1.st_ready.at(8 * B))
                const_rows_in(sp, 3)
                core_x1.first_loads(sp, (rows_q[0], rows_k[2]))
            split_x1.sync(sp, first_loads)
            split_x1.wait_written(sp)
            core_x1.sync(sp, (rows_q[0], rows_k[2]))

            sp.wait_ge(*core_x1.pv_done.at(4 * B))
            experts.load_weights(sp)
            experts.sync(sp, out)

        @block.tensor
        def _(pe):
            pe.wait_ge(*first_in.at(48))

            def ready(c):
                pe.wait_ge(*xt_in[c].at(16))
            split_a0.tensor(pe, ready)
            def ready():
                pe.wait_ge(*ident_in.at(32))
                pe.wait_ge(*weights_in.at(16))
                pe.wait_ge(*ones_set.at(1))
                pe.wait_ge(*split_a0.r1_ready.at(2 * NC))
                pe.wait_ge(*split_a0.v_ready.at(NC))
                pe.wait_ge(*zeroed.at(3))
            core_a0.tensor(pe, ready)

            def ready():
                pe.wait_ge(*core_a0.cx_done.at(NT))
                pe.wait_ge(*core_a0.ot_done.at(4 * B))
                pe.wait_ge(*core_a0.mx_done.at(16 * B))
            ready()
            post_a0.run("tensor", pe, "after")

            pe.wait_ge(*post_a0.xt_ready.at(NC))
            mask.tensor(pe)

            def ready():
                pe.wait_ge(*mask.copied.at(4))
                pe.wait_ge(*tables_in.at(16 * 19))
                pe.wait_ge(*const_rows[1].at(64))
                pe.wait_ge(*post_a0.xt_ready.at(NC))
            core_x0.tensor(pe, ready)

            def ready():
                pe.wait_ge(*core_x0.cx_done.at(NT))
                pe.wait_ge(*core_x0.ot_done.at(4 * B))
                pe.wait_ge(*core_x0.mx_done.at(16 * B))
            ready()
            post_x0.run("tensor", pe, "after")

            def ready(c):
                pe.wait_ge(*post_x0.xt_ready.at(c + 1))
            depths.select_tensor(pe, ready, split_x1_keys)

            def ready(c):
                pe.wait_ge(*depths.h_ready.at(1))
            split_f0.tensor(pe, ready)

            def ready():
                pe.wait_ge(*split_f0.r1_ready.at(2))
                pe.wait_ge(*split_f0.v_ready.at(1))
                pe.wait_ge(*const_rows[0].at(32))
            core_f0.tensor(pe, ready)

            def ready():
                pe.wait_ge(*core_f0.cx_done.at(depths.NP))
                pe.wait_ge(*core_f0.ot_done.at(4 * depths.NP))
                pe.wait_ge(*core_f0.mx_done.at(8 * depths.NP))

            def chunk_ready(c):
                pe.wait_ge(*depths.post.added.at(NC))
                pe.wait_ge(*depths.post.xt_ready.at(c + 1))
            depths.feed_tensor(pe, ready, split_a1.tensor_steps(pe, chunk_ready))
            gauss.tensor(pe)

            def ready():
                pe.wait_ge(*split_a1.r1_ready.at(2 * NC))
                pe.wait_ge(*split_a1.v_ready.at(NC))
                pe.wait_ge(*gauss.copied.at(2))
                pe.wait_ge(*const_rows[2].at(32))
            core_a1.tensor(pe, ready)

            def ready():
                pe.wait_ge(*core_a1.cx_done.at(NT))
                pe.wait_ge(*core_a1.ot_done.at(4 * B))
                pe.wait_ge(*core_a1.mx_done.at(16 * B))
            ready()

            def ready(c):
                pe.wait_ge(*post_a1.xt_ready.at(c + 1))
            post_a1.run("tensor", pe, "after", split_x1.tensor_steps(pe, ready))

            def ready():
                pe.wait_ge(*split_x1.r1_ready.at(NC))
                pe.wait_ge(*const_rows[3].at(32))
            core_x1.tensor(pe, ready)

            def ready():
                pe.wait_ge(*core_x1.cx_done.at(NT))
                pe.wait_ge(*core_x1.ot_done.at(4 * B))
                pe.wait_ge(*core_x1.mx_done.at(16 * B))
            ready()

            def steps():
                experts.place_tensor(pe, 0)
                yield
                yield
                experts.place_tensor(pe, 1)
                yield
            post_x1.run("tensor", pe, "after", steps())
            experts.tensor(pe)

        @block.scalar
        def _(act):
            split_a0.scalar(act)
            act.wait_ge(*ctxt_in.at(16))
            split_x0_keys.scalar(act)
            core_a0.scalar(act)

            def ready(a, c):
                a.wait_ge(*post_a0.xt_ready.at(c + 1))
            post_a0.run("scalar", act, "after", split_x0.scalar_steps(act, ready))
            mask.scalar(act)
            act.wait_ge(*tables_in.at(16 * 19))
            core_x0.scalar(act)
            post_x0.run("scalar", act, "after")
            act.wait_ge(*core_x0.va_ready.at(B))
            act.wait_ge(*experts.filled.at(16 * experts.FILLS))
            split_x1_keys.scalar(act)
            depths.select_scalar(act)
            split_f0.scalar(act)
            core_f0.scalar(act)
            depths.feed_scalar(act, split_a1.scalar_steps(act))
            gauss.scalar(act)
            core_a1.scalar(act)
            post_a1.run("scalar", act, "after", split_x1.scalar_steps(act))
            core_x1.scalar(act)
            post_x1.run("scalar", act, "after")
            router.scalar(act)
            experts.scalar(act)

        @block.vector
        def _(dve):
            for buf in g.K6:
                last = nc.vector.memset(buf[:, :, :].bitcast(F32), 0.0)
            last.then_inc(zeroed.sem, 1)
            dve.wait_ge(*first_in.at(48))
            split_a0.vector(dve)
            dve.wait_ge(*ctxt_in.at(16))
            split_x0_keys.vector(dve)
            for buf in g.VA:
                last = nc.vector.memset(buf[:, :, :, :], 0.0)
            last.then_inc(va_zeroed.sem, 1)
            dve.wait_ge(*zeroed.at(1))
            for buf in g.K6:
                last = nc.vector.memset(buf[MROW:MROW + 2, :, :].bitcast(F32), TWO_ONES)
            last.then_inc(ones_set.sem, 1)
            dve.wait_ge(*va_zeroed.at(1))
            for buf in g.VA:
                last = nc.vector.memset(buf[:, :, :, DH:DH + 1], 1.0)
            last.then_inc(va_zeroed.sem, 1)
            dve.wait_ge(*x_in.at(16))
            core_a0.vector(dve)

            def steps():
                mask.vector(dve)
                yield from split_x0.vector_steps(dve)
            post_a0.run("vector", dve, "after", steps())
            dve.wait_ge(*tables_in.at(16 * 19))
            core_x0.vector(dve)
            dve.wait_ge(*core_x0.cx_done.at(NT))
            post_x0.run("vector", dve, "after")
            depths.select_vector(dve, split_x1_keys)
            split_f0.vector(dve)
            core_f0.vector(dve)

            def steps():
                for c, _ in enumerate(split_a1.vector_steps(dve)):
                    gauss.sums(dve, c, split_a1.kept)
                    yield
            depths.feed_vector(dve, steps())
            gauss.vector(dve)
            core_a1.vector(dve)
            post_a1.run("vector", dve, "after", split_x1.vector_steps(dve))
            core_x1.vector(dve)

            def steps():
                for half in range(2):
                    router.vector(dve, half)
                    experts.place_vector(dve, half)
                    yield
            post_x1.run("vector", dve, "after", steps())
            router.weigh(dve)
            experts.vector(dve)

        @block.gpsimd
        def _(pool):
            for buf in g.Q6:
                nc.gpsimd.memset(buf[:, :, :].bitcast(F32), 0.0).then_inc(zeroed.sem, 1)
            split_a0.gpsimd(pool)
            n_a0 = WEIGHTS.index("a0_o")
            pool.dma_start(g.W[:, n_a0:, :], io["weights"][:, n_a0:, :]).then_inc(weights_in.sem, 16)
            pool.dma_start(g.X[:, :, :], io["x"].rearrange("(t p) d -> p t d", p=P)).then_inc(x_in.sem, 16)
            pool.dma_start(g.CTX[:, :, :], io["ctx"].rearrange("(t p) d -> p t d", p=P)).then_inc(ctx_in.sem, 16)
            split_x0_keys.gpsimd(pool)
            def ready():
                pool.wait_ge(*va_zeroed.at(2))
                pool.wait_ge(*split_a0.v_ready.at(NC))
            core_a0.gpsimd(pool, g.V, ready)
            pool.wait_ge(*ctx_in.at(16))
            experts.fill(pool, (0,))
            split_x0.gpsimd(pool)
            def ready():
                pool.wait_ge(*ctx_in.at(16))
                pool.wait_ge(*core_a0.pv_done.at(4 * B))
            core_x0.gpsimd(pool, g.CTX, ready)
            experts.fill(pool, (1, 2))
            split_x1_keys.gpsimd(pool)
            split_f0.gpsimd(pool)
            def ready():
                pool.wait_ge(*split_f0.v_ready.at(1))
                pool.wait_ge(*core_x0.pv_done.at(4 * B))
            core_f0.gpsimd(pool, g.V, ready)
            split_a1.gpsimd(pool)
            def ready():
                pool.wait_ge(*split_a1.v_ready.at(NC))
                pool.wait_ge(*core_f0.pv_done.at(4 * depths.NP))
            pool.wait_ge(*depths.post.xt_turned.at(NC))
            post_a1.add_bias(pool, g.row("a1_bo"))
            core_a1.gpsimd(pool, g.V, ready, g.row("a1_bv"))
            split_x1.gpsimd(pool)
            def ready():
                pool.wait_ge(*split_x1_keys.v_ready.at(NC))
                pool.wait_ge(*core_a1.pv_done.at(4 * B))
            pool.wait_ge(*post_a1.xt_turned.at(NC))
            post_x1.add_bias(pool, g.row("x1_bo"))
            core_x1.gpsimd(pool, g.CTX, ready)
            experts.scatter(pool, post_x1.normed)
            experts.gather(pool)


DFIRST = np.arange(D).reshape(H, DH).T.reshape(-1)


def rope_order(w, second):
    h, j = DFIRST // DH, DFIRST % DH
    i, high = j % (DH // 2), j >= DH // 2
    odd = high != second
    return w[h * DH + 2 * i + odd]


def constants():
    bf = mybir.dt.np(BF16)
    out = {}
    inv_freq = (np.float32(1.0) / np.float32(10000.0) ** (np.arange(0, DH, 2, dtype=np.float32) / np.float32(DH))).astype(np.float32)
    ang = (np.arange(S, dtype=np.float32)[None, :] * inv_freq[DFIRST % (DH // 2)][:, None]).astype(np.float32)
    sign = np.where(DFIRST % DH < DH // 2, -1.0, 1.0).astype(np.float32)[:, None]
    out["cos"] = np.cos(ang).astype(np.float32)
    out["sin"] = (np.sin(ang) * sign).astype(np.float32)
    out["ident"] = np.eye(P, dtype=np.float32)
    out["ident_bf"] = np.eye(P, dtype=np.float32).astype(bf)
    q, k = np.arange(P)[:, None], np.arange(P)[None, :]
    cq = np.zeros((P, 2 * S), np.float32)
    cq[:, 0:P] = np.where(k > q, NEG_CAUSAL, 0.0)
    cq[:, 2 * P + P:4 * P] = cq[:, 0:P]
    ck = np.zeros((P, 2 * S), np.float32)
    ck[:, 0:P] = cq[:, 0:P].T
    ck[:, 2 * P:3 * P] = cq[:, 0:P].T
    out["causal_q"], out["causal_k"] = cq.astype(bf), ck.astype(bf)

    dq = np.where((q // SEL != k // SEL) | (k > q), NEG_CAUSAL, 0.0)
    out["depth_q"], out["depth_k"] = dq.astype(bf), np.ascontiguousarray(dq.T).astype(bf)
    tok = np.arange(S)
    out["earlier"] = (tok[None, None, :] < (q + P * np.arange(2)[None, :])[:, :, None]).astype(np.float32)
    out["descending"] = np.broadcast_to(np.arange(EX, 0, -1, dtype=np.float32)[None], (P, EX)).copy()
    out["multiples"] = np.broadcast_to(P * np.arange(T // P, dtype=np.float32)[None], (P, T // P)).copy()
    out["up_to"] = np.broadcast_to(np.tril(np.ones((EX, EX), np.float32))[None], (P, EX, EX)).copy()
    out["upper_bf"] = np.triu(np.ones((P, P), np.float32), 1).astype(bf)
    out["ones_bf"] = np.ones((P, P), np.float32).astype(bf)
    out["iota"] = np.broadcast_to(np.arange(P, dtype=np.float32)[None], (P, P)).copy()

    def three(a):
        a = a.astype(np.float32)
        p1 = a.astype(bf)
        p2 = (a - p1.astype(np.float32)).astype(bf)
        p3 = (a - p1.astype(np.float32) - p2.astype(np.float32)).astype(bf)
        return [p1, p2, p3]

    kx = np.zeros((4, 16, H, S), bf)
    key = np.arange(S, dtype=np.float32)
    kx[1, 0:3] = key.astype(bf)
    j = key - S // 2
    sq1 = (j * j).astype(bf)
    sq2 = (j * j - sq1.astype(np.float32)).astype(bf)
    kx[2, 0:3], kx[2, 3:6], kx[2, 6:9] = sq1, sq2, j.astype(bf)
    out["k_extra"] = kx
    slopes = np.cumprod(np.full((H,), 2.0 ** (-8.0 / H), np.float32)).astype(np.float32)
    qx = np.zeros((16, H, S), bf)
    for n, part in enumerate(three(slopes * np.float32(DH ** 0.5))):
        qx[n] = part[:, None]
    out["q_extra"] = qx
    return out


def layout(a):
    io = {}
    w = {
        "a0_qa": rope_order(a["L0_attn_Wq"], False).T, "a0_qb": rope_order(a["L0_attn_Wq"], True).T,
        "a0_ka": rope_order(a["L0_attn_Wk"], False).T, "a0_kb": rope_order(a["L0_attn_Wk"], True).T,
        "a0_v": a["L0_attn_Wv"].T, "a0_o": a["L0_attn_Wo"].T,
        "a1_q": a["L1_attn_wq"], "a1_k": a["L1_attn_wk"], "a1_v": a["L1_attn_wv"], "a1_o": a["L1_attn_wo"],
        "a1_fq": a["L1_attn_wfq"], "a1_fg": a["L1_attn_wfg"],
        "x1_q": a["L1_xattn_Wq"].T, "x1_k": a["L1_xattn_Wk"].T, "x1_v": a["L1_xattn_Wv"].T, "x1_o": a["L1_xattn_Wo"].T,
        "f0_q": a["L0_ffn_W_qkv"][0:D].T, "f0_k": a["L0_ffn_W_qkv"][D:2 * D].T, "f0_v": a["L0_ffn_W_qkv"][2 * D:].T,
        "f0_o": a["L0_ffn_W_out"].T,
    }
    for n in w:
        w[n] = w[n][DFIRST] if n in ("a0_qa", "a0_qb", "a0_ka", "a0_kb") else w[n][DFIRST][:, DFIRST]
    io["weights"] = np.stack([w[n] for n in WEIGHTS], axis=1)
    cols = {"a1_bq": a["L1_attn_bq"], "a1_bk": a["L1_attn_bk"], "a1_bfq": a["L1_attn_bfq"], "a1_bfg": a["L1_attn_bfg"],
            "f0_g1": a["L0_ffn_g1"], "f0_g2": a["L0_ffn_g2"]}
    io["cols"] = np.stack([cols[n][DFIRST] for n in COLUMNS], axis=1)
    rows = {"a1_bv": a["L1_attn_bv"], "a1_bo": a["L1_attn_bo"], "x1_bo": a["L1_xattn_bo"]}
    io["rowvecs"] = np.repeat(np.stack([rows[n][DFIRST] for n in ROWVECS])[None], P, axis=0)
    io["router"] = np.repeat(a["L0_ffn_w_router"][DFIRST][:, None], P, axis=1)
    io["f0_w12"] = np.stack([a["L0_ffn_W1"].T[DFIRST], a["L0_ffn_W2"].T[DFIRST]], axis=1)
    w3 = np.zeros((3 * P, D), np.float32)
    w3[0:F0] = a["L0_ffn_W3"].T[:, DFIRST]
    io["f0_w3"] = w3.reshape(3, P, D).transpose(1, 0, 2)
    upz = np.zeros((D, 2 * H), np.float32)
    for n, name in enumerate(("L1_attn_up", "L1_attn_uz")):
        for h in range(H):
            upz[np.arange(DH) * H + h, n * H + h] = a[name][h, 0]
    io["upz"] = upz
    io["router_w"] = a["L1_ffn_router_w"].T[DFIRST]
    io["router_b"] = np.repeat(a["L1_ffn_router_b"][None], P, axis=0)
    io["ex_w12"] = np.stack([a[f"L1_ffn_{n}_w"].transpose(2, 0, 1)[DFIRST] for n in ("gate", "up")], axis=1)
    io["ex_w3"] = a["L1_ffn_down_w"][:, DFIRST].reshape(EX, D, FE // P, P).transpose(3, 0, 2, 1)
    io["mask"] = a["mask_Bx1xSxS2_if1"].reshape(B * S, S)
    io["x"] = a["x"].reshape(T, D)[:, DFIRST]
    io["xt"] = io["x"].T
    io["ctx"] = a["ctx_1024"].reshape(T, D)[:, DFIRST]
    io["ctxt"] = io["ctx"].T
    return io


def kernel(**inputs):
    import concourse.bacc as _bacc
    from concourse.bass_utils import run_bass_kernel_spmd as _run

    arrays = {n: np.ascontiguousarray(v) for n, v in
              (layout({k: np.asarray(v) for k, v in inputs.items()}) | constants()).items()}
    nc = _bacc.Bacc("TRN2", target_bir_lowering=False, num_devices=1)
    io = {n: nc.dram_tensor(f"in_{n}", v.shape, mybir.dt.from_np(v.dtype), kind="ExternalInput").ap()
          for n, v in arrays.items()}
    out = nc.dram_tensor("out_0", (T, D), F32, kind="ExternalOutput").ap()
    program(nc, io, out)
    r = _run(nc, [{f"in_{n}": v for n, v in arrays.items()}], core_ids=[0])
    return r.results[0]["out_0"][:, np.argsort(DFIRST)].reshape(B, S, D)
```
